# Optimizing a Trainium2 kernel written in Bass

```python
import numpy as np
import jax
import jax.numpy as jnp

def _softmax(x, axis=-1):
    return jax.nn.softmax(x, axis=axis)

def _gelu(x):
    return jax.nn.gelu(x, approximate=True)

def _silu(x):
    return jax.nn.silu(x)

def _sigmoid(x):
    return jax.nn.sigmoid(x)

def _layernorm(x, axis=-1, eps=1e-05):
    m = jnp.mean(x, axis=axis, keepdims=True)
    v = jnp.var(x, axis=axis, keepdims=True)
    return (x - m) / jnp.sqrt(v + eps)

def _scatter_add(tgt, idx, src, axis=0):
    return tgt.at[idx].add(src)

def _segment_sum(src, seg, n):
    return jax.ops.segment_sum(src, seg, n)
kernel_name = 'mk_decoder_preln_d1_seqx_r4_5abea3'

def setup_inputs(seed: int=0):
    np.random.seed(seed)
    _w = jnp.asarray

    def _rec_inputs():
        import jax
        import jax.numpy as jnp
        _rk = jax.random.key(seed)
        x = -0.0003929 + 0.9999 * jax.random.normal(jax.random.fold_in(_rk, 1), (32, 128, 512), jnp.float32)
        _lenS = 128 - jax.random.randint(jax.random.fold_in(_rk, 7), (32,), 0, max(1, 128 // 4) + 1, jnp.int32)
        _lenS2 = 128 - jax.random.randint(jax.random.fold_in(_rk, 8), (32,), 0, max(1, 128 // 4) + 1, jnp.int32)
        _ctx_2048P = jax.random.normal(jax.random.fold_in(_rk, 11), (32, 16, 512), jnp.float32)
        _ctx_2048c = jax.random.dirichlet(jax.random.fold_in(_rk, 511), 0.3 * jnp.ones((16,), jnp.float32), (32, 128))
        _ctx_2048t = jnp.einsum('bsk,bkd->bsd', _ctx_2048c, _ctx_2048P)
        _ctx_2048t = _ctx_2048t * jax.lax.rsqrt(jnp.mean(jnp.square(_ctx_2048t)) + 1e-12) * 0.953939
        ctx_2048 = -0.000514642 + 1.00011 * (_ctx_2048t + 0.3 * jax.random.normal(jax.random.fold_in(_rk, 611), (32, 128, 512), jnp.float32))
        return (x, ctx_2048)
    x, ctx_2048 = _rec_inputs()

    def _L0_attn_setup():
        import jax, jax.numpy as jnp
        import numpy as np
        B, T, E, H = (2, 512, 512, 16)
        D = E // H
        ROPE_BASE = 10000.0

        def _rope(x):
            t, d = (x.shape[-2], x.shape[-1])
            j = jnp.arange(d // 2, dtype=x.dtype)
            thetas = ROPE_BASE ** (-2.0 * j / d)
            m = jnp.arange(1, t + 1, dtype=x.dtype)
            ang = m[:, None] * thetas[None, :]
            C = jnp.concatenate([ang, ang], axis=-1)
            x_rot = jnp.concatenate([-x[..., d // 2:], x[..., :d // 2]], axis=-1)
            return x * jnp.cos(C) + x_rot * jnp.sin(C)
        key = jax.random.key(seed)
        ks = jax.random.split(key, 9)
        s = 1.0 / np.sqrt(E)
        return {'x': jax.random.normal(ks[0], (B, T, E), jnp.float32), 'Wq': jax.random.normal(ks[1], (E, E), jnp.float32) * s, 'bq': jax.random.normal(ks[2], (E,), jnp.float32) * s, 'Wk': jax.random.normal(ks[3], (E, E), jnp.float32) * s, 'bk': jax.random.normal(ks[4], (E,), jnp.float32) * s, 'Wv': jax.random.normal(ks[5], (E, E), jnp.float32) * s, 'bv': jax.random.normal(ks[6], (E,), jnp.float32) * s, 'Wo': jax.random.normal(ks[7], (E, E), jnp.float32) * s, 'bo': jax.random.normal(ks[8], (E,), jnp.float32) * s}
    _L0_attn_all = _L0_attn_setup()
    _L0_attn_in = {k: v for k, v in _L0_attn_all.items() if k in ('Wq', 'bq', 'Wk', 'bk', 'Wv', 'bv', 'Wo', 'bo')}
    del _L0_attn_all

    def _L0_xattn_setup():
        import jax, jax.numpy as jnp
        import numpy as np
        NUM_HEADS = 16

        def _qdq(x):
            s = jnp.maximum(jnp.max(jnp.abs(x), axis=-1, keepdims=True) / 127.0, 1e-08)
            return jnp.clip(jnp.round(x / s), -127.0, 127.0) * s
        key = jax.random.key(seed)
        ks = jax.random.split(key, 8)
        B, N, M, D = (2, 1024, 128, 512)
        w_std = 0.02
        return {'x': jax.random.normal(ks[0], (B, N, D), jnp.float32), 'cond': jax.random.normal(ks[1], (B, M, D), jnp.float32), 'wq': jax.random.normal(ks[2], (D, D), jnp.float32) * w_std, 'bq': jax.random.normal(ks[3], (D,), jnp.float32) * w_std, 'wkv': jax.random.normal(ks[4], (2 * D, D), jnp.float32) * w_std, 'bkv': jax.random.normal(ks[5], (2 * D,), jnp.float32) * w_std, 'wp': jax.random.normal(ks[6], (D, D), jnp.float32) * w_std, 'bp': jax.random.normal(ks[7], (D,), jnp.float32) * w_std}
    _L0_xattn_all = _L0_xattn_setup()
    _L0_xattn_in = {k: v for k, v in _L0_xattn_all.items() if k in ('wq', 'bq', 'wkv', 'bkv', 'wp', 'bp')}
    del _L0_xattn_all

    def _L0_ffn_setup():
        import jax, jax.numpy as jnp
        import numpy as np
        B, S, H = (2, 256, 512)
        E, K, F = (64, 8, 192)
        CAP = 128
        key = jax.random.key(seed)
        k1, k2, k3, k4, k5 = jax.random.split(key, 5)
        scale_h = 1.0 / np.sqrt(H)
        scale_f = 1.0 / np.sqrt(F)
        return {'hidden_states': jax.random.normal(k1, (B, S, H), jnp.float32), 'router_w': jax.random.normal(k2, (E, H), jnp.float32) * scale_h, 'w_gate': jax.random.normal(k3, (E, H, F), jnp.float32) * scale_h, 'w_up': jax.random.normal(k4, (E, H, F), jnp.float32) * scale_h, 'w_down': jax.random.normal(k5, (E, F, H), jnp.float32) * scale_f}
    _L0_ffn_all = _L0_ffn_setup()
    _L0_ffn_in = {k: v for k, v in _L0_ffn_all.items() if k in ('router_w', 'w_gate', 'w_up', 'w_down')}
    del _L0_ffn_all
    return {'x': x, 'ctx_2048': ctx_2048, 'L0_attn_Wq': _L0_attn_in['Wq'], 'L0_attn_bq': _L0_attn_in['bq'], 'L0_attn_Wk': _L0_attn_in['Wk'], 'L0_attn_bk': _L0_attn_in['bk'], 'L0_attn_Wv': _L0_attn_in['Wv'], 'L0_attn_bv': _L0_attn_in['bv'], 'L0_attn_Wo': _L0_attn_in['Wo'], 'L0_attn_bo': _L0_attn_in['bo'], 'L0_xattn_wq': _L0_xattn_in['wq'], 'L0_xattn_bq': _L0_xattn_in['bq'], 'L0_xattn_wkv': _L0_xattn_in['wkv'], 'L0_xattn_bkv': _L0_xattn_in['bkv'], 'L0_xattn_wp': _L0_xattn_in['wp'], 'L0_xattn_bp': _L0_xattn_in['bp'], 'L0_ffn_router_w': _L0_ffn_in['router_w'], 'L0_ffn_w_gate': _L0_ffn_in['w_gate'], 'L0_ffn_w_up': _L0_ffn_in['w_up'], 'L0_ffn_w_down': _L0_ffn_in['w_down']}

def reference(x, ctx_2048, L0_attn_Wq, L0_attn_bq, L0_attn_Wk, L0_attn_bk, L0_attn_Wv, L0_attn_bv, L0_attn_Wo, L0_attn_bo, L0_xattn_wq, L0_xattn_bq, L0_xattn_wkv, L0_xattn_bkv, L0_xattn_wp, L0_xattn_bp, L0_ffn_router_w, L0_ffn_w_gate, L0_ffn_w_up, L0_ffn_w_down):
    import jax
    import jax.numpy as jnp

    def _L0_attn_ref(x, Wq, bq, Wk, bk, Wv, bv, Wo, bo):
        import jax, jax.numpy as jnp
        import numpy as np
        B, T, E, H = (2, 512, 512, 16)
        D = E // H
        ROPE_BASE = 10000.0

        def _rope(x):
            t, d = (x.shape[-2], x.shape[-1])
            j = jnp.arange(d // 2, dtype=x.dtype)
            thetas = ROPE_BASE ** (-2.0 * j / d)
            m = jnp.arange(1, t + 1, dtype=x.dtype)
            ang = m[:, None] * thetas[None, :]
            C = jnp.concatenate([ang, ang], axis=-1)
            x_rot = jnp.concatenate([-x[..., d // 2:], x[..., :d // 2]], axis=-1)
            return x * jnp.cos(C) + x_rot * jnp.sin(C)
        b, t, e = x.shape

        def proj(W, bias):
            y = jnp.einsum('bte,fe->btf', x, W) + bias
            return y.reshape(b, t, H, D).transpose(0, 2, 1, 3)
        q = _rope(proj(Wq, bq))
        k = _rope(proj(Wk, bk))
        v = proj(Wv, bv)
        scale = jnp.sqrt(jnp.asarray(D, x.dtype))
        att = jnp.einsum('bhqd,bhkd->bhqk', q, k) / scale
        causal = jnp.tril(jnp.ones((t, t), bool))
        att = jnp.where(causal, att, -jnp.inf)
        att = jax.nn.softmax(att, axis=-1)
        y = jnp.einsum('bhqk,bhkd->bhqd', att, v)
        y = y.transpose(0, 2, 1, 3).reshape(b, t, e)
        y = jnp.einsum('bte,fe->btf', y, Wo) + bo
        return y

    def _L0_xattn_ref(x, cond, wq, bq, wkv, bkv, wp, bp):
        import jax, jax.numpy as jnp
        import numpy as np
        NUM_HEADS = 16

        def _qdq(x):
            s = jnp.maximum(jnp.max(jnp.abs(x), axis=-1, keepdims=True) / 127.0, 1e-08)
            return jnp.clip(jnp.round(x / s), -127.0, 127.0) * s
        B, N, C = x.shape
        M = cond.shape[1]
        H = NUM_HEADS
        Dh = C // H
        q = _qdq(x) @ _qdq(wq).T + bq
        kv = cond @ wkv.T + bkv
        k, v = jnp.split(kv, 2, axis=-1)
        q = q.reshape(B, N, H, Dh)
        k = k.reshape(B, M, H, Dh)
        v = v.reshape(B, M, H, Dh)
        scale = 1.0 / np.sqrt(Dh)
        attn = jax.nn.softmax(jnp.einsum('bnhd,bmhd->bhnm', q, k) * scale, axis=-1)
        o = jnp.einsum('bhnm,bmhd->bnhd', attn, v).reshape(B, N, C)
        out = _qdq(o) @ _qdq(wp).T + bp
        return out

    def _L0_ffn_ref(hidden_states, router_w, w_gate, w_up, w_down):
        import jax, jax.numpy as jnp
        import numpy as np
        B, S, H = (2, 256, 512)
        E, K, F = (64, 8, 192)
        CAP = 128
        b, s, h = hidden_states.shape
        T = b * s
        xf = hidden_states.reshape(T, h)
        logits = xf @ router_w.T
        scores = jax.nn.softmax(logits.astype(jnp.float32), axis=-1)
        topk_w, topk_idx = jax.lax.top_k(scores, K)
        topk_w = topk_w / (topk_w.sum(axis=-1, keepdims=True) + 1e-20)
        slot_expert = topk_idx.reshape(-1)
        slot_token = jnp.repeat(jnp.arange(T), K)
        onehot = jax.nn.one_hot(slot_expert, E, dtype=jnp.int32)
        pos = (jnp.cumsum(onehot, axis=0) * onehot).sum(-1) - 1
        valid = pos < CAP
        dest = jnp.where(valid, slot_expert * CAP + pos, E * CAP)
        buf = jnp.zeros((E * CAP + 1, h), xf.dtype).at[dest].set(xf[slot_token])
        xb = buf[:E * CAP].reshape(E, CAP, h)
        gate = jnp.einsum('ech,ehf->ecf', xb, w_gate)
        up = jnp.einsum('ech,ehf->ecf', xb, w_up)
        hmid = jax.nn.silu(gate) * up
        yb = jnp.einsum('ecf,efh->ech', hmid, w_down).reshape(E * CAP, h)
        yb = jnp.concatenate([yb, jnp.zeros((1, h), yb.dtype)], axis=0)
        slot_out = yb[dest] * topk_w.reshape(-1)[:, None].astype(yb.dtype)
        out = jnp.zeros((T, h), yb.dtype).at[slot_token].add(slot_out)
        return out.reshape(b, s, h)
    x = x + _L0_attn_ref(_layernorm(x, axis=-1), L0_attn_Wq, L0_attn_bq, L0_attn_Wk, L0_attn_bk, L0_attn_Wv, L0_attn_bv, L0_attn_Wo, L0_attn_bo)
    x = x + _L0_xattn_ref(_layernorm(x, axis=-1), ctx_2048, L0_xattn_wq, L0_xattn_bq, L0_xattn_wkv, L0_xattn_bkv, L0_xattn_wp, L0_xattn_bp)
    x = x + _L0_ffn_ref(_layernorm(x, axis=-1), L0_ffn_router_w, L0_ffn_w_gate, L0_ffn_w_up, L0_ffn_w_down)
    return x

_drawn_inputs = setup_inputs


def setup_inputs(seed=0):
    import zlib

    import numpy as np

    out = dict(_drawn_inputs(seed))
    spreads = {}
    factors = {'L0_attn_bq': 3.982,
     'L0_attn_bk': 6.271,
     'L0_xattn_wq': 4.79,
     'L0_xattn_bq': 64.0,
     'L0_xattn_bkv': 3.452}
    for name, (base, spread) in spreads.items():
        noise = np.random.default_rng([zlib.crc32(name.encode()), seed]).standard_normal(out[name].shape)
        drawn = base * np.exp(spread * noise) if base else spread * noise
        out[name] = jnp.asarray(drawn.astype(out[name].dtype))
    for name, factor in factors.items():
        out[name] = (out[name] * factor).astype(out[name].dtype)
    return out
```

```python
from contextlib import ExitStack

import numpy as np

import concourse.bass as bass
from concourse import mybir

F32 = mybir.dt.float32
F32R = mybir.dt.float32r
BF16 = mybir.dt.bfloat16
U32 = mybir.dt.uint32
ALU = mybir.AluOpType
ACT = mybir.ActivationFunctionType
AX_X = mybir.AxisListType.X

P = 128
B = 32
D = 512
KT = D // P
H = 16
DH = D // H
NG = 4
GH = H // NG
VW = DH + 1
E = 64
TOPK = 8
CAP = 128
F = 192
FP = F // 2
ROW = D + 1 + E
TOKENS = B * P
SLOTS = E * CAP
NOWHERE = 2 * SLOTS
SCALE = float(DH) ** -0.5
LN_EPS = 1e-5
ROUND = 1.5 * 2.0 ** 23
QMAX = 127.0
MASKED = -1e30
RING = 4


def nth(ordinal, per, j):
    return (ordinal - 1) * per + j


def until(eng, semaphore, value):
    if not isinstance(value, int) or value > 0:
        eng.wait_ge(semaphore, value)


def apart(eng):
    eng.nop(nofuse=True)


def layer(nc, x, ctx_in, qT_w, kT_w, vT_w, oT_w, xkT_w, xvT_w, xq_w, xp_w, bq, bk, bv, bo, xbq, xbk, xbv,
          xbp, routerT, w_gate, w_up, w_down, cos_t, sin_t, ident_f, causal, prior, slot0, out):
    routed = nc.dram_tensor("routed", (SLOTS, ROW), F32).ap()
    st = ExitStack()

    def sb(name, shape, dt=F32):
        return st.enter_context(nc.sbuf_tensor(name, shape, dt))

    def sem(name):
        return st.enter_context(nc.semaphore(name))

    with st:
        bank = st.enter_context(nc.psum_tensor("bank", [P, 8, 512], F32))

        def bank_bf16(b):
            return bank[:, b, :].bitcast(BF16)[:, 0:D]

        idf = sb("idf", [P, P])
        idb = sb("idb", [P, P], BF16)
        mask_add = sb("mask_add", [P, P], BF16)
        before = sb("before", [P, P], BF16)
        ones_b = sb("ones_b", [P, P], BF16)
        ones_f = sb("ones_f", [P, P])
        cos_sb = sb("cos_sb", [P, DH])
        sin_sb = sb("sin_sb", [P, DH])
        slot_base = sb("slot_base", [P, E])
        bias2 = {name: sb(f"b_{name}", [2, D], F32R) for name in ("q", "k", "v", "o", "xk", "xv")}
        ones2 = sb("ones2", [2, P], F32R)
        pick = sb("pick", [2, 2])
        xq_wT = sb("xq_wT", [P, KT, D], BF16)
        xp_wT = sb("xp_wT", [P, KT, D], BF16)
        xq_ws = sb("xq_ws", [P, KT])
        xp_ws = sb("xp_ws", [P, KT])
        xq_bs = sb("xq_bs", [P, KT])
        xp_row = sb("xp_row", [P, D])
        xp_bias = sb("xp_bias", [P, D])
        r_hi = sb("r_hi", [P, KT, E], F32R)
        r_lo = sb("r_lo", [P, KT, E], F32R)
        rstep = sb("rstep", [P, 8])

        x_in = sb("x_in", [P, D])
        x_res = sb("x_res", [P, D])
        ctx_sb = sb("ctx_sb", [P, D])
        xn = sb("xn", [P, D])
        xT_hi = sb("xT_hi", [P, KT, P], F32R)
        xT_lo = sb("xT_lo", [P, KT, P], F32R)
        roped = sb("roped", [P, 2 * D])
        qT = sb("qT", [P, NG, P])
        kbd = sb("kbd", [P, NG, GH, P])
        v1 = sb("v1", [P, H, VW])
        probs = sb("probs", [P, NG, GH * P])
        probsT = sb("probsT", [P, NG, GH * P])
        rot = probsT[:, 0:2, :].rearrange("p a n -> p (a n)")
        att = sb("att", [P, D])
        attT_hi = sb("attT_hi", [P, KT, P], F32R)
        attT_lo = sb("attT_lo", [P, KT, P], F32R)
        x1 = sb("x1", [P, D])
        cT_hi = sb("cT_hi", [P, KT, P], F32R)
        cT_lo = sb("cT_lo", [P, KT, P], F32R)
        xk_sb = sb("xk_sb", [P, D])
        xkbd = sb("xkbd", [P, NG, GH, P])
        xv1 = sb("xv1", [P, H, VW])
        xn2 = sb("xn2", [P, D])
        xq8 = sb("xq8", [P, D], BF16)
        xq8T = sb("xq8T", [P, KT, P], BF16)
        cq = xk_sb
        cqT = qT
        xatt = sb("xatt", [P, D])
        xo8, xo8T = xq8, xq8T
        x2 = sb("x2", [P, D])
        row = sb("row", [P, ROW])
        x3T_hi, x3T_lo = attT_hi, attT_lo
        small = sb("small", [P, 128])
        half = sb("half", [P, 1])
        router = sb("router", [P, 8, E])
        chosen = sb("chosen", [P, E], BF16)
        chosen_before = sb("chosen_before", [P, E], BF16)
        slots = sb("slots", [P, TOPK], U32)
        SMALL_AT = [0]

        def cols(n):
            SMALL_AT[0] += n
            return small[:, SMALL_AT[0] - n:SMALL_AT[0]]

        ln = {k: dict(stats=cols(6), mv=cols(2), v=cols(1), r0=cols(1), t=cols(1), u=cols(1), r=cols(1))
              for k in ("self", "cross", "ffn")}
        x_amax, x_s, x_rs = cols(1), cols(1), cols(1)
        o_amax, o_s, o_rs = cols(1), cols(1), cols(1)
        sums = cols(H)
        xsums = cols(H)
        negmax = cols(H)
        l_max, e_sum, e_rs, t_sum, t_den, t_rd, t_f = (cols(1) for _ in range(7))
        top8 = router[:, 7, 0:TOPK]
        key8 = router[:, 7, 8:8 + TOPK]

        s_const = sem("const_loaded")
        s_wload = [sem(f"weight_loaded_{k}") for k in range(2)]
        s_bload = sem("bias_loaded")
        d_wchain = sem("dve_setup_step")
        s_x_in, s_x_res, s_ctx = sem("x_in_loaded"), sem("x_res_loaded"), sem("ctx_loaded")
        s_x2_stored, s_scatter, s_filled = sem("x2_stored"), sem("rows_scattered"), sem("routed_filled")
        s_init, s_init2 = sem("pool_constants"), sem("fill_row_ready")
        s_wsplit, s_wprep, s_wT, s_wTr = sem("weights_split"), sem("weight_steps"), sem("weight_transposed"), sem("weight_transposes_read")
        p_xT, p_qk, p_v = sem("pe_xT"), sem("pe_qk"), sem("pe_v")
        p_qkT = sem("pe_qkT")
        p_s, p_pT, p_pv = sem("pe_scores"), sem("pe_probsT"), sem("pe_pv")
        p_aT, p_y = sem("pe_attT"), sem("pe_y")
        p_cT, p_xk, p_xv, p_xkT = sem("pe_ctxT"), sem("pe_xk"), sem("pe_xv"), sem("pe_xkT")
        p_q8T, p_cq, p_cqT = sem("pe_xq8T"), sem("pe_cq"), sem("pe_cqT")
        p_xs, p_xpT, p_xpv = sem("pe_xscores"), sem("pe_xprobsT"), sem("pe_xpv")
        p_o8T, p_xp = sem("pe_xo8T"), sem("pe_xp")
        p_x3T, p_log, p_pos = sem("pe_x3T"), sem("pe_logits"), sem("pe_positions")
        a_xT, a_v, a_kbd = sem("act_xT"), sem("act_v"), sem("act_kbd")
        a_exp, a_pT = sem("act_exp"), sem("act_probsT")
        a_aT = sem("act_attT")
        a_cT, a_xk, a_xv, a_xkbd = sem("act_ctxT"), sem("act_xk"), sem("act_xv"), sem("act_xkbd")
        a_q8T, a_cq, a_cqT = sem("act_xq8T"), sem("act_cq"), sem("act_cqT")
        a_xexp, a_xpT, a_o8T = sem("act_xexp"), sem("act_xprobsT"), sem("act_xo8T")
        a_x3T, a_rexp = sem("act_x3T"), sem("act_router_exp")
        d_ln = {k: sem(f"dve_ln_{k}") for k in ln}
        d_xT, d_rope, d_qT = sem("dve_xT"), sem("dve_rope"), sem("dve_qT")
        d_max, d_pT, d_att = sem("dve_max"), sem("dve_probsT"), sem("dve_att")
        d_aT, d_x1 = sem("dve_attT"), sem("dve_x1")
        d_cT = sem("dve_ctxT")
        d_q8, d_xmax, d_xpT = sem("dve_quant_x"), sem("dve_xmax"), sem("dve_xprobsT")
        d_xatt, d_o8, d_x2 = sem("dve_xatt"), sem("dve_quant_o"), sem("dve_x2")
        d_x3T, d_r1, d_r2 = sem("dve_x3T"), sem("dve_route"), sem("dve_slots")
        g_pow = {k: sem(f"pool_rsqrt_{k}") for k in ln}
        g_x1b, g_tok = sem("pool_x1_bias"), sem("pool_token_number")

        weights_in = (("q", qT_w), ("k", kT_w), ("v", vT_w), ("xk", xkT_w), ("xv", xvT_w), ("o", oT_w))
        STAGE = {0: probs, 1: probsT, 2: kbd[:, :, :, :].rearrange("p g j t -> p g (j t)"),
                 3: xkbd[:, :, :, :].rearrange("p g j t -> p g (j t)")}
        bias_in = (("q", bq), ("k", bk), ("v", bv), ("xk", xbk), ("xv", xbv), ("o", bo))
        N_CONST = 8 + 3
        bias_f = roped[0:2, :]

        W = {}
        with ExitStack() as matrices:
            for name in ("q", "k", "v", "xk", "xv", "o"):
                W[name] = tuple(matrices.enter_context(nc.sbuf_tensor(f"w_{name}_{part}", [P, KT, D], F32R))
                                for part in ("hi", "lo"))
        w_gu, w_dn = [], []
        for k in range(RING):
            w_gu.append(sb(f"w_gate_up{k}", [P, 2, KT, F]))
            w_dn.append(sb(f"w_down{k}", [FP, 2, D]))
        tiles = [t[:, :, :, :].rearrange("p g j t -> p (g j t)") for t in (kbd, xkbd)] + \
                [t[:, :, :].rearrange("p g n -> p (g n)") for t in (probs, probsT)]
        rows = [t[:, 0:D + 1] for t in tiles]
        share = [t[:, D + 1:D + 2] for t in tiles]
        rowsT = [x_in, x_res]
        gated = [xn[:, 0:F], xn2[:, 0:F]]
        hidden = [att[:, 0:F], xatt[:, 0:F]]
        hiddenT = [cq[0:FP, 0:2 * P], ctx_sb[0:FP, 0:2 * P]]
        scaled_y = [x1, x2]
        token_of = [slots[:, 0:1], slots[:, 1:2]]
        s_ring = [sem(f"expert_weights_loaded{k}") for k in range(RING)]
        s_rows = [sem(f"expert_rows_loaded{k}") for k in range(RING)]
        s_added = sem("outputs_added")
        m_xT, m_gu, m_hT, m_down = sem("moe_rowsT"), sem("moe_gate_up"), sem("moe_hiddenT"), sem("moe_down")
        m_xTc, m_silu = sem("moe_rowsT_copied"), sem("moe_silu")
        m_h, m_hTc, m_y = sem("moe_hidden"), sem("moe_hiddenT_copied"), sem("moe_scaled")
        gate_e = w_gate.rearrange("e (p t) f -> e p t f", t=KT)
        up_e = w_up.rearrange("e (p t) f -> e p t f", t=KT)
        down_e = w_down.rearrange("e (p u) h -> e p u h", u=2)
        routed_e = routed.rearrange("(e p) c -> e p c", p=CAP)

        def share_of(e):
            return routed_e[e][:, bass.ds(e + (D + 1), 1)]

        def load_weights(e, k):
            nc.sync.dma_start(w_gu[k][:, 0, :, :], gate_e[e]).then_inc(s_ring[k], 16)
            nc.sync.dma_start(w_gu[k][:, 1, :, :], up_e[e]).then_inc(s_ring[k], 16)
            nc.sync.dma_start(w_dn[k][:, :, :], down_e[e]).then_inc(s_ring[k], 16)

        block = st.enter_context(nc.Block())

        @block.sync
        def _(sp):
            sp.dma_start(x_in[:, :], x[0]).then_inc(s_x_in, 16)
            for dst, src in ((idf, ident_f), (cos_sb, cos_t), (sin_sb, sin_t), (slot_base, slot0)):
                sp.dma_start(dst[:, :], src).then_inc(s_const, 16)
            for k, src in enumerate((causal, prior)):
                sp.dma_start(att[:, k * P:(k + 1) * P], src).then_inc(s_const, 16)
            sp.dma_start(xq_bs[:, :], xbq.rearrange("(g p) -> p g", p=P),
                         allow_slow_non_contiguous=True).then_inc(s_const, 16)
            sp.dma_start(xp_bias[:, :], xbp.unsqueeze(0).to_broadcast([P, D])).then_inc(s_const, 16)
            sp.dma_start(pick[:, :], ident_f[0:2, 0:2]).then_inc(s_const, 16)
            for n, (name, src) in enumerate(weights_in):
                if n >= 2:
                    sp.wait_ge(s_wsplit, n - 1)
                sp.dma_start(STAGE[n % 2][:, :, :], src.rearrange("(t p) n -> p t n", p=P)).then_inc(s_wload[n % 2], 16)
                if n == 0:
                    sp.dma_start(STAGE[2][:, :, :], xq_w.rearrange("(g p) n -> p g n", p=P)).then_inc(s_const, 16)
                    sp.dma_start(STAGE[3][:, :, :], xp_w.rearrange("(g p) n -> p g n", p=P)).then_inc(s_const, 16)
            sp.wait_ge(s_wsplit, len(weights_in) - 1)
            sp.dma_start(STAGE[0][:, 0, 0:KT * E].rearrange("p (t e) -> p t e", t=KT),
                         routerT.rearrange("(t p) e -> p t e", p=P)).then_inc(s_wload[0], 16)
            for n, (name, src) in enumerate(bias_in):
                if n >= 1:
                    sp.wait_ge(s_wprep, n)
                sp.dma_start(bias_f[:, 0:D], src.unsqueeze(0).to_broadcast([2, D])).then_inc(s_bload, 16)
            sp.wait_ge(s_init2, 2)
            empty = row[:, :]
            for c in range(4):
                sp.dma_start(routed.rearrange("(e p) c -> p e c", p=CAP)[:, c * 16:(c + 1) * 16, :],
                             empty.unsqueeze(1).to_broadcast([P, 16, ROW])).then_inc(s_filled, 16)
            sp.dma_start(out[B], row[:, 0:D]).then_inc(s_filled, 16)

            def body(cur, with_self, with_cross, last_x):
                prev = cur - 1
                at = {k: (v if isinstance(v, int) else sp.snap(v)) for k, v in dict(
                    prev=prev, normed=nth(cur, 7, 7), x2=nth(prev, 2, 2), i=prev, i_cross=cur - 2, i_next=cur).items()}
                if with_self:
                    until(sp, p_cT, at["prev"])
                    sp.dma_start(ctx_sb[:, :], ctx_in[at["i"]]).then_inc(s_ctx, 16)
                    if not last_x:
                        until(sp, d_ln["self"], at["normed"])
                        sp.dma_start(x_in[:, :], x[at["i_next"]]).then_inc(s_x_in, 16)
                    until(sp, d_x1, at["prev"])
                    sp.dma_start(x_res[:, :], x[at["i"]]).then_inc(s_x_res, 16)
                if with_cross:
                    until(sp, d_x2, at["x2"])
                    sp.dma_start(out[at["i_cross"]], x2[:, :]).then_inc(s_x2_stored, 16)

            body(1, True, False, False)
            body(2, True, True, False)
            with sp.Fori(3, B) as cur:
                body(cur, True, True, False)
            body(B, True, True, True)
            sp.wait_ge(p_y, B)
            for k in range(RING):
                load_weights(k, k)
            body(B + 1, False, True, True)

            sp.wait_ge(s_x2_stored, 16 * B)
            sp.wait_ge(s_scatter, 16 * TOPK * B)

            def load_expert(n, e, k, first):
                if not first:
                    freed = sp.snap(n - RING)
                    scaled = sp.snap(nth(n - RING, 2, 2))
                    until(sp, m_down, freed)
                    load_weights(e, k)
                    until(sp, m_y, scaled)
                sp.dma_start(rows[k][:, :], routed_e[e][:, 0:D + 1]).then_inc(s_rows[k], 16)
                sp.dma_start(share[k][:, :], share_of(e), allow_slow_non_contiguous=True).then_inc(s_rows[k], 16)

            for n in range(1, RING + 1):
                load_expert(n, n - 1, n - 1, True)
            with sp.Fori(1, E // RING) as j:
                for k in range(RING):
                    load_expert(j * RING + (k + 1), sp.snap(j * RING + k), k, False)
            sp.wait_ge(s_added, 16 * E)

        @block.tensor
        def _(pe):
            def turn(b, src, done):
                for t in range(KT):
                    last = pe.transpose(bank[:, b, t * P:(t + 1) * P], src[:, t * P:(t + 1) * P], idf[:, :])
                last.then_inc(done, 1)

            def turn_bf16(b, src, done):
                for t in range(KT):
                    last = pe.transpose(bank_bf16(b)[:, t * P:(t + 1) * P], src[:, t * P:(t + 1) * P], idb[:, :])
                last.then_inc(done, 1)

            def project(b, hi, lo, name):
                w_hi, w_lo = W[name]
                pe.matmul(bank[:, b, :], ones2[:, :], bias2[name][:, :], start=True, stop=False)
                for t in range(KT):
                    pe.matmul(bank[:, b, :], hi[:, t, :], w_hi[:, t, :], start=False, stop=False)
                    pe.matmul(bank[:, b, :], hi[:, t, :], w_lo[:, t, :], start=False, stop=False)
                for t in range(KT):
                    last = pe.matmul(bank[:, b, :], lo[:, t, :], w_hi[:, t, :], start=False, stop=(t == KT - 1))
                return last

            def project_int8(b, src, w, done):
                for t in range(KT):
                    last = pe.matmul(bank[:, b, :], src[:, t, :], w[:, t, :], start=(t == 0), stop=(t == KT - 1))
                last.then_inc(done, 1)

            def scores(b, g, q, kb, causal_mask, done):
                last = pe.matmul(bank[:, b, :], q[:, g, :], kb[:, g, :, :].rearrange("p j t -> p (j t)"),
                                 start=True, stop=not causal_mask)
                if causal_mask:
                    last = pe.matmul(bank[:, b, :], idb[:, :], mask_add[:, :].unsqueeze(1).to_broadcast([P, GH, P]),
                                     start=False, stop=True)
                last.then_inc(done, 1)

            def turn_probs(b, g, done):
                for j in range(GH):
                    last = pe.transpose(bank[:, b, j * P:(j + 1) * P], probs[:, g, j * P:(j + 1) * P], idf[:, :])
                last.then_inc(done, 1)

            def weigh(b, g, vals, done):
                for j in range(GH):
                    h = g * GH + j
                    at = (h % 8) * VW
                    last = pe.matmul(bank[:, b, at:at + VW], probsT[:, g, j * P:(j + 1) * P], vals[:, h, :],
                                     start=True, stop=True)
                last.then_inc(done, 1)

            def positions(m):
                until(pe, d_r1, nth(m, 11, 9))
                until(pe, d_r2, nth(m - 1, 6, 6))
                pe.matmul(bank[:, 4, E:2 * E], before[:, :], chosen[:, :], start=True, stop=False)
                pe.matmul(bank[:, 4, E:2 * E], ones_b[:, :], chosen_before[:, :], start=False,
                          stop=True).then_inc(p_pos, 1)

            def body(cur, with_self, with_cross, with_before):
                prev = cur - 1
                if with_self:
                    until(pe, d_ln["self"], nth(cur, 7, 7))
                    until(pe, a_pT, nth(prev, 2, 2))
                    turn(0, xn, p_xT)
                    until(pe, a_xT, cur)
                    until(pe, d_xT, cur)
                    until(pe, d_att, nth(prev, 4, 4))
                    project(1, xT_hi, xT_lo, "q")
                    project(2, xT_hi, xT_lo, "k").then_inc(p_qk, 1)
                if with_before:
                    positions(prev - 1)
                if with_cross:
                    until(pe, d_q8, nth(prev, 6, 6))
                    until(pe, a_x3T, prev - 1)
                    until(pe, d_x3T, prev - 1)
                    turn_bf16(3, xq8, p_q8T)
                    if with_before:
                        until(pe, d_r2, nth(prev - 1, 6, 2))
                    until(pe, a_q8T, prev)
                    project_int8(4, xq8T, xq_wT, p_cq)
                if with_self:
                    until(pe, s_ctx, cur * 16)
                    until(pe, a_aT, prev)
                    until(pe, d_aT, prev)
                    turn(5, ctx_sb, p_cT)
                if with_cross:
                    until(pe, a_cq, prev)
                    until(pe, d_x1, prev)
                    turn(6, cq, p_cqT)
                    until(pe, a_cqT, prev)
                    until(pe, a_xkbd, prev)
                    until(pe, d_pT, nth(prev, 2, 2))
                    scores(7, 0, cqT, xkbd, False, p_xs)
                    scores(0, 1, cqT, xkbd, False, p_xs)
                    if with_self:
                        until(pe, d_rope, nth(cur, 4, 3))
                    scores(1, 2, cqT, xkbd, False, p_xs)
                    scores(2, 3, cqT, xkbd, False, p_xs)
                if with_self:
                    if with_cross:
                        until(pe, a_q8T, prev)
                    project(3, xT_hi, xT_lo, "v").then_inc(p_v, 1)
                    until(pe, a_cT, cur)
                    until(pe, d_cT, cur)
                    project(4, cT_hi, cT_lo, "xk").then_inc(p_xk, 1)
                    until(pe, d_rope, nth(cur, 4, 4))
                    turn(5, roped[:, 0:D], p_qkT)
                    if with_cross:
                        until(pe, a_cqT, prev)
                    turn(6, roped[:, D:2 * D], p_qkT)
                if with_cross:
                    for g in range(NG):
                        until(pe, a_xexp, nth(prev, 4, g + 1))
                        turn_probs((7 + g) % 8, g, p_xpT)
                        if g == 0 and with_self:
                            until(pe, a_v, cur)
                            until(pe, a_xk, cur)
                        if g >= 1:
                            weigh_cross(g - 1, prev)
                    weigh_cross(3, prev)
                if with_self:
                    until(pe, d_qT, cur)
                    until(pe, a_kbd, cur)
                    scores(5, 0, qT, kbd, True, p_s)
                    scores(6, 1, qT, kbd, True, p_s)
                    scores(7, 2, qT, kbd, True, p_s)
                    scores(0, 3, qT, kbd, True, p_s)
                    project(1, cT_hi, cT_lo, "xv").then_inc(p_xv, 1)
                    until(pe, a_xk, cur)
                    turn(2, xk_sb, p_xkT)
                if with_cross:
                    until(pe, d_o8, nth(prev, 6, 6))
                    turn_bf16(3, xo8, p_o8T)
                    until(pe, a_o8T, prev)
                    project_int8(4, xo8T, xp_wT, p_xp)
                if with_self:
                    for g in range(NG):
                        until(pe, a_exp, nth(cur, 4, g + 1))
                        turn_probs((5 + g) % 8, g, p_pT)
                        if g == 0:
                            until(pe, a_xv, cur)
                            until(pe, a_xkbd, cur)
                        if g >= 1:
                            weigh_self(g - 1, cur)
                    weigh_self(3, cur)
                if with_cross:
                    until(pe, d_ln["ffn"], nth(prev, 7, 7))
                    turn(3, row[:, 0:D], p_x3T)
                    until(pe, a_x3T, prev)
                    until(pe, d_x3T, prev)
                    for t in range(KT):
                        pe.matmul(bank[:, 4, 0:E], x3T_hi[:, t, :], r_hi[:, t, :], start=(t == 0), stop=False)
                        pe.matmul(bank[:, 4, 0:E], x3T_hi[:, t, :], r_lo[:, t, :], start=False, stop=False)
                        last = pe.matmul(bank[:, 4, 0:E], x3T_lo[:, t, :], r_hi[:, t, :], start=False,
                                         stop=(t == KT - 1))
                    last.then_inc(p_log, 1)
                if with_self:
                    until(pe, d_att, nth(cur, 4, 4))
                    turn(5, att, p_aT)
                    until(pe, a_aT, cur)
                    until(pe, d_aT, cur)
                    project(6, attT_hi, attT_lo, "o").then_inc(p_y, 1)

            def weigh_cross(g, prev):
                until(pe, d_xpT if g % 2 == 0 else a_xpT, nth(prev, 2, g // 2 + 1))
                weigh(3 + g // 2, g, xv1, p_xpv)

            def weigh_self(g, cur):
                until(pe, d_pT if g % 2 == 0 else a_pT, nth(cur, 2, g // 2 + 1))
                weigh(1 + g // 2, g, v1, p_pv)

            pe.wait_ge(s_const, 16 * N_CONST)
            pe.wait_ge(s_init, 9)
            for n, (w8, bias_row) in enumerate(((0, None), (1, None))):
                pe.wait_ge(s_wprep, 6 + n + 1)
                src = roped[:, :].bitcast(BF16).rearrange("p (g n) -> p g n", g=KT) if n == 0 else \
                    rot[:, :].bitcast(BF16).rearrange("p (g n) -> p g n", g=KT)
                for t in range(KT):
                    for g in range(KT):
                        last = pe.transpose(bank_bf16(t)[:, g * P:(g + 1) * P], src[:, g, t * P:(t + 1) * P], idb[:, :])
                last.then_inc(s_wT, 1)
                pe.wait_ge(s_wTr, n + 1)
            pe.wait_ge(s_wprep, 9)
            for g in range(KT):
                last = pe.matmul(bank[:, 5, g * P:(g + 1) * P], ones_f[:, :], xn2[:, g * P:(g + 1) * P],
                                 start=True, stop=True)
            last.then_inc(s_wT, 1)
            pe.wait_ge(s_wsplit, 7)
            pe.wait_ge(s_wprep, 10)
            pe.wait_ge(s_wTr, 3)
            body(1, True, False, False)
            body(2, True, True, False)
            with pe.Fori(3, B + 1) as cur:
                body(cur, True, True, True)
            body(B + 1, False, True, True)
            positions(B)

            def turn_rows(n, k, use):
                until(pe, s_rows[k], use * 32)
                until(pe, m_xTc, n - 2)
                for t in range(KT):
                    last = pe.transpose(bank[:, k % 2, t * P:(t + 1) * P], rows[k][:, t:D:KT], idf[:, :])
                last.then_inc(m_xT, 1)

            def gate_up(n, k, use):
                until(pe, m_xTc, n)
                until(pe, s_ring[k], use * 48)
                until(pe, m_h, n - 2)
                for t in range(KT):
                    last = pe.matmul(bank[:, 2 + k % 2, 0:2 * F], rowsT[k % 2][:, t * P:(t + 1) * P],
                                     w_gu[k][:, :, t, :], start=(t == 0), stop=(t == KT - 1))
                last.then_inc(m_gu, 1)

            def down(n, k):
                until(pe, m_hTc, n)
                until(pe, m_y, nth(n - 2, 2, 2))
                for u in range(2):
                    last = pe.matmul(bank[:, 6 + k % 2, :], hiddenT[k % 2][:, u * P:(u + 1) * P], w_dn[k][:, u, :],
                                     start=(u == 0), stop=(u == 1))
                last.then_inc(m_down, 1)

            def turn_hidden(n, k):
                until(pe, m_h, n)
                until(pe, m_hTc, n - 2)
                for u in range(2):
                    last = pe.transpose(bank[0:FP, 4 + k % 2, u * P:(u + 1) * P], hidden[k % 2][:, u:F:2], idf[:, :])
                last.then_inc(m_hT, 1)

            def step(n, k, j):
                turn_rows(n, k, j + 1)
                if not isinstance(n, int) or n >= 2:
                    gate_up(n - 1, (k - 1) % RING, j + 1 if k >= 1 else j)
                if not isinstance(n, int) or n >= 3:
                    down(n - 2, (k - 2) % RING)
                if not isinstance(n, int) or n >= 2:
                    turn_hidden(n - 1, (k - 1) % RING)

            for k in range(RING):
                step(k + 1, k, 0)
            with pe.Fori(1, E // RING) as j:
                for k in range(RING):
                    step(j * RING + (k + 1), k, j)
            gate_up(E, RING - 1, E // RING)
            down(E - 1, RING - 2)
            turn_hidden(E, RING - 1)
            down(E, RING - 1)

        @block.scalar
        def _(act):
            def copy(dst, src, done):
                act.activation(dst, src, ACT.Copy).then_inc(done, 1)

            def spread_keys(b, kb, done, before_sem, value):
                for j in range(GH):
                    last = act.activation(kb[j * DH:(j + 1) * DH, :, j, :],
                                          bank[j * DH:(j + 1) * DH, b, :].rearrange("p (g t) -> p g t", g=NG), ACT.Copy)
                last.then_inc(done, 1)

            def exponentials(b, g, maxes, done, value):
                until(act, maxes, value)
                for j in range(GH):
                    h = g * GH + j
                    last = act.activation(probs[:, g, j * P:(j + 1) * P], bank[:, b, j * P:(j + 1) * P], ACT.Exp,
                                          bias=negmax[:, h:h + 1])
                last.then_inc(done, 1)

            def body(cur, with_self, with_cross):
                prev = cur - 1
                if with_self:
                    until(act, p_xT, cur)
                    until(act, p_v, prev)
                    copy(xT_hi[:, :, :].rearrange("p t n -> p (t n)"), bank[:, 0, :], a_xT)
                if with_cross:
                    until(act, p_q8T, prev)
                    until(act, p_xp, prev - 1)
                    copy(xq8T[:, :, :].rearrange("p t n -> p (t n)"), bank_bf16(3), a_q8T)
                    until(act, p_cq, prev)
                    until(act, p_xkT, prev)
                    act.activation(cq[:, :], bank[:, 4, :], ACT.Copy, scale=x_s).then_inc(a_cq, 1)
                if with_self:
                    until(act, p_cT, cur)
                    until(act, p_xv, prev)
                    copy(cT_hi[:, :, :].rearrange("p t n -> p (t n)"), bank[:, 5, :], a_cT)
                if with_cross:
                    until(act, p_cqT, prev)
                    until(act, p_s, nth(prev, 4, 4))
                    for g in range(NG):
                        last = act.activation(cqT[:, g, :], bank[:, 6, g * P:(g + 1) * P], ACT.Identity,
                                              scale=xq_ws[:, g:g + 1], bias=xq_bs[:, g:g + 1])
                    last.then_inc(a_cqT, 1)
                    until(act, p_pT, nth(prev, 4, 4))
                    for g in range(NG):
                        exponentials((7 + g) % 8, g, d_xmax, a_xexp, nth(prev, 4, g + 1))
                if with_self:
                    until(act, p_v, cur)
                    until(act, p_pv, nth(prev, 4, 4))
                    copy(v1[:, :, 0:DH], bank[:, 3, :].rearrange("p (h d) -> p h d", h=H), a_v)
                    until(act, p_xk, cur)
                    until(act, p_xkT, prev)
                    copy(xk_sb[:, :], bank[:, 4, :], a_xk)
                    until(act, p_qkT, nth(cur, 2, 2))
                    until(act, p_s, nth(prev, 4, 4))
                    spread_keys(6, kbd, a_kbd, None, None)
                if with_cross:
                    for g in (1, 3):
                        until(act, p_xpT, nth(prev, 4, g + 1))
                        until(act, p_pv, nth(prev, 4, 4))
                        copy(probsT[:, g, :], bank[:, (7 + g) % 8, :], a_xpT)
                if with_self:
                    if with_cross:
                        until(act, p_xpT, nth(prev, 4, 4))
                    for g in range(NG):
                        exponentials((5 + g) % 8, g, d_max, a_exp, nth(cur, 4, g + 1))
                    until(act, p_xv, cur)
                    until(act, p_xpv, nth(prev, 4, 4))
                    copy(xv1[:, :, 0:DH], bank[:, 1, :].rearrange("p (h d) -> p h d", h=H), a_xv)
                    until(act, p_xkT, cur)
                    until(act, p_xs, nth(prev, 4, 4))
                    spread_keys(2, xkbd, a_xkbd, None, None)
                if with_cross:
                    until(act, p_o8T, prev)
                    until(act, p_cq, prev)
                    copy(xo8T[:, :, :].rearrange("p t n -> p (t n)"), bank_bf16(3), a_o8T)
                if with_self:
                    for g in (1, 3):
                        until(act, p_pT, nth(cur, 4, g + 1))
                        if with_cross:
                            until(act, p_xpv, nth(prev, 4, 4))
                        copy(probsT[:, g, :], bank[:, (5 + g) % 8, :], a_pT)
                if with_cross:
                    until(act, p_x3T, prev)
                    until(act, p_y, prev)
                    copy(x3T_hi[:, :, :].rearrange("p t n -> p (t n)"), bank[:, 3, :], a_x3T)
                    until(act, d_r1, nth(prev, 11, 1))
                    act.activation(router[:, 0, :], bank[:, 4, 0:E], ACT.Exp, bias=l_max,
                                   accum_out=e_sum).then_inc(a_rexp, 1)
                if with_self:
                    until(act, p_aT, cur)
                    until(act, p_y, prev)
                    if with_cross:
                        until(act, p_log, prev)
                    copy(attT_hi[:, :, :].rearrange("p t n -> p (t n)"), bank[:, 5, :], a_aT)

            for n, dst in enumerate((xq_wT, xp_wT)):
                act.wait_ge(s_wT, n + 1)
                for t in range(KT):
                    last = act.activation(dst[:, t, :], bank_bf16(t), ACT.Copy)
                last.then_inc(s_wTr, 1)
            act.wait_ge(s_wT, 3)
            act.activation(xp_row[:, :], bank[:, 5, :], ACT.Copy).then_inc(s_wTr, 1)
            act.wait_ge(s_wprep, 10)
            act.wait_ge(s_init, 6)
            body(1, True, False)
            body(2, True, True)
            with act.Fori(3, B + 1) as cur:
                body(cur, True, True)
            body(B + 1, False, True)

            def copy_rows(n, k):
                until(act, m_xT, n)
                until(act, m_gu, n - 2)
                copy(rowsT[k % 2][:, :], bank[:, k % 2, :], m_xTc)

            def silu(n, k):
                until(act, m_gu, n)
                until(act, m_h, n - 2)
                act.activation(gated[k % 2], bank[:, 2 + k % 2, 0:F], ACT.Silu).then_inc(m_silu, 1)

            for k in range(RING):
                copy_rows(k + 1, k)
                if k >= 1:
                    silu(k, k - 1)
            with act.Fori(1, E // RING) as j:
                for k in range(RING):
                    copy_rows(j * RING + (k + 1), k)
                    silu(j * RING + k, (k - 1) % RING)
            silu(E, RING - 1)

        @block.vector
        def _(dve):
            def norm_start(kind, src, m):
                s, c = d_ln[kind], ln[kind]
                dve.bn_stats(c["stats"], src).then_inc(s, 1)
                until(dve, s, nth(m, 7, 1))
                apart(dve)
                dve.bn_aggr(c["mv"], c["stats"]).then_inc(s, 1)
                until(dve, s, nth(m, 7, 2))
                dve.tensor_scalar(c["v"], c["mv"][:, 1:2], LN_EPS, None, ALU.add).then_inc(s, 1)

            def norm_end(kind, src, dst, m):
                s, c = d_ln[kind], ln[kind]
                until(dve, g_pow[kind], m)
                dve.scalar_tensor_tensor(out=c["t"], in0=c["v"], scalar=c["r0"], in1=c["r0"], op0=ALU.mult,
                                         op1=ALU.mult).then_inc(s, 1)
                until(dve, s, nth(m, 7, 4))
                dve.tensor_scalar(c["u"], c["t"], -0.5, 1.5, ALU.mult, ALU.add).then_inc(s, 1)
                until(dve, s, nth(m, 7, 5))
                dve.tensor_tensor(c["r"], c["u"], c["r0"], ALU.mult).then_inc(s, 1)
                until(dve, s, nth(m, 7, 6))
                dve.tensor_scalar(dst, src, c["mv"][:, 0:1], c["r"], ALU.subtract, ALU.mult).then_inc(s, 1)

            def quantise(src, tmp, dst, amax, scale, rscale, s, m, dst_free=None, dst_value=0):
                dve.tensor_reduce(amax, src, AX_X, ALU.max, apply_absolute_value=True).then_inc(s, 1)
                until(dve, s, nth(m, 6, 1))
                dve.tensor_scalar(scale, amax, 1.0 / QMAX, 1e-8, ALU.mult, ALU.max).then_inc(s, 1)
                until(dve, s, nth(m, 6, 2))
                dve.reciprocal(rscale, scale).then_inc(s, 1)
                until(dve, s, nth(m, 6, 3))
                dve.tensor_scalar(tmp, src, rscale, ROUND, ALU.mult, ALU.add).then_inc(s, 1)
                until(dve, s, nth(m, 6, 4))
                dve.tensor_scalar(tmp, tmp, ROUND + QMAX, ROUND - QMAX, ALU.min, ALU.max).then_inc(s, 1)
                until(dve, s, nth(m, 6, 5))
                if dst_free is not None:
                    until(dve, dst_free, dst_value)
                dve.tensor_scalar(dst, tmp, ROUND, None, ALU.subtract).then_inc(s, 1)

            def low_part(dst, b, hi, done):
                dve.tensor_tensor(dst[:, :, :].rearrange("p t n -> p (t n)"), bank[:, b, :],
                                  hi[:, :, :].rearrange("p t n -> p (t n)").bitcast(F32), ALU.subtract).then_inc(done, 1)

            def group_max(b, g, ready, value, done):
                until(dve, ready, value)
                dve.tensor_reduce(negmax[:, g * GH:(g + 1) * GH], bank[:, b, :].rearrange("p (j k) -> p j k", j=GH),
                                  AX_X, ALU.max, negate=True).then_inc(done, 1)

            def average(b, dst, total, done, m, ready):
                for half_ in range(2):
                    until(dve, ready, nth(m, 4, 2 + 2 * half_))
                    o = bank[:, b + half_, 0:8 * VW].rearrange("p (h d) -> p h d", h=8)
                    t = total[:, 8 * half_:8 * half_ + 8]
                    dve.reciprocal(t, o[:, :, DH]).then_inc(done, 1)
                    until(dve, done, nth(m, 4, 2 * half_ + 1))
                    dve.tensor_tensor(dst[:, 256 * half_:256 * half_ + 256].rearrange("p (h d) -> p h d", h=8),
                                      o[:, :, 0:DH], t.unsqueeze(2).to_broadcast([P, 8, DH]),
                                      ALU.mult).then_inc(done, 1)

            def route_slots(m):
                s = d_r2
                m01, ok, at, key = (router[:, k, :] for k in (2, 3, 4, 5))
                until(dve, p_pos, m)
                dve.scalar_tensor_tensor(out=ok, in0=bank[:, 4, E:2 * E], scalar=float(CAP), in1=m01,
                                         op0=ALU.is_lt, op1=ALU.mult).then_inc(s, 1)
                dve.scalar_tensor_tensor(out=at, in0=bank[:, 4, E:2 * E], scalar=-1.0, in1=slot_base[:, :],
                                         op0=ALU.mult, op1=ALU.add).then_inc(s, 1)
                until(dve, s, nth(m, 6, 2))
                dve.tensor_tensor(key, ok, at, ALU.mult).then_inc(s, 1)
                until(dve, s, nth(m, 6, 3))
                apart(dve)
                dve.max(key8, key).then_inc(s, 1)
                until(dve, s, nth(m, 6, 4))
                until(dve, s_scatter, nth(m - 1, 16 * TOPK, 16 * TOPK))
                dve.tensor_scalar(slots[:, :], key8, -1.0, float(NOWHERE), ALU.mult, ALU.add).then_inc(s, 1)
                dve.tensor_tensor(chosen_before[:, :], chosen_before[:, :], chosen[:, :], ALU.add).then_inc(s, 1)

            def body(cur, with_self, with_cross, with_before, last_x):
                prev = cur - 1
                if with_self:
                    until(dve, a_xT, cur)
                    until(dve, p_v, prev)
                    low_part(xT_lo, 0, xT_hi, d_xT)
                if with_cross:
                    until(dve, p_y, prev)
                    until(dve, s_x_res, prev * 16)
                    dve.tensor_tensor(x1[:, :], bank[:, 6, :], x_res[:, :], ALU.add).then_inc(d_x1, 1)
                    until(dve, d_x1, prev)
                    norm_start("cross", x1[:, :], prev)
                if with_before:
                    route_slots(prev - 1)
                if with_cross:
                    norm_end("cross", x1[:, :], xn2[:, :], prev)
                    until(dve, d_ln["cross"], nth(prev, 7, 7))
                    until(dve, a_cq, prev - 1)
                    quantise(xn2[:, :], xatt[:, :], xq8[:, :], x_amax, x_s, x_rs, d_q8, prev, p_o8T, prev - 1)
                if with_self:
                    until(dve, p_qk, cur)
                    until(dve, p_qkT, nth(prev, 2, 2))
                    until(dve, p_pv, nth(prev, 4, 4))
                    qk = bank[:, 1:3, :].rearrange("p b (h d) -> p (b h) d", h=H)
                    ro = roped[:, :].rearrange("p (h d) -> p h d", d=DH)
                    rt = rot[:, :].rearrange("p (h d) -> p h d", d=DH)
                    hd = DH // 2
                    heads = 2 * H
                    dve.tensor_tensor(ro, qk, cos_sb[:, :].unsqueeze(1).to_broadcast([P, heads, DH]),
                                      ALU.mult).then_inc(d_rope, 1)
                    dve.tensor_tensor(rt[:, :, 0:hd], qk[:, :, hd:DH],
                                      sin_sb[:, 0:hd].unsqueeze(1).to_broadcast([P, heads, hd]),
                                      ALU.mult).then_inc(d_rope, 1)
                    dve.tensor_tensor(rt[:, :, hd:DH], qk[:, :, 0:hd],
                                      sin_sb[:, hd:DH].unsqueeze(1).to_broadcast([P, heads, hd]),
                                      ALU.mult).then_inc(d_rope, 1)
                    until(dve, d_rope, nth(cur, 4, 3))
                    dve.tensor_tensor(roped[:, :], roped[:, :], rot[:, :], ALU.add).then_inc(d_rope, 1)
                    until(dve, a_cT, cur)
                    until(dve, p_xv, prev)
                    low_part(cT_lo, 5, cT_hi, d_cT)
                if with_cross:
                    until(dve, a_exp, nth(prev, 4, 4))
                    for g in range(NG):
                        group_max((7 + g) % 8, g, p_xs, nth(prev, 4, g + 1), d_xmax)
                if with_self:
                    if not last_x:
                        until(dve, s_x_in, (cur + 1) * 16)
                        norm_start("self", x_in[:, :], cur + 1)
                    until(dve, p_qkT, nth(cur, 2, 1))
                    until(dve, p_s, nth(prev, 4, 4))
                    if with_cross:
                        until(dve, p_xs, nth(prev, 4, 4))
                    dve.tensor_scalar(qT[:, :, :].rearrange("p g t -> p (g t)"), bank[:, 5, :], SCALE, None,
                                      ALU.mult).then_inc(d_qT, 1)
                    if not last_x:
                        until(dve, p_xT, cur)
                        norm_end("self", x_in[:, :], xn[:, :], cur + 1)
                if with_cross:
                    for g in (0, 2):
                        until(dve, p_xpT, nth(prev, 4, g + 1))
                        until(dve, p_pv, nth(prev, 4, 4))
                        dve.tensor_copy(probsT[:, g, :], bank[:, (7 + g) % 8, :]).then_inc(d_xpT, 1)
                    average(3, xatt, xsums, d_xatt, prev, p_xpv)
                if with_self:
                    if with_cross:
                        until(dve, a_xexp, nth(prev, 4, 4))
                    for g in range(NG):
                        group_max((5 + g) % 8, g, p_s, nth(cur, 4, g + 1), d_max)
                if with_cross:
                    until(dve, d_xatt, nth(prev, 4, 4))
                    quantise(xatt[:, :], xn2[:, :], xo8[:, :], o_amax, o_s, o_rs, d_o8, prev, p_q8T, prev)
                if with_self:
                    for g in (0, 2):
                        until(dve, p_pT, nth(cur, 4, g + 1))
                        if with_cross:
                            until(dve, p_xpv, nth(prev, 4, 4))
                        dve.tensor_copy(probsT[:, g, :], bank[:, (5 + g) % 8, :]).then_inc(d_pT, 1)
                if with_cross:
                    until(dve, p_xp, prev)
                    until(dve, s_x2_stored, (prev - 1) * 16)
                    until(dve, d_o8, nth(prev, 6, 6))
                    dve.scalar_tensor_tensor(out=x2[:, :], in0=bank[:, 4, :], scalar=o_s, in1=xp_row[:, :],
                                             op0=ALU.mult, op1=ALU.mult).then_inc(d_x2, 1)
                    until(dve, d_x2, nth(prev, 2, 1))
                    until(dve, g_x1b, prev)
                    dve.tensor_tensor(x2[:, :], x2[:, :], x1[:, :], ALU.add).then_inc(d_x2, 1)
                    until(dve, d_x2, nth(prev, 2, 2))
                    norm_start("ffn", x2[:, :], prev)
                if with_self:
                    average(1, att, sums, d_att, cur, p_pv)
                if with_cross:
                    until(dve, s_scatter, nth(prev - 1, 16 * TOPK, 16 * TOPK))
                    norm_end("ffn", x2[:, :], row[:, 0:D], prev)
                    until(dve, a_x3T, prev)
                    until(dve, p_y, prev)
                    low_part(x3T_lo, 3, x3T_hi, d_x3T)
                if with_self:
                    if with_cross:
                        route_max(prev)
                    until(dve, a_aT, cur)
                    until(dve, p_y, prev)
                    low_part(attT_lo, 5, attT_hi, d_aT)
                elif with_cross:
                    route_max(prev)
                if with_cross:
                    route_choose_rest(prev)

            def route_max(m):
                until(dve, p_log, m)
                dve.tensor_reduce(l_max, bank[:, 4, 0:E], AX_X, ALU.max, negate=True).then_inc(d_r1, 1)

            def route_choose_rest(m):
                s = d_r1
                ex, left, m01 = (router[:, k, :] for k in (0, 1, 2))
                until(dve, a_rexp, m)
                apart(dve)
                dve.max(top8, ex).then_inc(s, 1)
                dve.reciprocal(e_rs, e_sum).then_inc(s, 1)
                until(dve, s, nth(m, 11, 3))
                apart(dve)
                dve.match_replace(left, top8, ex, -1.0).then_inc(s, 1)
                dve.reduce_sum(t_sum, top8, AX_X).then_inc(s, 1)
                until(dve, s, nth(m, 11, 5))
                dve.tensor_scalar(t_den, t_sum, e_rs, 1e-20, ALU.mult, ALU.add).then_inc(s, 1)
                dve.tensor_scalar(m01, left, 0.0, None, ALU.is_lt).then_inc(s, 1)
                until(dve, s, nth(m, 11, 7))
                until(dve, p_pos, m - 1)
                dve.reciprocal(t_rd, t_den).then_inc(s, 1)
                dve.tensor_copy(chosen[:, :], m01).then_inc(s, 1)
                until(dve, s, nth(m, 11, 9))
                dve.tensor_tensor(t_f, e_rs, t_rd, ALU.mult).then_inc(s, 1)
                until(dve, s, nth(m, 11, 10))
                dve.scalar_tensor_tensor(out=row[:, D + 1:ROW], in0=ex, scalar=t_f, in1=m01, op0=ALU.mult,
                                         op1=ALU.mult).then_inc(s, 1)

            dve.wait_ge(s_init, 6)
            dve.wait_ge(s_x_in, 16)
            norm_start("self", x_in[:, :], 1)
            norm_end("self", x_in[:, :], xn[:, :], 1)
            step = [0]

            def chained(instruction):
                step[0] += 1
                instruction.then_inc(d_wchain, 1)
                dve.wait_ge(d_wchain, step[0])

            for n, (name, _) in enumerate(weights_in):
                dve.wait_ge(s_wload[n % 2], 16 * (n // 2 + 1))
                hi, lo = W[name]
                chained(dve.tensor_copy(hi[:, :, :], STAGE[n % 2][:, :, :]))
                dve.tensor_tensor(lo[:, :, :], STAGE[n % 2][:, :, :], hi[:, :, :].bitcast(F32),
                                  ALU.subtract).then_inc(s_wsplit, 1)
            dve.wait_ge(s_wload[0], 16 * 4)
            staged = STAGE[0][:, 0, 0:KT * E].rearrange("p (t e) -> p t e", t=KT)
            chained(dve.tensor_copy(r_hi[:, :, :], staged))
            dve.tensor_tensor(r_lo[:, :, :], staged, r_hi[:, :, :].bitcast(F32), ALU.subtract).then_inc(s_wsplit, 1)
            dve.wait_ge(s_const, 16 * N_CONST)
            hi_b, lo_b = x1[0:2, :].bitcast(F32R), x2[0:2, :]
            for n, (name, _) in enumerate(bias_in):
                dve.wait_ge(s_bload, 16 * (n + 1))
                chained(dve.tensor_copy(hi_b, bias_f[:, 0:D]))
                chained(dve.tensor_tensor(lo_b, bias_f[:, 0:D], x1[0:2, :], ALU.subtract))
                chained(dve.tensor_scalar(lo_b, lo_b, pick[:, 1:2], None, ALU.mult))
                dve.scalar_tensor_tensor(out=bias2[name][:, :], in0=x1[0:2, :], scalar=pick[:, 0:1], in1=lo_b,
                                         op0=ALU.mult, op1=ALU.add).then_inc(s_wprep, 1)
                dve.wait_ge(s_wprep, n + 1)
            for n, (src, dst, ws) in enumerate(((STAGE[2], roped, xq_ws), (STAGE[3], rot, xp_ws))):
                whole = dst[:, :].bitcast(BF16).rearrange("p (g n) -> p g n", g=KT)
                am = rstep[:, 0:KT]
                rs = rstep[:, KT:2 * KT]
                chained(dve.tensor_reduce(am, src[:, :, :], AX_X, ALU.max, apply_absolute_value=True))
                chained(dve.tensor_scalar(ws[:, :], am, 1.0 / QMAX, 1e-8, ALU.mult, ALU.max))
                chained(dve.reciprocal(rs, ws[:, :]))
                for g in range(KT):
                    chained(dve.tensor_scalar(src[:, g, :], src[:, g, :], rs[:, g:g + 1], ROUND, ALU.mult, ALU.add))
                chained(dve.tensor_scalar(src[:, :, :], src[:, :, :], ROUND + QMAX, ROUND - QMAX, ALU.min, ALU.max))
                dve.tensor_scalar(whole, src[:, :, :], ROUND, None, ALU.subtract).then_inc(s_wprep, 1)
                dve.wait_ge(s_wprep, 7 + n)
            for g in range(KT):
                last = dve.tensor_scalar(xn2[:, g * P:(g + 1) * P], idf[:, :], xp_ws[:, g:g + 1], None, ALU.mult)
            last.then_inc(s_wprep, 1)
            chained(dve.tensor_scalar(xq_ws[:, :], xq_ws[:, :], SCALE, None, ALU.mult))
            chained(dve.tensor_scalar(xq_bs[:, :], xq_bs[:, :], SCALE, None, ALU.mult))
            dve.memset(kbd[:, :, :, :], 0.0).then_inc(d_wchain, 1)
            dve.memset(xkbd[:, :, :, :], 0.0).then_inc(d_wchain, 1)
            step[0] += 2
            dve.wait_ge(d_wchain, step[0])
            dve.memset(chosen_before[:, :], 0.0).then_inc(s_wprep, 1)
            dve.wait_ge(s_wT, 3)
            dve.wait_ge(s_init, 9)
            body(1, True, False, False, False)
            body(2, True, True, False, False)
            with dve.Fori(3, B) as cur:
                body(cur, True, True, True, False)
            body(B, True, True, True, True)
            body(B + 1, False, True, True, True)
            route_slots(B)

            def multiply(n, k):
                until(dve, m_silu, n)
                until(dve, m_hT, n - 2)
                dve.tensor_tensor(hidden[k % 2], bank[:, 2 + k % 2, F:2 * F], gated[k % 2],
                                  ALU.mult).then_inc(m_h, 1)

            def scale_output(n, k, use):
                until(dve, s_added, (n - 2) * 16)
                until(dve, s_rows[k], use * 32)
                dve.tensor_copy(token_of[k % 2], rows[k][:, D:D + 1]).then_inc(m_y, 1)
                until(dve, m_down, n)
                dve.tensor_scalar(scaled_y[k % 2][:, :], bank[:, 6 + k % 2, :], share[k], None,
                                  ALU.mult).then_inc(m_y, 1)

            def copy_hidden(n, k):
                until(dve, m_hT, n)
                until(dve, m_down, n - 2)
                dve.tensor_copy(hiddenT[k % 2], bank[0:FP, 4 + k % 2, 0:2 * P]).then_inc(m_hTc, 1)

            def step(n, k, j):
                if not isinstance(n, int) or n >= 2:
                    multiply(n - 1, (k - 1) % RING)
                if not isinstance(n, int) or n >= 3:
                    scale_output(n - 2, (k - 2) % RING, j + 1 if k >= 2 else j)
                if not isinstance(n, int) or n >= 2:
                    copy_hidden(n - 1, (k - 1) % RING)

            for k in range(RING):
                step(k + 1, k, 0)
            with dve.Fori(1, E // RING) as j:
                for k in range(RING):
                    step(j * RING + (k + 1), k, j)
            multiply(E, RING - 1)
            scale_output(E - 1, RING - 2, E // RING)
            copy_hidden(E, RING - 1)
            scale_output(E, RING - 1, E // RING)

        @block.gpsimd
        def _(pool):
            def rsqrt(kind, m):
                c = ln[kind]
                until(pool, d_ln[kind], nth(m, 7, 3))
                pool.tensor_tensor(c["r0"], c["v"], half[:, :], ALU.pow).then_inc(g_pow[kind], 1)

            def scatter(m):
                until(pool, d_r2, nth(m, 6, 5))
                until(pool, g_tok, m)
                apart(pool)
                for k in range(TOPK):
                    pool.indirect_dma_start(routed, bass.IndirectOffsetOnAxis(ap=slots[:, k:k + 1], axis=0),
                                            row[:, :], None, bounds_check=SLOTS - 1,
                                            oob_is_err=False).then_inc(s_scatter, 16)

            def number_tokens(m):
                until(pool, s_scatter, nth(m - 1, 16 * TOPK, 16 * TOPK))
                apart(pool)
                pool.tensor_scalar(row[:, D:D + 1], row[:, D:D + 1], float(P), None, ALU.add).then_inc(g_tok, 1)

            def body(cur, with_self, with_cross, with_before, last_x):
                prev = cur - 1
                if with_cross:
                    rsqrt("cross", prev)
                    until(pool, d_ln["cross"], nth(prev, 7, 7))
                    pool.tensor_tensor(x1[:, :], x1[:, :], xp_bias[:, :], ALU.add).then_inc(g_x1b, 1)
                if with_self and not last_x:
                    rsqrt("self", cur + 1)
                if with_before:
                    scatter(prev - 1)
                if with_cross:
                    rsqrt("ffn", prev)
                    number_tokens(prev)

            pool.memset(ones_b[:, :], 1.0).then_inc(s_init, 1)
            pool.memset(ones_f[:, :], 1.0).then_inc(s_init, 1)
            pool.memset(half[:, :], -0.5).then_inc(s_init, 1)
            pool.memset(v1[:, :, DH:VW], 1.0).then_inc(s_init, 1)
            pool.memset(xv1[:, :, DH:VW], 1.0).then_inc(s_init, 1)
            pool.memset(row[:, :], 0.0).then_inc(s_init2, 1)
            pool.wait_ge(s_init, 2)
            pool.tensor_copy(ones2[:, :], ones_f[0:2, :]).then_inc(s_init, 1)
            pool.wait_ge(s_init2, 1)
            pool.iota(row[:, D:D + 1], pattern=[[0, 1]], base=TOKENS, channel_multiplier=1,
                      allow_small_or_imprecise_dtypes=True).then_inc(s_init2, 1)
            rsqrt("self", 1)
            pool.wait_ge(s_const, 16 * N_CONST)
            for dst, src in ((idb, idf[:, :]), (mask_add, att[:, 0:P]), (before, att[:, P:2 * P])):
                pool.tensor_copy(dst[:, :], src).then_inc(s_init, 1)
            pool.wait_ge(s_filled, 16 * 5)
            pool.wait_ge(s_init2, 2)
            pool.iota(row[:, D:D + 1], pattern=[[0, 1]], base=-P, channel_multiplier=1,
                      allow_small_or_imprecise_dtypes=True).then_inc(s_init2, 1)
            pool.wait_ge(s_init2, 3)
            body(1, True, False, False, False)
            body(2, True, True, False, False)
            with pool.Fori(3, B) as cur:
                body(cur, True, True, True, False)
            body(B, True, True, True, True)
            body(B + 1, False, True, True, True)
            scatter(B)
            pool.wait_ge(s_scatter, 16 * TOPK * B)

            def add_output(n, k):
                until(pool, m_y, nth(n, 2, 2))
                until(pool, s_added, (n - 1) * 16)
                apart(pool)
                pool.indirect_dma_start(out.rearrange("b p d -> (b p) d"),
                                        bass.IndirectOffsetOnAxis(ap=token_of[k % 2], axis=0),
                                        scaled_y[k % 2][:, :], None, bounds_check=TOKENS + P - 1,
                                        oob_is_err=True, compute_op=ALU.add).then_inc(s_added, 16)

            for k in range(RING):
                add_output(k + 1, k)
            with pool.Fori(1, E // RING) as j:
                for k in range(RING):
                    add_output(j * RING + (k + 1), k)
            pool.wait_ge(s_added, 16 * E)


def tables():
    theta = np.float32(10000.0) ** (np.float32(-2.0) * np.arange(DH // 2, dtype=np.float32) / np.float32(DH))
    ang = np.arange(1, P + 1, dtype=np.float32)[:, None] * theta[None, :].astype(np.float32)
    cos, sin = np.cos(ang), np.sin(ang)
    p = np.arange(P)
    return {
        "cos_t": np.concatenate([cos, cos], 1).astype(np.float32),
        "sin_t": np.concatenate([-sin, sin], 1).astype(np.float32),
        "ident_f": np.eye(P, dtype=np.float32),
        "causal": np.where(p[None, :] > p[:, None], MASKED, 0.0).astype(np.float32),
        "prior": (p[:, None] < p[None, :]).astype(np.float32),
        "slot0": np.tile(np.float32(NOWHERE) - CAP * np.arange(E, dtype=np.float32), (P, 1)).astype(np.float32),
    }


def kernel(**inputs):
    from concourse import bacc
    from concourse.bass_utils import run_bass_kernel_spmd

    a = {k: np.asarray(v) for k, v in inputs.items()}
    wkv, bkv = a["L0_xattn_wkv"], a["L0_xattn_bkv"]
    arrays = {
        "x": a["x"], "ctx_in": a["ctx_2048"],
        "qT_w": a["L0_attn_Wq"].T, "kT_w": a["L0_attn_Wk"].T, "vT_w": a["L0_attn_Wv"].T, "oT_w": a["L0_attn_Wo"].T,
        "xkT_w": wkv[:D].T, "xvT_w": wkv[D:].T, "xq_w": a["L0_xattn_wq"], "xp_w": a["L0_xattn_wp"],
        "bq": a["L0_attn_bq"], "bk": a["L0_attn_bk"], "bv": a["L0_attn_bv"], "bo": a["L0_attn_bo"],
        "xbq": a["L0_xattn_bq"], "xbk": bkv[:D], "xbv": bkv[D:], "xbp": a["L0_xattn_bp"],
        "routerT": a["L0_ffn_router_w"].T, "w_gate": a["L0_ffn_w_gate"], "w_up": a["L0_ffn_w_up"],
        "w_down": a["L0_ffn_w_down"], **tables(),
    }
    arrays = {k: np.ascontiguousarray(v) for k, v in arrays.items()}
    nc = bacc.Bacc("TRN2", target_bir_lowering=False, num_devices=1)
    args = {k: nc.dram_tensor(f"in_{k}", v.shape, mybir.dt.from_np(v.dtype), kind="ExternalInput").ap()
            for k, v in arrays.items()}
    out = nc.dram_tensor("out", (B + 1, P, D), F32, kind="ExternalOutput").ap()
    layer(nc, out=out, **args)
    result = run_bass_kernel_spmd(nc, [{f"in_{k}": v for k, v in arrays.items()}], core_ids=[0])
    return result.results[0]["out"][:B]
```

```python
from contextlib import ExitStack

import numpy as np

import concourse.bass as bass
from concourse import mybir

F32 = mybir.dt.float32
F32R = mybir.dt.float32r
BF16 = mybir.dt.bfloat16
U32 = mybir.dt.uint32
ALU = mybir.AluOpType
ACT = mybir.ActivationFunctionType
AX_X = mybir.AxisListType.X

P = 128
B = 32
D = 512
KT = D // P
H = 16
DH = D // H
NG = 4
GH = H // NG
VW = DH + 1
E = 64
TOPK = 8
CAP = 128
F = 192
FP = F // 2
ROW = D + 1 + E
TOKENS = B * P
SLOTS = E * CAP
NOWHERE = 2 * SLOTS
SCALE = float(DH) ** -0.5
LN_EPS = 1e-5
ROUND = 1.5 * 2.0 ** 23
QMAX = 127.0
MASKED = -1e30
RING = 8


CROSS_BANK = (0, 4, 3, 1)
SELF_BANK = (2, 6, 0, 4)


def nth(ordinal, per, j):
    return (ordinal - 1) * per + j


def until(eng, semaphore, value):
    if not isinstance(value, int) or value > 0:
        eng.wait_ge(semaphore, value)


def apart(eng):
    eng.nop(nofuse=True)


def layer(nc, x, ctxT_in, qT_w, kT_w, vT_w, oT_w, xkT_w, xvT_w, xq_w, xp_w, bq, bk, bv, bo, xbq, xbk, xbv,
          xbp, routerT, w_gate, w_up, w_down, cos_t, sin_t, ident_f, causal, prior, slot0, out):
    routed = nc.dram_tensor("routed", (SLOTS, ROW), F32).ap()
    st = ExitStack()

    def sb(name, shape, dt=F32):
        return st.enter_context(nc.sbuf_tensor(name, shape, dt))

    def sem(name):
        return st.enter_context(nc.semaphore(name))

    with st:
        bank = st.enter_context(nc.psum_tensor("bank", [P, 8, 512], F32))

        def bank_bf16(b):
            return bank[:, b, :].bitcast(BF16)[:, 0:D]

        idf = sb("idf", [P, P])
        idb = sb("idb", [P, P], BF16)
        mask_add = sb("mask_add", [P, P], BF16)
        before = sb("before", [P, P], BF16)
        ones_b = sb("ones_b", [P, P], BF16)
        ones_f = sb("ones_f", [P, P])
        cos_sb = sb("cos_sb", [P, DH])
        sin_sb = sb("sin_sb", [P, DH])
        slot_base = sb("slot_base", [P, E])
        bias2 = {name: sb(f"b_{name}", [2, D], F32R) for name in ("q", "k", "v", "o", "xk", "xv")}
        ones2 = sb("ones2", [2, P], F32R)
        pick = sb("pick", [2, 2])
        xq_wT = sb("xq_wT", [P, KT, D], BF16)
        xp_wT = sb("xp_wT", [P, KT, D], BF16)
        xq_ws = sb("xq_ws", [P, KT])
        xp_ws = sb("xp_ws", [P, KT])
        xq_bs = sb("xq_bs", [P, KT])
        xp_row = sb("xp_row", [P, D])
        xp_bias = sb("xp_bias", [P, D])
        router_w = sb("router_w", [P, KT, E])
        rstep = sb("rstep", [P, 8])

        x_in = sb("x_in", [P, D])
        x_res = sb("x_res", [P, D])
        ctx_sb = sb("ctx_sb", [P, D])
        xn = sb("xn", [P, D])
        xT_hi = sb("xT_hi", [P, KT, P], F32R)
        xT_lo = sb("xT_lo", [P, KT, P], F32R)
        roped = sb("roped", [P, 2 * D])
        qT = sb("qT", [P, NG, P])
        kbd = sb("kbd", [P, NG, GH, P])
        v1 = sb("v1", [P, H, VW])
        probs = sb("probs", [P, NG, GH * P])
        probsT = sb("probsT", [P, NG, GH * P])
        rot = probsT[:, 0:2, :].rearrange("p a n -> p (a n)")
        att = sb("att", [P, D])
        attT_hi = sb("attT_hi", [P, KT, P], F32R)
        attT_lo = sb("attT_lo", [P, KT, P], F32R)
        x1 = sb("x1", [P, D])
        cT_hi = sb("cT_hi", [P, KT, P], F32R)
        cT_lo = sb("cT_lo", [P, KT, P], F32R)
        xk_sb = sb("xk_sb", [P, D])
        xkbd = sb("xkbd", [P, NG, GH, P])
        xv1 = sb("xv1", [P, H, VW])
        xn2 = sb("xn2", [P, D])
        xq8 = sb("xq8", [P, D], BF16)
        xq8T = sb("xq8T", [P, KT, P], BF16)
        cq = xk_sb
        xatt = sb("xatt", [P, D])
        xo8, xo8T = xq8, xq8T
        x2 = sb("x2", [P, D])
        cqT = x2[:, :].rearrange("p (g t) -> p g t", g=NG)
        row = sb("row", [P, ROW])
        x3T = xn2[:, :]
        small = sb("small", [P, 128])
        half = sb("half", [P, 1])
        router = sb("router", [P, 8, E])
        chosen = sb("chosen", [P, E], BF16)
        chosen_before = sb("chosen_before", [P, E], BF16)
        slots = sb("slots", [P, TOPK], U32)
        SMALL_AT = [0]

        def cols(n):
            SMALL_AT[0] += n
            return small[:, SMALL_AT[0] - n:SMALL_AT[0]]

        ln = {k: dict(stats=cols(6), mv=cols(2), v=cols(1), r0=cols(1), t=cols(1), u=cols(1), r=cols(1))
              for k in ("self", "cross", "ffn")}
        x_amax, x_s, x_rs = cols(1), cols(1), cols(1)
        o_amax, o_s, o_rs = cols(1), cols(1), cols(1)
        sums = cols(H)
        xsums = cols(H)
        negmax = cols(H)
        l_max, e_sum, e_rs, t_sum, t_den, t_rd, t_f = (cols(1) for _ in range(7))
        top8 = router[:, 7, 0:TOPK]
        key8 = router[:, 7, 8:8 + TOPK]

        s_const = sem("const_loaded")
        s_wload = [sem(f"weight_loaded_{k}") for k in range(2)]
        s_bload = sem("bias_loaded")
        d_wchain = sem("dve_setup_step")
        s_x_in, s_x_res, s_ctx = sem("x_in_loaded"), sem("x_res_loaded"), sem("ctx_loaded")
        s_x2_stored, s_scatter, s_filled = sem("x2_stored"), sem("rows_scattered"), sem("routed_filled")
        s_init, s_init2 = sem("pool_constants"), sem("fill_row_ready")
        s_wsplit, s_wprep, s_wT, s_wTr = sem("weights_split"), sem("weight_steps"), sem("weight_transposed"), sem("weight_transposes_read")
        p_xT, p_qk, p_v = sem("pe_xT"), sem("pe_qk"), sem("pe_v")
        p_qkT = sem("pe_qkT")
        p_s, p_pT, p_pv = sem("pe_scores"), sem("pe_probsT"), sem("pe_pv")
        p_aT, p_y = sem("pe_attT"), sem("pe_y")
        p_xk, p_xv, p_xkT = sem("pe_xk"), sem("pe_xv"), sem("pe_xkT")
        p_q8T, p_cq, p_cqT = sem("pe_xq8T"), sem("pe_cq"), sem("pe_cqT")
        p_xs, p_xpT, p_xpv = sem("pe_xscores"), sem("pe_xprobsT"), sem("pe_xpv")
        p_o8T, p_xp = sem("pe_xo8T"), sem("pe_xp")
        p_x3T, p_log, p_pos = sem("pe_x3T"), sem("pe_logits"), sem("pe_positions")
        a_xT, a_v, a_kbd = sem("act_xT"), sem("act_v"), sem("act_kbd")
        a_exp, a_pT = sem("act_exp"), sem("act_probsT")
        a_aT = sem("act_attT")
        a_xk, a_xv, a_xkbd = sem("act_xk"), sem("act_xv"), sem("act_xkbd")
        a_q8T, a_cq, a_cqT = sem("act_xq8T"), sem("act_cq"), sem("act_cqT")
        a_xexp, a_xpT, a_o8T = sem("act_xexp"), sem("act_xprobsT"), sem("act_xo8T")
        a_x3T, a_rexp = sem("act_x3T"), sem("act_router_exp")
        d_ln = {k: sem(f"dve_ln_{k}") for k in ln}
        d_xT, d_rope, d_qT = sem("dve_xT"), sem("dve_rope"), sem("dve_qT")
        d_kbd = sem("dve_kbd")
        d_max, d_att = sem("dve_max"), sem("dve_att")
        d_aT, d_x1 = sem("dve_attT"), sem("dve_x1")
        d_cqT = sem("dve_cqT")
        d_q8, d_xmax = sem("dve_quant_x"), sem("dve_xmax")
        d_xatt, d_o8, d_x2 = sem("dve_xatt"), sem("dve_quant_o"), sem("dve_x2")
        d_r1, d_r2 = sem("dve_route"), sem("dve_slots")
        g_pow = {k: sem(f"pool_rsqrt_{k}") for k in ln}
        g_cT = sem("pool_ctxT")
        g_x1b, g_tok = sem("pool_x1_bias"), sem("pool_token_number")

        weights_in = (("q", qT_w), ("k", kT_w), ("v", vT_w), ("xk", xkT_w), ("xv", xvT_w), ("o", oT_w))
        STAGE = {0: probs, 1: probsT, 2: kbd[:, :, :, :].rearrange("p g j t -> p g (j t)"),
                 3: xkbd[:, :, :, :].rearrange("p g j t -> p g (j t)")}
        bias_in = (("q", bq), ("k", bk), ("v", bv), ("xk", xbk), ("xv", xbv), ("o", bo))
        N_CONST = 8 + 4
        bias_f = roped[0:2, :]

        W = {}
        with ExitStack() as matrices:
            for name in ("q", "k", "v", "xk", "xv", "o"):
                W[name] = tuple(matrices.enter_context(nc.sbuf_tensor(f"w_{name}_{part}", [P, KT, D], F32R))
                                for part in ("hi", "lo"))
        w_gu, w_dn = [], []
        for k in range(RING):
            w_gu.append(sb(f"w_gate_up{k}", [P, 2, KT, F]))
            w_dn.append(sb(f"w_down{k}", [FP, 2, D]))
        tiles = [t[:, :, :, :].rearrange("p g j t -> p (g j t)") for t in (kbd, xkbd)] + \
                [t[:, :, :].rearrange("p g n -> p (g n)") for t in (probs, probsT)]
        rows = [tiles[k // 2][:, (k % 2) * 2 * D:][:, 0:D + 1] for k in range(RING)]
        share = [tiles[k // 2][:, (k % 2) * 2 * D:][:, D + 1:D + 2] for k in range(RING)]
        rowsT = [x_in, x_res]
        gated = [xn[:, 0:F], xn2[:, 0:F]]
        hidden = [att[:, 0:F], xatt[:, 0:F]]
        hiddenT = [cq[0:FP, 0:2 * P], ctx_sb[0:FP, 0:2 * P]]
        scaled_y = [x1, x2]
        token_of = [slots[:, 0:1], slots[:, 1:2]]
        s_ring = [sem(f"expert_weights_loaded{k}") for k in range(RING)]
        s_rows = [sem(f"expert_rows_loaded{k}") for k in range(RING)]
        s_added = sem("outputs_added")
        m_xT, m_gu, m_hT, m_down = sem("moe_rowsT"), sem("moe_gate_up"), sem("moe_hiddenT"), sem("moe_down")
        m_xTc, m_silu = sem("moe_rowsT_copied"), sem("moe_silu")
        m_h, m_hTc, m_y = sem("moe_hidden"), sem("moe_hiddenT_copied"), sem("moe_scaled")
        gate_e = w_gate.rearrange("e (p t) f -> e p t f", t=KT)
        up_e = w_up.rearrange("e (p t) f -> e p t f", t=KT)
        down_e = w_down.rearrange("e (p u) h -> e p u h", u=2)
        routed_e = routed.rearrange("(e p) c -> e p c", p=CAP)

        def share_of(e):
            return routed_e[e][:, bass.ds(e + (D + 1), 1)]

        def load_weights(e, k):
            nc.sync.dma_start(w_gu[k][:, 0, :, :], gate_e[e]).then_inc(s_ring[k], 16)
            nc.sync.dma_start(w_gu[k][:, 1, :, :], up_e[e]).then_inc(s_ring[k], 16)
            nc.sync.dma_start(w_dn[k][:, :, :], down_e[e]).then_inc(s_ring[k], 16)

        block = st.enter_context(nc.Block())

        @block.sync
        def _(sp):
            sp.dma_start(x_in[:, :], x[0]).then_inc(s_x_in, 16)
            for dst, src in ((idf, ident_f), (cos_sb, cos_t), (sin_sb, sin_t), (slot_base, slot0)):
                sp.dma_start(dst[:, :], src).then_inc(s_const, 16)
            for k, src in enumerate((causal, prior)):
                sp.dma_start(att[:, k * P:(k + 1) * P], src).then_inc(s_const, 16)
            sp.dma_start(xq_bs[:, :], xbq.rearrange("(g p) -> p g", p=P),
                         allow_slow_non_contiguous=True).then_inc(s_const, 16)
            sp.dma_start(xp_bias[:, :], xbp.unsqueeze(0).to_broadcast([P, D])).then_inc(s_const, 16)
            sp.dma_start(pick[:, :], ident_f[0:2, 0:2]).then_inc(s_const, 16)
            sp.dma_start(router_w[:, :, :], routerT.rearrange("(t p) e -> p t e", p=P)).then_inc(s_const, 16)
            for n, (name, src) in enumerate(weights_in):
                if n >= 2:
                    sp.wait_ge(s_wsplit, n - 1)
                sp.dma_start(STAGE[n % 2][:, :, :], src.rearrange("(t p) n -> p t n", p=P)).then_inc(s_wload[n % 2], 16)
                if n == 0:
                    sp.dma_start(STAGE[2][:, :, :], xq_w.rearrange("(g p) n -> p g n", p=P)).then_inc(s_const, 16)
                    sp.dma_start(STAGE[3][:, :, :], xp_w.rearrange("(g p) n -> p g n", p=P)).then_inc(s_const, 16)
            for n, (name, src) in enumerate(bias_in):
                if n >= 1:
                    sp.wait_ge(s_wprep, n)
                sp.dma_start(bias_f[:, 0:D], src.unsqueeze(0).to_broadcast([2, D])).then_inc(s_bload, 16)
            sp.wait_ge(s_init2, 2)
            empty = row[:, :]
            for c in range(4):
                sp.dma_start(routed.rearrange("(e p) c -> p e c", p=CAP)[:, c * 16:(c + 1) * 16, :],
                             empty.unsqueeze(1).to_broadcast([P, 16, ROW])).then_inc(s_filled, 16)
            sp.dma_start(out[B], row[:, 0:D]).then_inc(s_filled, 16)

            def body(cur, with_self, with_cross, last_x):
                prev = cur - 1
                at = {k: (v if isinstance(v, int) else sp.snap(v)) for k, v in dict(
                    prev=prev, normed=nth(cur, 7, 7), x2=nth(prev, 2, 2), split=nth(prev, 2, 2), i=prev, i_cross=cur - 2, i_next=cur).items()}
                if with_self:
                    until(sp, g_cT, at["split"])
                    sp.dma_start(ctx_sb[:, :].rearrange("p (t n) -> p t n", t=KT), ctxT_in[at["i"]].rearrange("(t p) n -> p t n", p=P)).then_inc(s_ctx, 16)
                    if not last_x:
                        until(sp, d_ln["self"], at["normed"])
                        sp.dma_start(x_in[:, :], x[at["i_next"]]).then_inc(s_x_in, 16)
                    until(sp, d_x1, at["prev"])
                    sp.dma_start(x_res[:, :], x[at["i"]]).then_inc(s_x_res, 16)
                if with_cross:
                    until(sp, d_x2, at["x2"])
                    sp.dma_start(out[at["i_cross"]], x2[:, :]).then_inc(s_x2_stored, 16)

            body(1, True, False, False)
            body(2, True, True, False)
            with sp.Fori(3, B) as cur:
                body(cur, True, True, False)
            body(B, True, True, True)
            sp.wait_ge(p_y, B)
            for k in range(RING):
                load_weights(k, k)
            body(B + 1, False, True, True)

            sp.wait_ge(s_x2_stored, 16 * B)
            sp.wait_ge(s_scatter, 16 * TOPK * B)

            def load_expert(n, e, k, first):
                if not first:
                    scaled = sp.snap(nth(n - RING, 2, 2))
                    until(sp, m_y, scaled)
                sp.dma_start(rows[k][:, :], routed_e[e][:, 0:D + 1]).then_inc(s_rows[k], 16)
                sp.dma_start(share[k][:, :], share_of(e), allow_slow_non_contiguous=True).then_inc(s_rows[k], 16)
                if not first:
                    load_weights(e, k)

            for n in range(1, RING + 1):
                load_expert(n, n - 1, n - 1, True)
            with sp.Fori(1, E // RING) as j:
                for k in range(RING):
                    load_expert(j * RING + (k + 1), sp.snap(j * RING + k), k, False)
            sp.wait_ge(s_added, 16 * E)

        @block.tensor
        def _(pe):
            def turn(b, src, done):
                for t in range(KT):
                    last = pe.transpose(bank[:, b, t * P:(t + 1) * P], src[:, t * P:(t + 1) * P], idf[:, :])
                last.then_inc(done, 1)

            def turn_bf16(b, src, done):
                for t in range(KT):
                    last = pe.transpose(bank_bf16(b)[:, t * P:(t + 1) * P], src[:, t * P:(t + 1) * P], idb[:, :])
                last.then_inc(done, 1)

            def project(b, hi, lo, name, halfway=None):
                w_hi, w_lo = W[name]
                pe.matmul(bank[:, b, :], ones2[:, :], bias2[name][:, :], start=True, stop=False)
                for t in range(KT):
                    pe.matmul(bank[:, b, :], hi[:, t, :], w_hi[:, t, :], start=False, stop=False)
                    pe.matmul(bank[:, b, :], hi[:, t, :], w_lo[:, t, :], start=False, stop=False)
                    if t == 1 and halfway:
                        halfway()
                for t in range(KT):
                    last = pe.matmul(bank[:, b, :], lo[:, t, :], w_hi[:, t, :], start=False, stop=(t == KT - 1))
                return last

            def project_int8(b, src, w, done):
                for t in range(KT):
                    last = pe.matmul(bank[:, b, :], src[:, t, :], w[:, t, :], start=(t == 0), stop=(t == KT - 1))
                last.then_inc(done, 1)

            def scores(b, g, q, kb, causal_mask, done):
                last = pe.matmul(bank[:, b, :], q[:, g, :], kb[:, g, :, :].rearrange("p j t -> p (j t)"),
                                 start=True, stop=not causal_mask)
                if causal_mask:
                    last = pe.matmul(bank[:, b, :], idb[:, :], mask_add[:, :].unsqueeze(1).to_broadcast([P, GH, P]),
                                     start=False, stop=True)
                last.then_inc(done, 1)

            def turn_probs(b, g, done):
                for j in range(GH):
                    last = pe.transpose(bank[:, b, j * P:(j + 1) * P], probs[:, g, j * P:(j + 1) * P], idf[:, :])
                last.then_inc(done, 1)

            def weigh(b, g, vals, done):
                for j in range(GH):
                    h = g * GH + j
                    at = (h % 8) * VW
                    last = pe.matmul(bank[:, b, at:at + VW], probsT[:, g, j * P:(j + 1) * P], vals[:, h, :],
                                     start=True, stop=True)
                last.then_inc(done, 1)

            def positions(m):
                until(pe, d_r1, nth(m, 11, 9))
                until(pe, d_r2, nth(m - 1, 6, 6))
                pe.matmul(bank[:, 7, E:2 * E], before[:, :], chosen[:, :], start=True, stop=False)
                pe.matmul(bank[:, 7, E:2 * E], ones_b[:, :], chosen_before[:, :], start=False,
                          stop=True).then_inc(p_pos, 1)

            def next_xT(ordinal):
                until(pe, d_ln["self"], nth(ordinal, 7, 7))
                until(pe, a_pT, nth(ordinal - 1, 4, 3))
                turn(0, xn, p_xT)

            def body(cur, with_self, with_cross, with_before, last_x):
                prev = cur - 1
                if with_self:
                    until(pe, a_xT, cur)
                    until(pe, d_xT, cur)
                    until(pe, a_xkbd, prev)
                    project(1, xT_hi, xT_lo, "q")
                    until(pe, d_att, nth(prev, 4, 4))
                    project(2, xT_hi, xT_lo, "k").then_inc(p_qk, 1)
                if with_before:
                    positions(prev - 1)
                def quantised_x():
                    until(pe, d_q8, nth(prev, 6, 6))
                    turn_bf16(3, xq8, p_q8T)

                if with_self:
                    until(pe, a_aT, prev)
                    until(pe, d_aT, prev)
                    project(6, xT_hi, xT_lo, "v", quantised_x if with_cross else None).then_inc(p_v, 1)
                else:
                    quantised_x()
                if with_cross:
                    until(pe, a_q8T, prev)
                    until(pe, d_x1, prev)
                    project_int8(4, xq8T, xq_wT, p_cq)
                if with_self:
                    until(pe, g_cT, nth(cur, 2, 2))
                    until(pe, a_x3T, prev - 1)
                    project(5, cT_hi, cT_lo, "xk").then_inc(p_xk, 1)
                if with_cross:
                    until(pe, a_cq, prev)
                    if with_before:
                        until(pe, d_r2, nth(prev - 1, 6, 2))
                    for t in range(KT):
                        last = pe.transpose(bank[:, 7 if t < 2 else 3, t * P:(t + 1) * P], cq[:, t * P:(t + 1) * P],
                                            idf[:, :])
                    last.then_inc(p_cqT, 1)
                if with_self:
                    until(pe, d_rope, nth(cur, 4, 4))
                    turn(2, roped[:, 0:D], p_qkT)
                    until(pe, a_v, cur)
                    turn(6, roped[:, D:2 * D], p_qkT)
                if with_cross:
                    until(pe, a_cqT, prev)
                    until(pe, d_cqT, prev)
                    until(pe, a_xkbd, prev)
                    for g in range(NG):
                        scores(CROSS_BANK[g], g, cqT, xkbd, False, p_xs)
                if with_self:
                    until(pe, d_qT, cur)
                    until(pe, a_kbd, cur)
                    until(pe, d_kbd, cur)
                for g in range(NG):
                    if with_cross:
                        until(pe, a_xexp, nth(prev, 4, g + 1))
                        turn_probs(CROSS_BANK[g], g, p_xpT)
                    if with_self and g < 2:
                        scores(SELF_BANK[g], g, qT, kbd, True, p_s)
                if with_self:
                    until(pe, a_xk, cur)
                if with_cross:
                    for g in range(NG):
                        until(pe, a_xpT, nth(prev, 4, g + 1))
                        weigh(5 if g < 2 else 7, g, xv1, p_xpv)
                if with_self:
                    scores(0, 2, qT, kbd, True, p_s)
                    scores(4, 3, qT, kbd, True, p_s)
                    project(3, cT_hi, cT_lo, "xv").then_inc(p_xv, 1)
                    turn(1, xk_sb, p_xkT)
                if with_cross:
                    until(pe, d_o8, nth(prev, 6, 6))
                    turn_bf16(5, xo8, p_o8T)
                if with_self:
                    for g in range(2):
                        until(pe, a_exp, nth(cur, 4, g + 1))
                        turn_probs(SELF_BANK[g], g, p_pT)
                if with_cross:
                    until(pe, a_o8T, prev)
                    project_int8(7, xo8T, xp_wT, p_xp)
                if with_self:
                    for g in range(2, 4):
                        until(pe, a_exp, nth(cur, 4, g + 1))
                        turn_probs(SELF_BANK[g], g, p_pT)
                    until(pe, a_xv, cur)
                    for g in range(NG):
                        until(pe, a_pT, nth(cur, 4, g + 1))
                        weigh(3 if g < 2 else 2, g, v1, p_pv)
                    if not last_x:
                        next_xT(cur + 1)
                if with_cross:
                    until(pe, d_ln["ffn"], nth(prev, 7, 7))
                    turn(5, row[:, 0:D], p_x3T)
                if with_self:
                    until(pe, d_att, nth(cur, 4, 4))
                    turn(6, att, p_aT)
                if with_cross:
                    until(pe, a_x3T, prev)
                    for t in range(KT):
                        last = pe.matmul(bank[:, 7, 0:E], x3T[:, t * P:(t + 1) * P], router_w[:, t, :],
                                         start=(t == 0), stop=(t == KT - 1))
                    last.then_inc(p_log, 1)
                if with_self:
                    until(pe, a_aT, cur)
                    until(pe, d_aT, cur)
                    project(4, attT_hi, attT_lo, "o").then_inc(p_y, 1)

            pe.wait_ge(s_const, 16 * N_CONST)
            pe.wait_ge(s_init, 9)
            for n, (w8, bias_row) in enumerate(((0, None), (1, None))):
                pe.wait_ge(s_wprep, 6 + n + 1)
                src = roped[:, :].bitcast(BF16).rearrange("p (g n) -> p g n", g=KT) if n == 0 else \
                    rot[:, :].bitcast(BF16).rearrange("p (g n) -> p g n", g=KT)
                for t in range(KT):
                    for g in range(KT):
                        last = pe.transpose(bank_bf16(t)[:, g * P:(g + 1) * P], src[:, g, t * P:(t + 1) * P], idb[:, :])
                last.then_inc(s_wT, 1)
                pe.wait_ge(s_wTr, n + 1)
            pe.wait_ge(s_wprep, 9)
            for g in range(KT):
                last = pe.matmul(bank[:, 5, g * P:(g + 1) * P], ones_f[:, :], xn2[:, g * P:(g + 1) * P],
                                 start=True, stop=True)
            last.then_inc(s_wT, 1)
            pe.wait_ge(s_wsplit, len(weights_in))
            pe.wait_ge(s_wprep, 10)
            pe.wait_ge(s_wTr, 3)
            next_xT(1)
            body(1, True, False, False, False)
            body(2, True, True, False, False)
            with pe.Fori(3, B) as cur:
                body(cur, True, True, True, False)
            body(B, True, True, True, True)
            body(B + 1, False, True, True, True)
            positions(B)

            def turn_rows(n, k, use):
                until(pe, s_rows[k], use * 32)
                until(pe, m_xTc, n - 2)
                for t in range(KT):
                    last = pe.transpose(bank[:, k % 2, t * P:(t + 1) * P], rows[k][:, t:D:KT], idf[:, :])
                last.then_inc(m_xT, 1)

            def gate_up(n, k, use):
                until(pe, m_xTc, n)
                until(pe, s_ring[k], use * 48)
                until(pe, m_h, n - 2)
                for t in range(KT):
                    last = pe.matmul(bank[:, 2 + k % 2, 0:2 * F], rowsT[k % 2][:, t * P:(t + 1) * P],
                                     w_gu[k][:, :, t, :], start=(t == 0), stop=(t == KT - 1))
                last.then_inc(m_gu, 1)

            def down(n, k):
                until(pe, m_hTc, n)
                until(pe, m_y, nth(n - 2, 2, 2))
                for u in range(2):
                    last = pe.matmul(bank[:, 6 + k % 2, :], hiddenT[k % 2][:, u * P:(u + 1) * P], w_dn[k][:, u, :],
                                     start=(u == 0), stop=(u == 1))
                last.then_inc(m_down, 1)

            def turn_hidden(n, k):
                until(pe, m_h, n)
                until(pe, m_hTc, n - 2)
                for u in range(2):
                    last = pe.transpose(bank[0:FP, 4 + k % 2, u * P:(u + 1) * P], hidden[k % 2][:, u:F:2], idf[:, :])
                last.then_inc(m_hT, 1)

            def step(n, k, j):
                turn_rows(n, k, j + 1)
                if not isinstance(n, int) or n >= 2:
                    gate_up(n - 1, (k - 1) % RING, j + 1 if k >= 1 else j)
                if not isinstance(n, int) or n >= 3:
                    down(n - 2, (k - 2) % RING)
                if not isinstance(n, int) or n >= 2:
                    turn_hidden(n - 1, (k - 1) % RING)

            for k in range(RING):
                step(k + 1, k, 0)
            with pe.Fori(1, E // RING) as j:
                for k in range(RING):
                    step(j * RING + (k + 1), k, j)
            gate_up(E, RING - 1, E // RING)
            down(E - 1, RING - 2)
            turn_hidden(E, RING - 1)
            down(E, RING - 1)

        @block.scalar
        def _(act):
            def copy(dst, src, done):
                act.activation(dst, src, ACT.Copy).then_inc(done, 1)

            def spread_keys(b, kb, heads):
                for j in heads:
                    last = act.activation(kb[j * DH:(j + 1) * DH, :, j, :],
                                          bank[j * DH:(j + 1) * DH, b, :].rearrange("p (g t) -> p g t", g=NG), ACT.Copy)
                return last

            def exponentials(b, g, done):
                for j in range(GH):
                    h = g * GH + j
                    last = act.activation(probs[:, g, j * P:(j + 1) * P], bank[:, b, j * P:(j + 1) * P], ACT.Exp,
                                          bias=negmax[:, h:h + 1])
                last.then_inc(done, 1)

            def flat(t):
                return t[:, :, :].rearrange("p t n -> p (t n)")

            def next_xT(ordinal):
                until(act, p_xT, ordinal)
                until(act, p_v, ordinal - 1)
                copy(flat(xT_hi), bank[:, 0, :], a_xT)

            def cross_exp(g, prev):
                until(act, d_xmax, nth(prev, 4, g + 1))
                until(act, p_pT, nth(prev, 4, 4))
                exponentials(CROSS_BANK[g], g, a_xexp)

            def body(cur, with_self, with_cross, last_x):
                prev = cur - 1
                if with_cross:
                    until(act, p_q8T, prev)
                    until(act, p_xp, prev - 1)
                    copy(flat(xq8T), bank_bf16(3), a_q8T)
                if with_self:
                    until(act, p_v, cur)
                    until(act, p_pv, nth(prev, 4, 4))
                    copy(v1[:, :, 0:DH], bank[:, 6, :].rearrange("p (h d) -> p h d", h=H), a_v)
                if with_cross:
                    until(act, p_cq, prev)
                    until(act, p_xkT, prev)
                    act.activation(cq[:, :], bank[:, 4, :], ACT.Copy, scale=x_s).then_inc(a_cq, 1)
                    until(act, p_cqT, prev)
                    until(act, s_x2_stored, (prev - 1) * 16)
                    for g in (0, 1):
                        last = act.activation(cqT[:, g, :], bank[:, 7, g * P:(g + 1) * P], ACT.Identity,
                                              scale=xq_ws[:, g:g + 1], bias=xq_bs[:, g:g + 1])
                    last.then_inc(a_cqT, 1)
                if with_self:
                    until(act, p_xk, cur)
                    until(act, p_xkT, prev)
                    copy(xk_sb[:, :], bank[:, 5, :], a_xk)
                    until(act, p_qkT, nth(cur, 2, 2))
                    until(act, p_s, nth(prev, 4, 4))
                    spread_keys(6, kbd, (0, 1)).then_inc(a_kbd, 1)
                if with_cross:
                    for g in range(3):
                        cross_exp(g, prev)
                if with_cross:
                    cross_exp(3, prev)
                    for g in range(NG):
                        until(act, p_xpT, nth(prev, 4, g + 1))
                        until(act, p_pv, nth(prev, 4, 4))
                        copy(probsT[:, g, :], bank[:, CROSS_BANK[g], :], a_xpT)
                if with_self:
                    for g in range(NG):
                        if with_cross:
                            until(act, p_xpT, nth(prev, 4, g + 1))
                        until(act, d_max, nth(cur, 4, g + 1))
                        exponentials(SELF_BANK[g], g, a_exp)
                    until(act, p_xv, cur)
                    until(act, p_xpv, nth(prev, 4, 4))
                    copy(xv1[:, :, 0:DH], bank[:, 3, :].rearrange("p (h d) -> p h d", h=H), a_xv)
                if with_cross:
                    until(act, p_o8T, prev)
                    until(act, p_cq, prev)
                    copy(flat(xo8T), bank_bf16(5), a_o8T)
                if with_self:
                    for g in range(NG):
                        until(act, p_pT, nth(cur, 4, g + 1))
                        if with_cross:
                            until(act, p_xpv, nth(prev, 4, 4))
                        copy(probsT[:, g, :], bank[:, SELF_BANK[g], :], a_pT)
                    if not last_x:
                        next_xT(cur + 1)
                if with_cross:
                    until(act, p_x3T, prev)
                    copy(x3T, bank[:, 5, :], a_x3T)
                if with_self:
                    until(act, p_aT, cur)
                    until(act, p_y, prev)
                    copy(flat(attT_hi), bank[:, 6, :], a_aT)
                    until(act, p_xkT, cur)
                    until(act, p_xs, nth(prev, 4, 4))
                    spread_keys(1, xkbd, (0, 1))
                if with_cross:
                    until(act, d_r1, nth(prev, 11, 1))
                    act.activation(router[:, 0, :], bank[:, 7, 0:E], ACT.Exp, bias=l_max,
                                   accum_out=e_sum).then_inc(a_rexp, 1)
                if with_self:
                    spread_keys(1, xkbd, (2, 3)).then_inc(a_xkbd, 1)

            for n, dst in enumerate((xq_wT, xp_wT)):
                act.wait_ge(s_wT, n + 1)
                for t in range(KT):
                    last = act.activation(dst[:, t, :], bank_bf16(t), ACT.Copy)
                last.then_inc(s_wTr, 1)
            act.wait_ge(s_wT, 3)
            act.activation(xp_row[:, :], bank[:, 5, :], ACT.Copy).then_inc(s_wTr, 1)
            act.wait_ge(s_wprep, 10)
            act.wait_ge(s_init, 6)
            next_xT(1)
            body(1, True, False, False)
            body(2, True, True, False)
            with act.Fori(3, B) as cur:
                body(cur, True, True, False)
            body(B, True, True, True)
            body(B + 1, False, True, True)

            def copy_rows(n, k):
                until(act, m_xT, n)
                until(act, m_gu, n - 2)
                copy(rowsT[k % 2][:, :], bank[:, k % 2, :], m_xTc)

            def silu(n, k):
                until(act, m_gu, n)
                until(act, m_h, n - 2)
                act.activation(gated[k % 2], bank[:, 2 + k % 2, 0:F], ACT.Silu).then_inc(m_silu, 1)

            for k in range(RING):
                copy_rows(k + 1, k)
                if k >= 1:
                    silu(k, k - 1)
            with act.Fori(1, E // RING) as j:
                for k in range(RING):
                    copy_rows(j * RING + (k + 1), k)
                    silu(j * RING + k, (k - 1) % RING)
            silu(E, RING - 1)

        @block.vector
        def _(dve):
            def norm_start(kind, src, m):
                s, c = d_ln[kind], ln[kind]
                dve.bn_stats(c["stats"], src).then_inc(s, 1)
                until(dve, s, nth(m, 7, 1))
                apart(dve)
                dve.bn_aggr(c["mv"], c["stats"]).then_inc(s, 1)
                until(dve, s, nth(m, 7, 2))
                dve.tensor_scalar(c["v"], c["mv"][:, 1:2], LN_EPS, None, ALU.add).then_inc(s, 1)

            def norm_end(kind, src, dst, m):
                s, c = d_ln[kind], ln[kind]
                until(dve, g_pow[kind], m)
                dve.scalar_tensor_tensor(out=c["t"], in0=c["v"], scalar=c["r0"], in1=c["r0"], op0=ALU.mult,
                                         op1=ALU.mult).then_inc(s, 1)
                until(dve, s, nth(m, 7, 4))
                dve.tensor_scalar(c["u"], c["t"], -0.5, 1.5, ALU.mult, ALU.add).then_inc(s, 1)
                until(dve, s, nth(m, 7, 5))
                dve.tensor_tensor(c["r"], c["u"], c["r0"], ALU.mult).then_inc(s, 1)
                until(dve, s, nth(m, 7, 6))
                dve.tensor_scalar(dst, src, c["mv"][:, 0:1], c["r"], ALU.subtract, ALU.mult).then_inc(s, 1)

            def find_scale(src, amax, scale, rscale, s, m):
                dve.tensor_reduce(amax, src, AX_X, ALU.max, apply_absolute_value=True).then_inc(s, 1)
                until(dve, s, nth(m, 6, 1))
                dve.tensor_scalar(scale, amax, 1.0 / QMAX, 1e-8, ALU.mult, ALU.max).then_inc(s, 1)
                until(dve, s, nth(m, 6, 2))
                dve.reciprocal(rscale, scale).then_inc(s, 1)

            def quantise(src, tmp, dst, rscale, s, m, free, free_value):
                until(dve, s, nth(m, 6, 3))
                dve.tensor_scalar(tmp, src, rscale, ROUND, ALU.mult, ALU.add).then_inc(s, 1)
                until(dve, s, nth(m, 6, 4))
                dve.tensor_scalar(tmp, tmp, ROUND + QMAX, ROUND - QMAX, ALU.min, ALU.max).then_inc(s, 1)
                until(dve, s, nth(m, 6, 5))
                until(dve, free, free_value)
                dve.tensor_scalar(dst, tmp, ROUND, None, ALU.subtract).then_inc(s, 1)

            def low_part(dst, b, hi, done):
                dve.tensor_tensor(dst[:, :, :].rearrange("p t n -> p (t n)"), bank[:, b, :],
                                  hi[:, :, :].rearrange("p t n -> p (t n)").bitcast(F32), ALU.subtract).then_inc(done, 1)

            def group_max(b, g, ready, value, done):
                until(dve, ready, value)
                dve.tensor_reduce(negmax[:, g * GH:(g + 1) * GH], bank[:, b, :].rearrange("p (j k) -> p j k", j=GH),
                                  AX_X, ALU.max, negate=True).then_inc(done, 1)

            def average(half_, b, dst, total, done, m, ready):
                until(dve, ready, nth(m, 4, 2 + 2 * half_))
                o = bank[:, b, 0:8 * VW].rearrange("p (h d) -> p h d", h=8)
                t = total[:, 8 * half_:8 * half_ + 8]
                dve.reciprocal(t, o[:, :, DH]).then_inc(done, 1)
                until(dve, done, nth(m, 4, 2 * half_ + 1))
                dve.tensor_tensor(dst[:, 256 * half_:256 * half_ + 256].rearrange("p (h d) -> p h d", h=8),
                                  o[:, :, 0:DH], t.unsqueeze(2).to_broadcast([P, 8, DH]),
                                  ALU.mult).then_inc(done, 1)

            def slot_candidates(m):
                m01, ok, at = (router[:, k, :] for k in (2, 3, 4))
                until(dve, p_pos, m)
                dve.scalar_tensor_tensor(out=ok, in0=bank[:, 7, E:2 * E], scalar=float(CAP), in1=m01,
                                         op0=ALU.is_lt, op1=ALU.mult).then_inc(d_r2, 1)
                dve.scalar_tensor_tensor(out=at, in0=bank[:, 7, E:2 * E], scalar=-1.0, in1=slot_base[:, :],
                                         op0=ALU.mult, op1=ALU.add).then_inc(d_r2, 1)

            def route_slots(m):
                s = d_r2
                ok, at, key = (router[:, k, :] for k in (3, 4, 5))
                until(dve, s, nth(m, 6, 2))
                dve.tensor_tensor(key, ok, at, ALU.mult).then_inc(s, 1)
                until(dve, s, nth(m, 6, 3))
                apart(dve)
                dve.max(key8, key).then_inc(s, 1)
                until(dve, s, nth(m, 6, 4))
                until(dve, s_scatter, nth(m - 1, 16 * TOPK, 16 * TOPK))
                dve.tensor_scalar(slots[:, :], key8, -1.0, float(NOWHERE), ALU.mult, ALU.add).then_inc(s, 1)
                dve.tensor_tensor(chosen_before[:, :], chosen_before[:, :], chosen[:, :], ALU.add).then_inc(s, 1)

            def next_xT(ordinal):
                until(dve, a_xT, ordinal)
                until(dve, p_v, ordinal - 1)
                low_part(xT_lo, 0, xT_hi, d_xT)

            def rotate(cur):
                until(dve, p_qk, cur)
                until(dve, p_qkT, nth(cur - 1, 2, 2))
                until(dve, p_pv, nth(cur - 1, 4, 4))
                qk = bank[:, 1:3, :].rearrange("p b (h d) -> p (b h) d", h=H)
                ro = roped[:, :].rearrange("p (h d) -> p h d", d=DH)
                rt = rot[:, :].rearrange("p (h d) -> p h d", d=DH)
                hd = DH // 2
                heads = 2 * H
                dve.tensor_tensor(ro, qk, cos_sb[:, :].unsqueeze(1).to_broadcast([P, heads, DH]),
                                  ALU.mult).then_inc(d_rope, 1)
                dve.tensor_tensor(rt[:, :, 0:hd], qk[:, :, hd:DH],
                                  sin_sb[:, 0:hd].unsqueeze(1).to_broadcast([P, heads, hd]),
                                  ALU.mult).then_inc(d_rope, 1)
                dve.tensor_tensor(rt[:, :, hd:DH], qk[:, :, 0:hd],
                                  sin_sb[:, hd:DH].unsqueeze(1).to_broadcast([P, heads, hd]),
                                  ALU.mult).then_inc(d_rope, 1)
                until(dve, d_rope, nth(cur, 4, 3))
                dve.tensor_tensor(roped[:, :], roped[:, :], rot[:, :], ALU.add).then_inc(d_rope, 1)

            def body(cur, with_self, with_cross, with_before, last_x):
                prev = cur - 1
                if with_cross:
                    until(dve, p_y, prev)
                    until(dve, s_x_res, prev * 16)
                    dve.tensor_tensor(x1[:, :], bank[:, 4, :], x_res[:, :], ALU.add).then_inc(d_x1, 1)
                    until(dve, d_x1, prev)
                    norm_start("cross", x1[:, :], prev)
                    norm_end("cross", x1[:, :], xn2[:, :], prev)
                    until(dve, d_ln["cross"], nth(prev, 7, 7))
                    until(dve, a_cq, prev - 1)
                    find_scale(xn2[:, :], x_amax, x_s, x_rs, d_q8, prev)
                    quantise(xn2[:, :], xatt[:, :], xq8[:, :], x_rs, d_q8, prev, p_o8T, prev - 1)
                if with_before:
                    slot_candidates(prev - 1)
                if with_self:
                    rotate(cur)
                    if not last_x:
                        until(dve, s_x_in, (cur + 1) * 16)
                        norm_start("self", x_in[:, :], cur + 1)
                if with_before:
                    route_slots(prev - 1)
                if with_self and not last_x:
                    until(dve, p_xT, cur)
                    norm_end("self", x_in[:, :], xn[:, :], cur + 1)
                if with_cross:
                    until(dve, p_cqT, prev)
                    until(dve, s_x2_stored, (prev - 1) * 16)
                    for g in (2, 3):
                        last = dve.tensor_scalar(cqT[:, g, :], bank[:, 3, g * P:(g + 1) * P], xq_ws[:, g:g + 1],
                                                 xq_bs[:, g:g + 1], ALU.mult, ALU.add)
                    last.then_inc(d_cqT, 1)
                if with_self:
                    until(dve, p_qkT, nth(cur, 2, 1))
                    until(dve, p_s, nth(prev, 4, 4))
                    dve.tensor_scalar(qT[:, :, :].rearrange("p g t -> p (g t)"), bank[:, 2, :], SCALE, None,
                                      ALU.mult).then_inc(d_qT, 1)
                if with_cross:
                    until(dve, a_exp, nth(prev, 4, 4))
                    for g in (0, 1):
                        group_max(CROSS_BANK[g], g, p_xs, nth(prev, 4, g + 1), d_xmax)
                if with_self:
                    until(dve, p_qkT, nth(cur, 2, 2))
                    for j in (2, 3):
                        last = dve.tensor_copy(kbd[j * DH:(j + 1) * DH, :, j, :],
                                               bank[j * DH:(j + 1) * DH, 6, :].rearrange("p (g t) -> p g t", g=NG))
                    last.then_inc(d_kbd, 1)
                if with_cross:
                    for g in (2, 3):
                        group_max(CROSS_BANK[g], g, p_xs, nth(prev, 4, g + 1), d_xmax)
                if with_self:
                    for g in range(2):
                        self_max(g, cur, with_cross)
                if with_cross:
                    average(0, 5, xatt, xsums, d_xatt, prev, p_xpv)
                    average(1, 7, xatt, xsums, d_xatt, prev, p_xpv)
                    until(dve, d_xatt, nth(prev, 4, 4))
                    find_scale(xatt[:, :], o_amax, o_s, o_rs, d_o8, prev)
                if with_self:
                    for g in range(2, NG):
                        self_max(g, cur, with_cross)
                if with_cross:
                    quantise(xatt[:, :], xn2[:, :], xo8[:, :], o_rs, d_o8, prev, p_q8T, prev)
                    until(dve, p_xp, prev)
                    until(dve, s_x2_stored, (prev - 1) * 16)
                    until(dve, d_o8, nth(prev, 6, 6))
                    dve.scalar_tensor_tensor(out=x2[:, :], in0=bank[:, 7, :], scalar=o_s, in1=xp_row[:, :],
                                             op0=ALU.mult, op1=ALU.mult).then_inc(d_x2, 1)
                    until(dve, d_x2, nth(prev, 2, 1))
                    until(dve, g_x1b, prev)
                    dve.tensor_tensor(x2[:, :], x2[:, :], x1[:, :], ALU.add).then_inc(d_x2, 1)
                    until(dve, d_x2, nth(prev, 2, 2))
                    norm_start("ffn", x2[:, :], prev)
                if with_self:
                    average(0, 3, att, sums, d_att, cur, p_pv)
                if with_cross:
                    until(dve, s_scatter, nth(prev - 1, 16 * TOPK, 16 * TOPK))
                    norm_end("ffn", x2[:, :], row[:, 0:D], prev)
                if with_self:
                    average(1, 2, att, sums, d_att, cur, p_pv)
                    if not last_x:
                        next_xT(cur + 1)
                    until(dve, a_aT, cur)
                    until(dve, p_y, prev)
                    low_part(attT_lo, 6, attT_hi, d_aT)
                if with_cross:
                    route_max(prev)
                    route_choose_rest(prev)

            def self_max(g, cur, with_cross):
                if with_cross:
                    until(dve, a_xexp, nth(cur - 1, 4, g + 1))
                group_max(SELF_BANK[g], g, p_s, nth(cur, 4, g + 1), d_max)

            def route_max(m):
                until(dve, p_log, m)
                dve.tensor_reduce(l_max, bank[:, 7, 0:E], AX_X, ALU.max, negate=True).then_inc(d_r1, 1)

            def route_choose_rest(m):
                s = d_r1
                ex, left, m01 = (router[:, k, :] for k in (0, 1, 2))
                until(dve, a_rexp, m)
                apart(dve)
                dve.max(top8, ex).then_inc(s, 1)
                dve.reciprocal(e_rs, e_sum).then_inc(s, 1)
                until(dve, s, nth(m, 11, 3))
                apart(dve)
                dve.match_replace(left, top8, ex, -1.0).then_inc(s, 1)
                dve.reduce_sum(t_sum, top8, AX_X).then_inc(s, 1)
                until(dve, s, nth(m, 11, 5))
                dve.tensor_scalar(t_den, t_sum, e_rs, 1e-20, ALU.mult, ALU.add).then_inc(s, 1)
                dve.tensor_scalar(m01, left, 0.0, None, ALU.is_lt).then_inc(s, 1)
                until(dve, s, nth(m, 11, 7))
                until(dve, p_pos, m - 1)
                dve.reciprocal(t_rd, t_den).then_inc(s, 1)
                dve.tensor_copy(chosen[:, :], m01).then_inc(s, 1)
                until(dve, s, nth(m, 11, 9))
                dve.tensor_tensor(t_f, e_rs, t_rd, ALU.mult).then_inc(s, 1)
                until(dve, s, nth(m, 11, 10))
                dve.scalar_tensor_tensor(out=row[:, D + 1:ROW], in0=ex, scalar=t_f, in1=m01, op0=ALU.mult,
                                         op1=ALU.mult).then_inc(s, 1)

            dve.wait_ge(s_init, 6)
            dve.wait_ge(s_x_in, 16)
            norm_start("self", x_in[:, :], 1)
            norm_end("self", x_in[:, :], xn[:, :], 1)
            step = [0]

            def chained(instruction):
                step[0] += 1
                instruction.then_inc(d_wchain, 1)
                dve.wait_ge(d_wchain, step[0])

            for n, (name, _) in enumerate(weights_in):
                dve.wait_ge(s_wload[n % 2], 16 * (n // 2 + 1))
                hi, lo = W[name]
                chained(dve.tensor_copy(hi[:, :, :], STAGE[n % 2][:, :, :]))
                dve.tensor_tensor(lo[:, :, :], STAGE[n % 2][:, :, :], hi[:, :, :].bitcast(F32),
                                  ALU.subtract).then_inc(s_wsplit, 1)
            dve.wait_ge(s_const, 16 * N_CONST)
            hi_b, lo_b = x1[0:2, :].bitcast(F32R), x2[0:2, :]
            for n, (name, _) in enumerate(bias_in):
                dve.wait_ge(s_bload, 16 * (n + 1))
                chained(dve.tensor_copy(hi_b, bias_f[:, 0:D]))
                chained(dve.tensor_tensor(lo_b, bias_f[:, 0:D], x1[0:2, :], ALU.subtract))
                chained(dve.tensor_scalar(lo_b, lo_b, pick[:, 1:2], None, ALU.mult))
                dve.scalar_tensor_tensor(out=bias2[name][:, :], in0=x1[0:2, :], scalar=pick[:, 0:1], in1=lo_b,
                                         op0=ALU.mult, op1=ALU.add).then_inc(s_wprep, 1)
                dve.wait_ge(s_wprep, n + 1)
            for n, (src, dst, ws) in enumerate(((STAGE[2], roped, xq_ws), (STAGE[3], rot, xp_ws))):
                whole = dst[:, :].bitcast(BF16).rearrange("p (g n) -> p g n", g=KT)
                am = rstep[:, 0:KT]
                rs = rstep[:, KT:2 * KT]
                chained(dve.tensor_reduce(am, src[:, :, :], AX_X, ALU.max, apply_absolute_value=True))
                chained(dve.tensor_scalar(ws[:, :], am, 1.0 / QMAX, 1e-8, ALU.mult, ALU.max))
                chained(dve.reciprocal(rs, ws[:, :]))
                for g in range(KT):
                    chained(dve.tensor_scalar(src[:, g, :], src[:, g, :], rs[:, g:g + 1], ROUND, ALU.mult, ALU.add))
                chained(dve.tensor_scalar(src[:, :, :], src[:, :, :], ROUND + QMAX, ROUND - QMAX, ALU.min, ALU.max))
                dve.tensor_scalar(whole, src[:, :, :], ROUND, None, ALU.subtract).then_inc(s_wprep, 1)
                dve.wait_ge(s_wprep, 7 + n)
            for g in range(KT):
                last = dve.tensor_scalar(xn2[:, g * P:(g + 1) * P], idf[:, :], xp_ws[:, g:g + 1], None, ALU.mult)
            last.then_inc(s_wprep, 1)
            chained(dve.tensor_scalar(xq_ws[:, :], xq_ws[:, :], SCALE, None, ALU.mult))
            chained(dve.tensor_scalar(xq_bs[:, :], xq_bs[:, :], SCALE, None, ALU.mult))
            dve.memset(kbd[:, :, :, :], 0.0).then_inc(d_wchain, 1)
            dve.memset(xkbd[:, :, :, :], 0.0).then_inc(d_wchain, 1)
            step[0] += 2
            dve.wait_ge(d_wchain, step[0])
            dve.memset(chosen_before[:, :], 0.0).then_inc(s_wprep, 1)
            dve.wait_ge(s_wT, 3)
            dve.wait_ge(s_init, 9)
            next_xT(1)
            body(1, True, False, False, False)
            body(2, True, True, False, False)
            with dve.Fori(3, B) as cur:
                body(cur, True, True, True, False)
            body(B, True, True, True, True)
            body(B + 1, False, True, True, True)
            slot_candidates(B)
            route_slots(B)

            def multiply(n, k):
                until(dve, m_silu, n)
                until(dve, m_hT, n - 2)
                dve.tensor_tensor(hidden[k % 2], bank[:, 2 + k % 2, F:2 * F], gated[k % 2],
                                  ALU.mult).then_inc(m_h, 1)

            def scale_output(n, k, use):
                until(dve, s_added, (n - 2) * 16)
                until(dve, s_rows[k], use * 32)
                dve.tensor_copy(token_of[k % 2], rows[k][:, D:D + 1]).then_inc(m_y, 1)
                until(dve, m_down, n)
                dve.tensor_scalar(scaled_y[k % 2][:, :], bank[:, 6 + k % 2, :], share[k], None,
                                  ALU.mult).then_inc(m_y, 1)

            def copy_hidden(n, k):
                until(dve, m_hT, n)
                until(dve, m_down, n - 2)
                dve.tensor_copy(hiddenT[k % 2], bank[0:FP, 4 + k % 2, 0:2 * P]).then_inc(m_hTc, 1)

            def step(n, k, j):
                if not isinstance(n, int) or n >= 2:
                    multiply(n - 1, (k - 1) % RING)
                if not isinstance(n, int) or n >= 3:
                    scale_output(n - 2, (k - 2) % RING, j + 1 if k >= 2 else j)
                if not isinstance(n, int) or n >= 2:
                    copy_hidden(n - 1, (k - 1) % RING)

            for k in range(RING):
                step(k + 1, k, 0)
            with dve.Fori(1, E // RING) as j:
                for k in range(RING):
                    step(j * RING + (k + 1), k, j)
            multiply(E, RING - 1)
            scale_output(E - 1, RING - 2, E // RING)
            copy_hidden(E, RING - 1)
            scale_output(E, RING - 1, E // RING)

        @block.gpsimd
        def _(pool):
            def rsqrt(kind, m):
                c = ln[kind]
                until(pool, d_ln[kind], nth(m, 7, 3))
                pool.tensor_tensor(c["r0"], c["v"], half[:, :], ALU.pow).then_inc(g_pow[kind], 1)

            def scatter(m):
                until(pool, d_r2, nth(m, 6, 5))
                until(pool, g_tok, m)
                apart(pool)
                for k in range(TOPK):
                    pool.indirect_dma_start(routed, bass.IndirectOffsetOnAxis(ap=slots[:, k:k + 1], axis=0),
                                            row[:, :], None, bounds_check=SLOTS - 1,
                                            oob_is_err=False).then_inc(s_scatter, 16)

            def number_tokens(m):
                until(pool, s_scatter, nth(m - 1, 16 * TOPK, 16 * TOPK))
                apart(pool)
                pool.tensor_scalar(row[:, D:D + 1], row[:, D:D + 1], float(P), None, ALU.add).then_inc(g_tok, 1)

            def body(cur, with_self, with_cross, with_before, last_x):
                prev = cur - 1
                if with_self:
                    until(pool, s_ctx, cur * 16)
                    until(pool, p_xv, prev)
                    apart(pool)
                    pool.tensor_copy(cT_hi[:, :, :].rearrange("p t n -> p (t n)"), ctx_sb[:, :]).then_inc(g_cT, 1)
                if with_cross:
                    rsqrt("cross", prev)
                if with_self:
                    until(pool, g_cT, nth(cur, 2, 1))
                    pool.tensor_tensor(cT_lo[:, :, :].rearrange("p t n -> p (t n)"), ctx_sb[:, :],
                                       cT_hi[:, :, :].rearrange("p t n -> p (t n)").bitcast(F32),
                                       ALU.subtract).then_inc(g_cT, 1)
                if with_cross:
                    until(pool, d_ln["cross"], nth(prev, 7, 7))
                    pool.tensor_tensor(x1[:, :], x1[:, :], xp_bias[:, :], ALU.add).then_inc(g_x1b, 1)
                if with_self and not last_x:
                    rsqrt("self", cur + 1)
                if with_before:
                    scatter(prev - 1)
                if with_cross:
                    rsqrt("ffn", prev)
                    number_tokens(prev)

            pool.memset(ones_b[:, :], 1.0).then_inc(s_init, 1)
            pool.memset(ones_f[:, :], 1.0).then_inc(s_init, 1)
            pool.memset(half[:, :], -0.5).then_inc(s_init, 1)
            pool.memset(v1[:, :, DH:VW], 1.0).then_inc(s_init, 1)
            pool.memset(xv1[:, :, DH:VW], 1.0).then_inc(s_init, 1)
            pool.memset(row[:, :], 0.0).then_inc(s_init2, 1)
            pool.wait_ge(s_init, 2)
            pool.tensor_copy(ones2[:, :], ones_f[0:2, :]).then_inc(s_init, 1)
            pool.wait_ge(s_init2, 1)
            pool.iota(row[:, D:D + 1], pattern=[[0, 1]], base=TOKENS, channel_multiplier=1,
                      allow_small_or_imprecise_dtypes=True).then_inc(s_init2, 1)
            rsqrt("self", 1)
            pool.wait_ge(s_const, 16 * N_CONST)
            for dst, src in ((idb, idf[:, :]), (mask_add, att[:, 0:P]), (before, att[:, P:2 * P])):
                pool.tensor_copy(dst[:, :], src).then_inc(s_init, 1)
            pool.wait_ge(s_filled, 16 * 5)
            pool.wait_ge(s_init2, 2)
            pool.iota(row[:, D:D + 1], pattern=[[0, 1]], base=-P, channel_multiplier=1,
                      allow_small_or_imprecise_dtypes=True).then_inc(s_init2, 1)
            pool.wait_ge(s_init2, 3)
            body(1, True, False, False, False)
            body(2, True, True, False, False)
            with pool.Fori(3, B) as cur:
                body(cur, True, True, True, False)
            body(B, True, True, True, True)
            body(B + 1, False, True, True, True)
            scatter(B)
            pool.wait_ge(s_scatter, 16 * TOPK * B)

            def add_output(n, k):
                until(pool, m_y, nth(n, 2, 2))
                until(pool, s_added, (n - 1) * 16)
                apart(pool)
                pool.indirect_dma_start(out.rearrange("b p d -> (b p) d"),
                                        bass.IndirectOffsetOnAxis(ap=token_of[k % 2], axis=0),
                                        scaled_y[k % 2][:, :], None, bounds_check=TOKENS + P - 1,
                                        oob_is_err=True, compute_op=ALU.add).then_inc(s_added, 16)

            for k in range(RING):
                add_output(k + 1, k)
            with pool.Fori(1, E // RING) as j:
                for k in range(RING):
                    add_output(j * RING + (k + 1), k)
            pool.wait_ge(s_added, 16 * E)


def tables():
    theta = np.float32(10000.0) ** (np.float32(-2.0) * np.arange(DH // 2, dtype=np.float32) / np.float32(DH))
    ang = np.arange(1, P + 1, dtype=np.float32)[:, None] * theta[None, :].astype(np.float32)
    cos, sin = np.cos(ang), np.sin(ang)
    p = np.arange(P)
    return {
        "cos_t": np.concatenate([cos, cos], 1).astype(np.float32),
        "sin_t": np.concatenate([-sin, sin], 1).astype(np.float32),
        "ident_f": np.eye(P, dtype=np.float32),
        "causal": np.where(p[None, :] > p[:, None], MASKED, 0.0).astype(np.float32),
        "prior": (p[:, None] < p[None, :]).astype(np.float32),
        "slot0": np.tile(np.float32(NOWHERE) - CAP * np.arange(E, dtype=np.float32), (P, 1)).astype(np.float32),
    }


def kernel(**inputs):
    from concourse import bacc
    from concourse.bass_utils import run_bass_kernel_spmd

    a = {k: np.asarray(v) for k, v in inputs.items()}
    wkv, bkv = a["L0_xattn_wkv"], a["L0_xattn_bkv"]
    arrays = {
        "x": a["x"], "ctxT_in": a["ctx_2048"].transpose(0, 2, 1),
        "qT_w": a["L0_attn_Wq"].T, "kT_w": a["L0_attn_Wk"].T, "vT_w": a["L0_attn_Wv"].T, "oT_w": a["L0_attn_Wo"].T,
        "xkT_w": wkv[:D].T, "xvT_w": wkv[D:].T, "xq_w": a["L0_xattn_wq"], "xp_w": a["L0_xattn_wp"],
        "bq": a["L0_attn_bq"], "bk": a["L0_attn_bk"], "bv": a["L0_attn_bv"], "bo": a["L0_attn_bo"],
        "xbq": a["L0_xattn_bq"], "xbk": bkv[:D], "xbv": bkv[D:], "xbp": a["L0_xattn_bp"],
        "routerT": a["L0_ffn_router_w"].T, "w_gate": a["L0_ffn_w_gate"], "w_up": a["L0_ffn_w_up"],
        "w_down": a["L0_ffn_w_down"], **tables(),
    }
    arrays = {k: np.ascontiguousarray(v) for k, v in arrays.items()}
    nc = bacc.Bacc("TRN2", target_bir_lowering=False, num_devices=1)
    args = {k: nc.dram_tensor(f"in_{k}", v.shape, mybir.dt.from_np(v.dtype), kind="ExternalInput").ap()
            for k, v in arrays.items()}
    out = nc.dram_tensor("out", (B + 1, P, D), F32, kind="ExternalOutput").ap()
    layer(nc, out=out, **args)
    result = run_bass_kernel_spmd(nc, [{f"in_{k}": v for k, v in arrays.items()}], core_ids=[0])
    return result.results[0]["out"][:B]
```

```python
from contextlib import ExitStack

import numpy as np

import concourse.bass as bass
from concourse import mybir

F32 = mybir.dt.float32
F32R = mybir.dt.float32r
BF16 = mybir.dt.bfloat16
U32 = mybir.dt.uint32
ALU = mybir.AluOpType
ACT = mybir.ActivationFunctionType
AX_X = mybir.AxisListType.X

P = 128
B = 32
D = 512
KT = D // P
H = 16
DH = D // H
NG = 4
GH = H // NG
VW = DH + 1
E = 64
TOPK = 8
CAP = 128
F = 192
FP = F // 2
ROW = D + 1 + E
TOKENS = B * P
SLOTS = E * CAP
NOWHERE = 2 * SLOTS
SCALE = float(DH) ** -0.5
LN_EPS = 1e-5
ROUND = 1.5 * 2.0 ** 23
QMAX = 127.0
MASKED = -1e30
BIASES = ("q", "k", "v", "xk", "xv", "o")
NB = len(BIASES)
N_INIT = 9
BEGUN = 5
WITH_HI = 1 + 2 * KT
RING = 8


CROSS_BANK = (0, 4, 3, 1)
SELF_BANK = (2, 6, 0, 4)


def nth(ordinal, per, j):
    return (ordinal - 1) * per + j


def until(eng, semaphore, value):
    if not isinstance(value, int) or value > 0:
        eng.wait_ge(semaphore, value)


def apart(eng):
    eng.nop(nofuse=True)


def layer(nc, x, ctxT_in, qT_w, kT_w, vT_w, oT_w, xkT_w, xvT_w, xq_w, xp_w, biases, xbq, xbp, routerT,
          w_gate, w_up, w_down, cos_t, sin_t, ident_f, causal, prior, slot0, pick_t, bias_sel, out):
    routed = nc.dram_tensor("routed", (SLOTS, ROW), F32).ap()
    st = ExitStack()

    def sb(name, shape, dt=F32):
        return st.enter_context(nc.sbuf_tensor(name, shape, dt))

    def sem(name):
        return st.enter_context(nc.semaphore(name))

    with st:
        bank = st.enter_context(nc.psum_tensor("bank", [P, 8, 512], F32))

        def bank_bf16(b):
            return bank[:, b, :].bitcast(BF16)[:, 0:D]

        idf = sb("idf", [P, P])
        idb = sb("idb", [P, P], BF16)
        mask_add = sb("mask_add", [P, P], BF16)
        before = sb("before", [P, P], BF16)
        ones_b = sb("ones_b", [P, P], BF16)
        ones_f = sb("ones_f", [P, P])
        cos_sb = sb("cos_sb", [P, DH])
        sin_sb = sb("sin_sb", [P, DH])
        slot_base = sb("slot_base", [P, E])
        bias_rows = sb("bias_rows", [2 * NB, D], F32R)
        bias_of = sb("bias_of", [2 * NB, NB, P], F32R)
        pick = sb("pick", [2 * NB, 2])
        xq_wT = sb("xq_wT", [P, KT, D], BF16)
        xp_wT = sb("xp_wT", [P, KT, D], BF16)
        xq_ws = sb("xq_ws", [P, KT])
        xp_ws = sb("xp_ws", [P, KT])
        xq_bs = sb("xq_bs", [P, KT])
        xp_row = sb("xp_row", [P, D])
        xp_bias = sb("xp_bias", [P, D])
        router_w = sb("router_w", [P, KT, E])
        rstep = sb("rstep", [P, 8])

        x_in = sb("x_in", [P, D])
        x_res = sb("x_res", [P, D])
        ctx_sb = sb("ctx_sb", [P, D])
        xn = sb("xn", [P, D])
        xT_hi = sb("xT_hi", [P, KT, P], F32R)
        xT_lo = sb("xT_lo", [P, KT, P], F32R)
        roped = sb("roped", [P, 2 * D])
        qT = sb("qT", [P, NG, P])
        kbd = sb("kbd", [P, NG, GH, P])
        v_sb = sb("v_sb", [P, D])
        probs = sb("probs", [P, NG, GH * P])
        probsT = sb("probsT", [P, NG, GH * P])
        rot = probsT[:, 0:2, :].rearrange("p a n -> p (a n)")
        x3T = sb("x3T", [P, D])
        attT_hi = sb("attT_hi", [P, KT, P], F32R)
        attT_lo = sb("attT_lo", [P, KT, P], F32R)
        x1 = sb("x1", [P, D])
        cT_hi = sb("cT_hi", [P, KT, P], F32R)
        cT_lo = sb("cT_lo", [P, KT, P], F32R)
        xk_sb = sb("xk_sb", [P, D])
        xkbd = sb("xkbd", [P, NG, GH, P])
        xv1 = sb("xv1", [P, H, VW])
        xn2 = sb("xn2", [P, D])
        xq8 = sb("xq8", [P, D], BF16)
        xq8T = sb("xq8T", [P, KT, P], BF16)
        cq = xk_sb
        xatt = sb("xatt", [P, D])
        xo8, xo8T = xq8, xq8T
        x2 = sb("x2", [P, D])
        cqT = x2[:, :].rearrange("p (g t) -> p g t", g=NG)
        row = sb("row", [P, ROW])
        empty_row = sb("empty_row", [P, ROW])
        small = sb("small", [P, 128])
        half = sb("half", [P, 1])
        router = sb("router", [P, 8, E])
        chosen = sb("chosen", [P, E], BF16)
        chosen_before = sb("chosen_before", [P, E], BF16)
        slots = sb("slots", [P, TOPK], U32)
        SMALL_AT = [0]

        def cols(n):
            SMALL_AT[0] += n
            return small[:, SMALL_AT[0] - n:SMALL_AT[0]]

        ln = {k: dict(stats=cols(6), mv=cols(2), v=cols(1), r0=cols(1), t=cols(1), u=cols(1), r=cols(1))
              for k in ("self", "cross", "ffn")}
        x_amax, x_s, x_rs = cols(1), cols(1), cols(1)
        o_amax, o_s, o_rs = cols(1), cols(1), cols(1)
        sums = cols(H)
        xsums = cols(H)
        negmax = cols(H)
        l_max, e_sum, e_rs, t_sum, t_den, t_rd, t_f = (cols(1) for _ in range(7))
        top8 = router[:, 7, 0:TOPK]
        key8 = router[:, 7, 8:8 + TOPK]

        s_const = sem("const_loaded")
        s_wload = [sem(f"weight_loaded_{k}") for k in range(4)]
        d_wchain = sem("dve_setup_step")
        s_x_in, s_x_res, s_ctx = sem("x_in_loaded"), sem("x_res_loaded"), sem("ctx_loaded")
        s_x2_stored, s_scatter, s_filled = sem("x2_stored"), sem("rows_scattered"), sem("routed_filled")
        s_init, s_init2 = sem("pool_constants"), sem("fill_row_ready")
        s_hi, s_lo_dve, s_lo_pool = sem("weights_hi"), sem("weights_lo_dve"), sem("weights_lo_pool")
        s_zeroed, s_wprep = sem("key_blocks_zero"), sem("weight_steps")
        s_wT, s_wTr = sem("weight_transposed"), sem("weight_transposes_read")
        p_xT, p_qk, p_v = sem("pe_xT"), sem("pe_qk"), sem("pe_v")
        p_qkT = sem("pe_qkT")
        p_s, p_pT, p_pv = sem("pe_scores"), sem("pe_probsT"), sem("pe_pv")
        p_y = sem("pe_y")
        p_xk, p_xv, p_xkT = sem("pe_xk"), sem("pe_xv"), sem("pe_xkT")
        p_q8T, p_cq, p_cqT = sem("pe_xq8T"), sem("pe_cq"), sem("pe_cqT")
        p_xs, p_xpT, p_xpv = sem("pe_xscores"), sem("pe_xprobsT"), sem("pe_xpv")
        p_o8T, p_xp = sem("pe_xo8T"), sem("pe_xp")
        p_x3T, p_log, p_pos = sem("pe_x3T"), sem("pe_logits"), sem("pe_positions")
        a_xT, a_v, a_kbd = sem("act_xT"), sem("act_v"), sem("act_kbd")
        a_exp, a_pT = sem("act_exp"), sem("act_probsT")
        a_aT = sem("act_attT")
        a_xk, a_xv, a_xkbd = sem("act_xk"), sem("act_xv"), sem("act_xkbd")
        a_q8T, a_cq, a_cqT = sem("act_xq8T"), sem("act_cq"), sem("act_cqT")
        a_xexp, a_xpT, a_o8T = sem("act_xexp"), sem("act_xprobsT"), sem("act_xo8T")
        a_x3T, a_rexp = sem("act_x3T"), sem("act_router_exp")
        d_ln = {k: sem(f"dve_ln_{k}") for k in ln}
        d_xT, d_rope, d_qT = sem("dve_xT"), sem("dve_rope"), sem("dve_qT")
        d_kbd = sem("dve_kbd")
        d_max, d_norm = sem("dve_max"), sem("dve_normed_probs")
        d_aT, d_x1 = sem("dve_attT"), sem("dve_x1")
        d_cqT = sem("dve_cqT")
        d_q8, d_xmax = sem("dve_quant_x"), sem("dve_xmax")
        d_xatt, d_o8, d_x2 = sem("dve_xatt"), sem("dve_quant_o"), sem("dve_x2")
        d_r1, d_r2 = sem("dve_route"), sem("dve_slots")
        g_pow = {k: sem(f"pool_rsqrt_{k}") for k in ln}
        g_cT = sem("pool_ctxT")
        g_x1b, g_tok = sem("pool_x1_bias"), sem("pool_token_number")

        weights_in = (("q", qT_w), ("k", kT_w), ("v", vT_w), ("xk", xkT_w), ("xv", xvT_w), ("o", oT_w))
        BY_DVE = 4
        STAGE = [probs, probsT] + [t[:, :, :, :].rearrange("p g j t -> p g (j t)") for t in (kbd, xkbd)]
        N_CONST = 12

        W = {}
        with ExitStack() as matrices:
            for name in ("q", "k", "v", "xk", "xv", "o"):
                W[name] = tuple(matrices.enter_context(nc.sbuf_tensor(f"w_{name}_{part}", [P, KT, D], F32R))
                                for part in ("hi", "lo"))
        w_gu, w_dn = [], []
        for k in range(RING):
            w_gu.append(sb(f"w_gate_up{k}", [P, 2, KT, F]))
            w_dn.append(sb(f"w_down{k}", [FP, 2, D]))
        tiles = [t[:, :, :, :].rearrange("p g j t -> p (g j t)") for t in (kbd, xkbd)] + \
                [t[:, :, :].rearrange("p g n -> p (g n)") for t in (probs, probsT)]
        rows = [tiles[k // 2][:, (k % 2) * 2 * D:][:, 0:D + 1] for k in range(RING)]
        share = [tiles[k // 2][:, (k % 2) * 2 * D:][:, D + 1:D + 2] for k in range(RING)]
        rowsT = [x_in, x_res]
        gated = [xn[:, 0:F], xn2[:, 0:F]]
        hidden = [x3T[:, 0:F], xatt[:, 0:F]]
        hiddenT_hi = [sb(f"hiddenT_hi{k}", [FP, 2 * P], F32R) for k in range(2)]
        hiddenT_lo = [sb(f"hiddenT_lo{k}", [FP, 2 * P], F32R) for k in range(2)]
        matrix_tiles = [t[:, :, :].rearrange("p t n -> p (t n)")[0:FP, :]
                        for t in (xT_hi, xT_lo, attT_hi, attT_lo, cT_hi, cT_lo)]
        matrix_tiles += [sb(f"down_part{k}", [FP, D], F32R)[:, :] for k in range(2)]
        dn_hi = [matrix_tiles[0:2], matrix_tiles[2:4]]
        dn_lo = [matrix_tiles[4:6], matrix_tiles[6:8]]
        scaled_y = [x1, x2]
        token_of = [slots[:, 0:1], slots[:, 1:2]]
        s_ring = [sem(f"expert_weights_loaded{k}") for k in range(RING)]
        s_rows = [sem(f"expert_rows_loaded{k}") for k in range(RING)]
        s_added = sem("outputs_added")
        m_xT, m_gu, m_hT, m_down = sem("moe_rowsT"), sem("moe_gate_up"), sem("moe_hiddenT"), sem("moe_down")
        m_xTc, m_silu, m_hThi = sem("moe_rowsT_copied"), sem("moe_silu"), sem("moe_hiddenT_hi")
        m_dhi, m_dlo = sem("moe_down_hi"), sem("moe_down_lo")
        m_h, m_hTc, m_y = sem("moe_hidden"), sem("moe_hiddenT_copied"), sem("moe_scaled")
        gate_e = w_gate.rearrange("e (p t) f -> e p t f", t=KT)
        up_e = w_up.rearrange("e (p t) f -> e p t f", t=KT)
        down_e = w_down.rearrange("e (p u) h -> e p u h", u=2)
        routed_e = routed.rearrange("(e p) c -> e p c", p=CAP)

        def share_of(e):
            return routed_e[e][:, bass.ds(e + (D + 1), 1)]

        def load_weights(e, k):
            nc.sync.dma_start(w_gu[k][:, 0, :, :], gate_e[e]).then_inc(s_ring[k], 16)
            nc.sync.dma_start(w_gu[k][:, 1, :, :], up_e[e]).then_inc(s_ring[k], 16)
            nc.sync.dma_start(w_dn[k][:, :, :], down_e[e]).then_inc(s_ring[k], 16)

        block = st.enter_context(nc.Block())

        @block.sync
        def _(sp):
            sp.dma_start(x_in[:, :], x[0]).then_inc(s_x_in, 16)
            for n, (name, src) in enumerate(weights_in + (("xq", xq_w), ("xp", xp_w))):
                if n == len(STAGE):
                    for dst, src_c in ((idf, ident_f), (cos_sb, cos_t), (sin_sb, sin_t), (slot_base, slot0),
                                       (pick, pick_t)):
                        sp.dma_start(dst[:, :], src_c).then_inc(s_const, 16)
                    for k, src_c in enumerate((causal, prior)):
                        sp.dma_start(x3T[:, k * P:(k + 1) * P], src_c).then_inc(s_const, 16)
                    sp.dma_start(xn2[0:2 * NB, :], biases).then_inc(s_const, 16)
                    sp.dma_start(roped[0:2 * NB, 0:NB * P], bias_sel).then_inc(s_const, 16)
                    sp.dma_start(xq_bs[:, :], xbq.rearrange("(g p) -> p g", p=P),
                                 allow_slow_non_contiguous=True).then_inc(s_const, 16)
                    sp.dma_start(xp_bias[:, :], xbp.unsqueeze(0).to_broadcast([P, D])).then_inc(s_const, 16)
                    sp.dma_start(router_w[:, :, :], routerT.rearrange("(t p) e -> p t e", p=P)).then_inc(s_const, 16)
                if n >= len(STAGE):
                    sp.wait_ge(s_lo_dve, n - len(STAGE) + 1)
                sp.dma_start(STAGE[n % 4][:, :, :], src.rearrange("(t p) n -> p t n", p=P)).then_inc(s_wload[n % 4], 16)

            def fill(quarter):
                n = E // 4
                sp.dma_start(routed.rearrange("(e p) c -> p e c", p=CAP)[:, quarter * n:(quarter + 1) * n, :],
                             empty_row[:, :].unsqueeze(1).to_broadcast([P, n, ROW])).then_inc(s_filled, 16)

            def body(cur, with_self, with_cross, last_x, filling=False):
                prev = cur - 1
                at = {k: (v if isinstance(v, int) else sp.snap(v)) for k, v in dict(
                    prev=prev, normed=nth(cur, 7, 7), x2=nth(prev, 2, 2), split=nth(prev, 2, 2), i=prev,
                    i_cross=cur - 2, i_next=cur).items()}
                if with_self:
                    until(sp, g_cT, at["split"])
                    sp.dma_start(ctx_sb[:, :].rearrange("p (t n) -> p t n", t=KT),
                                 ctxT_in[at["i"]].rearrange("(t p) n -> p t n", p=P)).then_inc(s_ctx, 16)
                    if filling:
                        fill(2)
                    if not last_x:
                        until(sp, d_ln["self"], at["normed"])
                        sp.dma_start(x_in[:, :], x[at["i_next"]]).then_inc(s_x_in, 16)
                    until(sp, d_x1, at["prev"])
                    sp.dma_start(x_res[:, :], x[at["i"]]).then_inc(s_x_res, 16)
                    if filling:
                        fill(3)
                if with_cross:
                    until(sp, d_x2, at["x2"])
                    sp.dma_start(out[at["i_cross"]], x2[:, :]).then_inc(s_x2_stored, 16)

            body(1, True, False, False)
            sp.wait_ge(s_init2, 2)
            fill(0)
            fill(1)
            sp.dma_start(out[B], empty_row[:, 0:D]).then_inc(s_filled, 16)
            body(2, True, True, False, filling=True)
            with sp.Fori(3, B) as cur:
                body(cur, True, True, False)
            body(B, True, True, True)
            sp.wait_ge(p_y, B)
            for k in range(RING):
                load_weights(k, k)
            body(B + 1, False, True, True)

            sp.wait_ge(s_x2_stored, 16 * B)
            sp.wait_ge(s_scatter, 16 * TOPK * B)

            def load_expert(n, e, k, first):
                if not first:
                    scaled = sp.snap(nth(n - RING, 2, 2))
                    until(sp, m_y, scaled)
                sp.dma_start(rows[k][:, :], routed_e[e][:, 0:D + 1]).then_inc(s_rows[k], 16)
                sp.dma_start(share[k][:, :], share_of(e), allow_slow_non_contiguous=True).then_inc(s_rows[k], 16)
                if not first:
                    load_weights(e, k)

            for n in range(1, RING + 1):
                load_expert(n, n - 1, n - 1, True)
            with sp.Fori(1, E // RING) as j:
                for k in range(RING):
                    load_expert(j * RING + (k + 1), sp.snap(j * RING + k), k, False)
            sp.wait_ge(s_added, 16 * E)

        @block.tensor
        def _(pe):
            def turn(b, src, done):
                for t in range(KT):
                    last = pe.transpose(bank[:, b, t * P:(t + 1) * P], src[:, t * P:(t + 1) * P], idf[:, :])
                last.then_inc(done, 1)

            def turn_bf16(b, src, done):
                for t in range(KT):
                    last = pe.transpose(bank_bf16(b)[:, t * P:(t + 1) * P], src[:, t * P:(t + 1) * P], idb[:, :])
                last.then_inc(done, 1)

            def project(b, hi, lo, name, first=0, end=1 + 3 * KT):
                w_hi, w_lo = W[name]
                steps = [(bias_of[:, BIASES.index(name), :], bias_rows[:, :])]
                for t in range(KT):
                    steps += [(hi[:, t, :], w_hi[:, t, :]), (hi[:, t, :], w_lo[:, t, :])]
                steps += [(lo[:, t, :], w_hi[:, t, :]) for t in range(KT)]
                for k in range(first, end):
                    last = pe.matmul(bank[:, b, :], steps[k][0], steps[k][1], start=(k == 0),
                                     stop=(k == len(steps) - 1))
                return last

            def project_int8(b, src, w, done):
                for t in range(KT):
                    last = pe.matmul(bank[:, b, :], src[:, t, :], w[:, t, :], start=(t == 0), stop=(t == KT - 1))
                last.then_inc(done, 1)

            def scores(b, g, q, kb, causal_mask, done):
                last = pe.matmul(bank[:, b, :], q[:, g, :], kb[:, g, :, :].rearrange("p j t -> p (j t)"),
                                 start=True, stop=not causal_mask)
                if causal_mask:
                    last = pe.matmul(bank[:, b, :], idb[:, :], mask_add[:, :].unsqueeze(1).to_broadcast([P, GH, P]),
                                     start=False, stop=True)
                last.then_inc(done, 1)

            def turn_probs(b, g, done):
                for j in range(GH):
                    last = pe.transpose(bank[:, b, j * P:(j + 1) * P], probs[:, g, j * P:(j + 1) * P], idf[:, :])
                last.then_inc(done, 1)

            def weigh(b, g, vals, done):
                for j in range(GH):
                    h = g * GH + j
                    at = (h % 8) * VW
                    last = pe.matmul(bank[:, b, at:at + VW], probsT[:, g, j * P:(j + 1) * P], vals[:, h, :],
                                     start=True, stop=True)
                last.then_inc(done, 1)

            def weigh_turned(b, g):
                for j in range(GH):
                    h = g * GH + j
                    last = pe.matmul(bank[j * DH:(j + 1) * DH, b, g * P:(g + 1) * P], v_sb[:, h * DH:(h + 1) * DH],
                                     probsT[:, g, j * P:(j + 1) * P], start=True, stop=True)
                last.then_inc(p_pv, 1)

            def positions(m):
                until(pe, d_r1, nth(m, 11, 9))
                until(pe, d_r2, nth(m - 1, 6, 6))
                pe.matmul(bank[:, 0, E:2 * E], before[:, :], chosen[:, :], start=True, stop=False)
                pe.matmul(bank[:, 0, E:2 * E], ones_b[:, :], chosen_before[:, :], start=False,
                          stop=True).then_inc(p_pos, 1)

            def next_xT(ordinal):
                until(pe, d_ln["self"], nth(ordinal, 7, 7))
                until(pe, a_pT, nth(ordinal - 1, 4, 2))
                turn(6, xn, p_xT)

            def begin_queries(ordinal):
                until(pe, a_xT, ordinal)
                until(pe, a_xkbd, ordinal - 1)
                project(1, xT_hi, xT_lo, "q", end=WITH_HI)

            def end_queries(ordinal):
                until(pe, d_xT, ordinal)
                project(1, xT_hi, xT_lo, "q", first=WITH_HI)

            def body(cur, with_self, with_cross, with_before, last_x, then=None):
                prev = cur - 1
                if with_self:
                    project(2, xT_hi, xT_lo, "k").then_inc(p_qk, 1)
                    if then:
                        then()
                    project(6, xT_hi, xT_lo, "v").then_inc(p_v, 1)
                if with_before:
                    positions(prev - 1)
                if with_cross:
                    until(pe, d_q8, nth(prev, 6, 6))
                    turn_bf16(3, xq8, p_q8T)
                if with_self:
                    until(pe, g_cT, nth(cur, 2, 2))
                    until(pe, a_x3T, prev - 1)
                    project(5, cT_hi, cT_lo, "xk", end=BEGUN)
                if with_cross:
                    until(pe, a_q8T, prev)
                    until(pe, d_x1, prev)
                    project_int8(4, xq8T, xq_wT, p_cq)
                if with_self:
                    project(5, cT_hi, cT_lo, "xk", first=BEGUN, end=2 * BEGUN)
                if with_cross:
                    until(pe, a_cq, prev)
                    for t in range(KT):
                        last = pe.transpose(bank[:, 7 if t < 2 else 3, t * P:(t + 1) * P], cq[:, t * P:(t + 1) * P],
                                            idf[:, :])
                    last.then_inc(p_cqT, 1)
                if with_self:
                    project(5, cT_hi, cT_lo, "xk", first=2 * BEGUN).then_inc(p_xk, 1)
                if with_self:
                    until(pe, d_rope, nth(cur, 4, 4))
                    turn(2, roped[:, 0:D], p_qkT)
                    until(pe, a_v, cur)
                    turn(6, roped[:, D:2 * D], p_qkT)
                if with_cross:
                    until(pe, a_cqT, prev)
                    until(pe, d_cqT, prev)
                    until(pe, a_xkbd, prev)
                    if with_before:
                        until(pe, d_r2, nth(prev - 1, 6, 2))
                    for g in range(NG):
                        scores(CROSS_BANK[g], g, cqT, xkbd, False, p_xs)
                for g in range(NG):
                    if with_cross:
                        until(pe, a_xexp, nth(prev, 4, g + 1))
                        turn_probs(CROSS_BANK[g], g, p_xpT)
                    if with_self and g < 2:
                        if g == 0:
                            until(pe, d_qT, cur)
                            until(pe, a_kbd, cur)
                            until(pe, d_kbd, cur)
                        scores(SELF_BANK[g], g, qT, kbd, True, p_s)
                if with_self:
                    until(pe, a_xk, cur)
                for g in range(NG):
                    if with_cross:
                        until(pe, a_xpT, nth(prev, 4, g + 1))
                        weigh(5 if g < 2 else 7, g, xv1, p_xpv)
                    if g == 0 and with_self:
                        scores(0, 2, qT, kbd, True, p_s)
                if with_self:
                    turn(1, xk_sb, p_xkT)
                    scores(4, 3, qT, kbd, True, p_s)
                    project(3, cT_hi, cT_lo, "xv").then_inc(p_xv, 1)
                if with_cross:
                    until(pe, d_o8, nth(prev, 6, 6))
                    turn_bf16(5, xo8, p_o8T)
                if with_self:
                    for g in range(2):
                        until(pe, d_norm, nth(cur, 8, 2 * g + 2))
                        turn_probs(SELF_BANK[g], g, p_pT)
                if with_cross:
                    until(pe, a_o8T, prev)
                    project_int8(7, xo8T, xp_wT, p_xp)
                if with_self:
                    for g in range(2, 4):
                        until(pe, d_norm, nth(cur, 8, 2 * g + 2))
                        turn_probs(SELF_BANK[g], g, p_pT)
                    if not last_x:
                        next_xT(cur + 1)
                    until(pe, a_xv, cur)
                    for g in range(NG):
                        until(pe, a_pT, nth(cur, 4, g + 1))
                        weigh_turned(3, g)
                    if not last_x:
                        begin_queries(cur + 1)
                    until(pe, a_aT, cur)
                    until(pe, d_aT, cur)
                    project(4, attT_hi, attT_lo, "o").then_inc(p_y, 1)
                if with_cross:
                    until(pe, d_ln["ffn"], nth(prev, 7, 7))
                    turn(5, row[:, 0:D], p_x3T)
                if with_self and not last_x:
                    end_queries(cur + 1)
                if with_cross:
                    until(pe, a_x3T, prev)
                    for t in range(KT):
                        last = pe.matmul(bank[:, 0, 0:E], x3T[:, t * P:(t + 1) * P], router_w[:, t, :],
                                         start=(t == 0), stop=(t == KT - 1))
                    last.then_inc(p_log, 1)

            def turn_quantised_weights():
                for n, staged in enumerate((roped[:, :], rot[:, :])):
                    pe.wait_ge(s_wprep, n + 2)
                    if n == 1:
                        pe.wait_ge(s_wTr, 1)
                    src = staged.bitcast(BF16).rearrange("p (g n) -> p g n", g=KT)
                    for t in range(KT):
                        for g in range(KT):
                            last = pe.transpose(bank_bf16(4 + t)[:, g * P:(g + 1) * P],
                                                src[:, g, t * P:(t + 1) * P], idb[:, :])
                    last.then_inc(s_wT, 1)
                pe.wait_ge(s_wprep, 4)
                for g in range(KT):
                    last = pe.matmul(bank[:, 3, g * P:(g + 1) * P], ones_f[:, :], xn2[:, g * P:(g + 1) * P],
                                     start=True, stop=True)
                last.then_inc(s_wT, 1)
                pe.wait_ge(s_lo_pool, len(weights_in) - BY_DVE)
                pe.wait_ge(s_wTr, 3)

            pe.wait_ge(s_const, 16 * N_CONST)
            pe.wait_ge(s_init, N_INIT)
            pe.wait_ge(s_wprep, 1)
            pe.wait_ge(s_lo_dve, BY_DVE)
            next_xT(1)
            begin_queries(1)
            end_queries(1)
            body(1, True, False, False, False, turn_quantised_weights)
            body(2, True, True, False, False)
            with pe.Fori(3, B) as cur:
                body(cur, True, True, True, False)
            body(B, True, True, True, True)
            body(B + 1, False, True, True, True)
            positions(B)

            def turn_rows(n, k, use):
                until(pe, s_rows[k], use * 32)
                until(pe, m_xTc, n - 2)
                for t in range(KT):
                    last = pe.transpose(bank[:, k % 2, t * P:(t + 1) * P], rows[k][:, t:D:KT], idf[:, :])
                last.then_inc(m_xT, 1)

            def gate_up(n, k, use):
                until(pe, m_xTc, n)
                until(pe, s_ring[k], use * 48)
                until(pe, m_h, n - 2)
                for t in range(KT):
                    last = pe.matmul(bank[:, 2 + k % 2, 0:2 * F], rowsT[k % 2][:, t * P:(t + 1) * P],
                                     w_gu[k][:, :, t, :], start=(t == 0), stop=(t == KT - 1))
                last.then_inc(m_gu, 1)

            def down(n, k):
                until(pe, m_hTc, n)
                until(pe, m_dlo, n)
                until(pe, m_y, nth(n - 2, 2, 2))
                for u in range(2):
                    at = slice(u * P, (u + 1) * P)
                    for part, (lhsT, rhs) in enumerate(((hiddenT_hi, dn_hi), (hiddenT_hi, dn_lo), (hiddenT_lo, dn_hi))):
                        last = pe.matmul(bank[:, 6 + k % 2, :], lhsT[k % 2][:, at], rhs[k % 2][u],
                                         start=(u == 0 and part == 0), stop=(u == 1 and part == 2))
                last.then_inc(m_down, 1)

            def turn_hidden(n, k):
                until(pe, m_h, n)
                until(pe, m_hTc, n - 2)
                for u in range(2):
                    last = pe.transpose(bank[0:FP, 4 + k % 2, u * P:(u + 1) * P], hidden[k % 2][:, u:F:2], idf[:, :])
                last.then_inc(m_hT, 1)

            def step(n, k, j):
                if not isinstance(n, int) or n >= 3:
                    gate_up(n - 2, (k - 2) % RING, j + 1 if k >= 2 else j)
                if not isinstance(n, int) or n >= 4:
                    down(n - 3, (k - 3) % RING)
                turn_rows(n, k, j + 1)
                if not isinstance(n, int) or n >= 3:
                    turn_hidden(n - 2, (k - 2) % RING)

            for k in range(RING):
                step(k + 1, k, 0)
            with pe.Fori(1, E // RING) as j:
                for k in range(RING):
                    step(j * RING + (k + 1), k, j)
            for n in (E - 1, E):
                gate_up(n, (n - 1) % RING, E // RING)
                down(n - 1, (n - 2) % RING)
                turn_hidden(n, (n - 1) % RING)
            down(E, RING - 1)

        @block.scalar
        def _(act):
            def copy(dst, src, done):
                act.activation(dst, src, ACT.Copy).then_inc(done, 1)

            def spread_keys(b, kb, heads):
                for j in heads:
                    last = act.activation(kb[j * DH:(j + 1) * DH, :, j, :],
                                          bank[j * DH:(j + 1) * DH, b, :].rearrange("p (g t) -> p g t", g=NG), ACT.Copy)
                return last

            def exponentials(b, g, done, total=None):
                for j in range(GH):
                    h = g * GH + j
                    last = act.activation(probs[:, g, j * P:(j + 1) * P], bank[:, b, j * P:(j + 1) * P], ACT.Exp,
                                          bias=negmax[:, h:h + 1],
                                          **({"accum_out": total[:, h:h + 1]} if total is not None else {}))
                last.then_inc(done, 1)

            def flat(t):
                return t[:, :, :].rearrange("p t n -> p (t n)")

            def next_xT(ordinal):
                until(act, p_xT, ordinal)
                until(act, p_v, ordinal - 1)
                copy(flat(xT_hi), bank[:, 6, :], a_xT)

            def cross_exp(g, prev):
                until(act, d_xmax, nth(prev, 4, g + 1))
                until(act, p_pT, nth(prev, 4, 4))
                exponentials(CROSS_BANK[g], g, a_xexp)

            def copy_cross_probs(g, prev):
                until(act, p_xpT, nth(prev, 4, g + 1))
                until(act, p_pv, nth(prev, 4, 4))
                copy(probsT[:, g, :], bank[:, CROSS_BANK[g], :], a_xpT)

            def router_exp(m):
                until(act, d_r1, nth(m, 11, 1))
                act.activation(router[:, 0, :], bank[:, 0, 0:E], ACT.Exp, bias=l_max,
                               accum_out=e_sum).then_inc(a_rexp, 1)

            def body(cur, with_self, with_cross, with_before, last_x):
                prev = cur - 1
                if with_before:
                    router_exp(prev - 1)
                if with_cross:
                    until(act, p_q8T, prev)
                    until(act, p_xp, prev - 1)
                    copy(flat(xq8T), bank_bf16(3), a_q8T)
                if with_self:
                    until(act, p_v, cur)
                    until(act, p_pv, nth(prev, 4, 4))
                    copy(v_sb[:, :], bank[:, 6, :], a_v)
                if with_cross:
                    until(act, p_cq, prev)
                    until(act, p_xkT, prev)
                    act.activation(cq[:, :], bank[:, 4, :], ACT.Copy, scale=x_s).then_inc(a_cq, 1)
                    until(act, p_cqT, prev)
                    until(act, s_x2_stored, (prev - 1) * 16)
                    for g in (0, 1):
                        last = act.activation(cqT[:, g, :], bank[:, 7, g * P:(g + 1) * P], ACT.Identity,
                                              scale=xq_ws[:, g:g + 1], bias=xq_bs[:, g:g + 1])
                    last.then_inc(a_cqT, 1)
                if with_self:
                    until(act, p_xk, cur)
                    until(act, p_xkT, prev)
                    copy(xk_sb[:, :], bank[:, 5, :], a_xk)
                if with_self:
                    until(act, p_qkT, nth(cur, 2, 2))
                    until(act, p_s, nth(prev, 4, 4))
                    spread_keys(6, kbd, (0, 1)).then_inc(a_kbd, 1)
                if with_cross:
                    for g in range(NG):
                        cross_exp(g, prev)
                    for g in range(NG):
                        copy_cross_probs(g, prev)
                if with_self:
                    for g in range(NG):
                        if with_cross:
                            until(act, p_xpT, nth(prev, 4, g + 1))
                        if g == 3:
                            until(act, p_xkT, cur)
                            until(act, p_xs, nth(prev, 4, 4))
                            spread_keys(1, xkbd, range(GH)).then_inc(a_xkbd, 1)
                        until(act, d_max, nth(cur, 4, g + 1))
                        exponentials(SELF_BANK[g], g, a_exp, sums)
                if with_cross:
                    until(act, p_o8T, prev)
                    until(act, p_cq, prev)
                    copy(flat(xo8T), bank_bf16(5), a_o8T)
                if with_self:
                    until(act, p_xv, cur)
                    until(act, p_xpv, nth(prev, 4, 4))
                    copy(xv1[:, :, 0:DH], bank[:, 3, :].rearrange("p (h d) -> p h d", h=H), a_xv)
                    for g in range(NG):
                        until(act, p_pT, nth(cur, 4, g + 1))
                        if with_cross:
                            until(act, p_xpv, nth(prev, 4, 4))
                        copy(probsT[:, g, :], bank[:, SELF_BANK[g], :], a_pT)
                    if not last_x:
                        next_xT(cur + 1)
                if with_self:
                    until(act, p_pv, nth(cur, 4, 4))
                    until(act, p_y, prev)
                    copy(flat(attT_hi), bank[:, 3, :], a_aT)
                if with_cross:
                    until(act, p_x3T, prev)
                    copy(x3T[:, :], bank[:, 5, :], a_x3T)

            for n, (name, _) in enumerate(weights_in):
                act.wait_ge(s_wload[n % 4], 16 * (n // 4 + 1))
                act.activation(W[name][0][:, :, :], STAGE[n % 4][:, :, :], ACT.Copy).then_inc(s_hi, 1)
            next_xT(1)
            for n, dst in enumerate((xq_wT, xp_wT)):
                act.wait_ge(s_wT, n + 1)
                for t in range(KT):
                    last = act.activation(dst[:, t, :], bank_bf16(4 + t), ACT.Copy)
                last.then_inc(s_wTr, 1)
            act.wait_ge(s_wT, 3)
            act.activation(xp_row[:, :], bank[:, 3, :], ACT.Copy).then_inc(s_wTr, 1)
            act.wait_ge(s_wprep, 5)
            act.wait_ge(s_init, N_INIT)
            act.wait_ge(s_zeroed, 2)
            body(1, True, False, False, False)
            body(2, True, True, False, False)
            with act.Fori(3, B) as cur:
                body(cur, True, True, True, False)
            body(B, True, True, True, True)
            body(B + 1, False, True, True, True)
            router_exp(B)

            def copy_rows(n, k):
                until(act, m_xT, n)
                until(act, m_gu, n - 2)
                copy(rowsT[k % 2][:, :], bank[:, k % 2, :], m_xTc)

            def silu(n, k):
                until(act, m_gu, n)
                until(act, m_h, n - 2)
                act.activation(gated[k % 2], bank[:, 2 + k % 2, 0:F], ACT.Silu).then_inc(m_silu, 1)

            def down_hi(n, k, use):
                until(act, s_ring[k], use * 48)
                until(act, m_down, n - 2)
                for u in range(2):
                    last = act.activation(dn_hi[k % 2][u], w_dn[k][:, u, :], ACT.Copy)
                last.then_inc(m_dhi, 1)

            def hidden_hi(n, k):
                until(act, m_hT, n)
                copy(hiddenT_hi[k % 2][:, :], bank[0:FP, 4 + k % 2, 0:2 * P], m_hThi)

            def step(n, k, j):
                if not isinstance(n, int) or n >= 3:
                    silu(n - 2, (k - 2) % RING)
                    down_hi(n - 2, (k - 2) % RING, j + 1 if k >= 2 else j)
                copy_rows(n, k)
                if not isinstance(n, int) or n >= 3:
                    hidden_hi(n - 2, (k - 2) % RING)

            for k in range(RING):
                step(k + 1, k, 0)
            with act.Fori(1, E // RING) as j:
                for k in range(RING):
                    step(j * RING + (k + 1), k, j)
            for n in (E - 1, E):
                silu(n, (n - 1) % RING)
                down_hi(n, (n - 1) % RING, E // RING)
                hidden_hi(n, (n - 1) % RING)

        @block.vector
        def _(dve):
            def norm_start(kind, src, m):
                s, c = d_ln[kind], ln[kind]
                dve.bn_stats(c["stats"], src).then_inc(s, 1)
                until(dve, s, nth(m, 7, 1))
                apart(dve)
                dve.bn_aggr(c["mv"], c["stats"]).then_inc(s, 1)
                until(dve, s, nth(m, 7, 2))
                dve.tensor_scalar(c["v"], c["mv"][:, 1:2], LN_EPS, None, ALU.add).then_inc(s, 1)

            def norm_end(kind, src, dst, m):
                s, c = d_ln[kind], ln[kind]
                until(dve, g_pow[kind], m)
                dve.scalar_tensor_tensor(out=c["t"], in0=c["v"], scalar=c["r0"], in1=c["r0"], op0=ALU.mult,
                                         op1=ALU.mult).then_inc(s, 1)
                until(dve, s, nth(m, 7, 4))
                dve.tensor_scalar(c["u"], c["t"], -0.5, 1.5, ALU.mult, ALU.add).then_inc(s, 1)
                until(dve, s, nth(m, 7, 5))
                dve.tensor_tensor(c["r"], c["u"], c["r0"], ALU.mult).then_inc(s, 1)
                until(dve, s, nth(m, 7, 6))
                dve.tensor_scalar(dst, src, c["mv"][:, 0:1], c["r"], ALU.subtract, ALU.mult).then_inc(s, 1)

            def quantise(step, src, tmp, dst, amax, scale, rscale, s, m, free, free_value):
                if step > 1:
                    until(dve, s, nth(m, 6, step - 1))
                if step == 1:
                    dve.tensor_reduce(amax, src, AX_X, ALU.max, apply_absolute_value=True).then_inc(s, 1)
                if step == 2:
                    dve.tensor_scalar(scale, amax, 1.0 / QMAX, 1e-8, ALU.mult, ALU.max).then_inc(s, 1)
                if step == 3:
                    dve.reciprocal(rscale, scale).then_inc(s, 1)
                if step == 4:
                    dve.tensor_scalar(tmp, src, rscale, ROUND, ALU.mult, ALU.add).then_inc(s, 1)
                if step == 5:
                    dve.tensor_scalar(tmp, tmp, ROUND + QMAX, ROUND - QMAX, ALU.min, ALU.max).then_inc(s, 1)
                if step == 6:
                    until(dve, free, free_value)
                    dve.tensor_scalar(dst, tmp, ROUND, None, ALU.subtract).then_inc(s, 1)

            def quantise_x(step, m):
                quantise(step, xn2[:, :], xatt[:, :], xq8[:, :], x_amax, x_s, x_rs, d_q8, m, p_o8T, m - 1)

            def quantise_o(step, m):
                quantise(step, xatt[:, :], xn2[:, :], xo8[:, :], o_amax, o_s, o_rs, d_o8, m, p_q8T, m)

            def low_part(dst, b, hi, done):
                dve.tensor_tensor(dst[:, :, :].rearrange("p t n -> p (t n)"), bank[:, b, :],
                                  hi[:, :, :].rearrange("p t n -> p (t n)").bitcast(F32), ALU.subtract).then_inc(done, 1)

            def group_max(b, g, ready, value, done):
                until(dve, ready, value)
                dve.tensor_reduce(negmax[:, g * GH:(g + 1) * GH], bank[:, b, :].rearrange("p (j k) -> p j k", j=GH),
                                  AX_X, ALU.max, negate=True).then_inc(done, 1)

            def average(half_, b, dst, total, done, m, ready):
                until(dve, ready, nth(m, 4, 2 + 2 * half_))
                o = bank[:, b, 0:8 * VW].rearrange("p (h d) -> p h d", h=8)
                t = total[:, 8 * half_:8 * half_ + 8]
                dve.reciprocal(t, o[:, :, DH]).then_inc(done, 1)
                until(dve, done, nth(m, 4, 2 * half_ + 1))
                dve.tensor_tensor(dst[:, 256 * half_:256 * half_ + 256].rearrange("p (h d) -> p h d", h=8),
                                  o[:, :, 0:DH], t.unsqueeze(2).to_broadcast([P, 8, DH]),
                                  ALU.mult).then_inc(done, 1)

            def slot_candidates(m):
                m01, ok, at = (router[:, k, :] for k in (2, 3, 4))
                until(dve, p_pos, m)
                dve.scalar_tensor_tensor(out=ok, in0=bank[:, 0, E:2 * E], scalar=float(CAP), in1=m01,
                                         op0=ALU.is_lt, op1=ALU.mult).then_inc(d_r2, 1)
                dve.scalar_tensor_tensor(out=at, in0=bank[:, 0, E:2 * E], scalar=-1.0, in1=slot_base[:, :],
                                         op0=ALU.mult, op1=ALU.add).then_inc(d_r2, 1)

            def route_slots(m):
                s = d_r2
                ok, at, key = (router[:, k, :] for k in (3, 4, 5))
                until(dve, s, nth(m, 6, 2))
                dve.tensor_tensor(key, ok, at, ALU.mult).then_inc(s, 1)
                until(dve, s, nth(m, 6, 3))
                apart(dve)
                dve.max(key8, key).then_inc(s, 1)
                until(dve, s, nth(m, 6, 4))
                until(dve, s_scatter, nth(m - 1, 16 * TOPK, 16 * TOPK))
                dve.tensor_scalar(slots[:, :], key8, -1.0, float(NOWHERE), ALU.mult, ALU.add).then_inc(s, 1)
                dve.tensor_tensor(chosen_before[:, :], chosen_before[:, :], chosen[:, :], ALU.add).then_inc(s, 1)

            def next_xT(ordinal):
                until(dve, a_xT, ordinal)
                until(dve, p_v, ordinal - 1)
                low_part(xT_lo, 6, xT_hi, d_xT)

            def rotate(cur):
                until(dve, p_qk, cur)
                until(dve, p_qkT, nth(cur - 1, 2, 2))
                until(dve, p_pv, nth(cur - 1, 4, 4))
                qk = bank[:, 1:3, :].rearrange("p b (h d) -> p (b h) d", h=H)
                ro = roped[:, :].rearrange("p (h d) -> p h d", d=DH)
                rt = rot[:, :].rearrange("p (h d) -> p h d", d=DH)
                hd = DH // 2
                heads = 2 * H
                dve.tensor_tensor(ro, qk, cos_sb[:, :].unsqueeze(1).to_broadcast([P, heads, DH]),
                                  ALU.mult).then_inc(d_rope, 1)
                dve.tensor_tensor(rt[:, :, 0:hd], qk[:, :, hd:DH],
                                  sin_sb[:, 0:hd].unsqueeze(1).to_broadcast([P, heads, hd]),
                                  ALU.mult).then_inc(d_rope, 1)
                dve.tensor_tensor(rt[:, :, hd:DH], qk[:, :, 0:hd],
                                  sin_sb[:, hd:DH].unsqueeze(1).to_broadcast([P, heads, hd]),
                                  ALU.mult).then_inc(d_rope, 1)
                until(dve, d_rope, nth(cur, 4, 3))
                dve.tensor_tensor(roped[:, :], roped[:, :], rot[:, :], ALU.add).then_inc(d_rope, 1)

            def body(cur, with_self, with_cross, with_before, last_x):
                prev = cur - 1
                if with_cross:
                    until(dve, p_y, prev)
                    until(dve, s_x_res, prev * 16)
                    dve.tensor_tensor(x1[:, :], bank[:, 4, :], x_res[:, :], ALU.add).then_inc(d_x1, 1)
                    until(dve, d_x1, prev)
                    norm_start("cross", x1[:, :], prev)
                    norm_end("cross", x1[:, :], xn2[:, :], prev)
                    until(dve, d_ln["cross"], nth(prev, 7, 7))
                    until(dve, a_cq, prev - 1)
                for step in range(1, 8):
                    if with_before:
                        route(step, prev - 1)
                    if with_cross and step <= 6:
                        quantise_x(step, prev)
                if with_self:
                    rotate(cur)
                if with_before:
                    slot_candidates(prev - 1)
                if with_cross:
                    until(dve, p_cqT, prev)
                    until(dve, s_x2_stored, (prev - 1) * 16)
                    for g in (2, 3):
                        last = dve.tensor_scalar(cqT[:, g, :], bank[:, 3, g * P:(g + 1) * P], xq_ws[:, g:g + 1],
                                                 xq_bs[:, g:g + 1], ALU.mult, ALU.add)
                    last.then_inc(d_cqT, 1)
                if with_self and not last_x:
                    until(dve, s_x_in, (cur + 1) * 16)
                    norm_start("self", x_in[:, :], cur + 1)
                if with_self:
                    until(dve, p_qkT, nth(cur, 2, 1))
                    until(dve, p_s, nth(prev, 4, 4))
                    dve.tensor_scalar(qT[:, :, :].rearrange("p g t -> p (g t)"), bank[:, 2, :], SCALE, None,
                                      ALU.mult).then_inc(d_qT, 1)
                if with_cross:
                    until(dve, a_exp, nth(prev, 4, 4))
                    for g in (0, 1):
                        group_max(CROSS_BANK[g], g, p_xs, nth(prev, 4, g + 1), d_xmax)
                if with_self:
                    until(dve, p_qkT, nth(cur, 2, 2))
                    for j in (2, 3):
                        last = dve.tensor_copy(kbd[j * DH:(j + 1) * DH, :, j, :],
                                               bank[j * DH:(j + 1) * DH, 6, :].rearrange("p (g t) -> p g t", g=NG))
                    last.then_inc(d_kbd, 1)
                if with_cross:
                    for g in (2, 3):
                        group_max(CROSS_BANK[g], g, p_xs, nth(prev, 4, g + 1), d_xmax)
                if with_before:
                    route_slots(prev - 1)
                if with_self and not last_x:
                    until(dve, p_xT, cur)
                    norm_end("self", x_in[:, :], xn[:, :], cur + 1)
                if with_self:
                    for g in range(3):
                        self_max(g, cur, with_cross)
                    norm_probs(0, cur)
                if with_cross:
                    average(0, 5, xatt, xsums, d_xatt, prev, p_xpv)
                if with_self:
                    norm_probs(1, cur)
                if with_cross:
                    average(1, 7, xatt, xsums, d_xatt, prev, p_xpv)
                    until(dve, d_xatt, nth(prev, 4, 4))
                    for step in (1, 2, 3):
                        quantise_o(step, prev)
                if with_self:
                    self_max(3, cur, with_cross)
                if with_cross:
                    for step in (4, 5, 6):
                        quantise_o(step, prev)
                if with_self:
                    norm_probs(2, cur)
                    norm_probs(3, cur)
                if with_cross:
                    until(dve, p_xp, prev)
                    until(dve, s_x2_stored, (prev - 1) * 16)
                    until(dve, d_o8, nth(prev, 6, 6))
                    dve.scalar_tensor_tensor(out=x2[:, :], in0=bank[:, 7, :], scalar=o_s, in1=xp_row[:, :],
                                             op0=ALU.mult, op1=ALU.mult).then_inc(d_x2, 1)
                    until(dve, d_x2, nth(prev, 2, 1))
                    until(dve, g_x1b, prev)
                    dve.tensor_tensor(x2[:, :], x2[:, :], x1[:, :], ALU.add).then_inc(d_x2, 1)
                    until(dve, d_x2, nth(prev, 2, 2))
                    norm_start("ffn", x2[:, :], prev)
                if with_self:
                    until(dve, a_aT, cur)
                    until(dve, p_y, prev)
                    low_part(attT_lo, 3, attT_hi, d_aT)
                if with_cross:
                    until(dve, s_scatter, nth(prev - 1, 16 * TOPK, 16 * TOPK))
                    norm_end("ffn", x2[:, :], row[:, 0:D], prev)
                if with_self and not last_x:
                    next_xT(cur + 1)

            def norm_probs(g, cur):
                until(dve, a_exp, nth(cur, 4, g + 1))
                own = sums[:, g * GH:(g + 1) * GH]
                dve.reciprocal(own, own).then_inc(d_norm, 1)
                until(dve, d_norm, nth(cur, 8, 2 * g + 1))
                heads = probs[:, g, :].rearrange("p (j k) -> p j k", j=GH)
                dve.tensor_tensor(heads, heads, own.unsqueeze(2).to_broadcast([P, GH, P]), ALU.mult).then_inc(d_norm, 1)

            def self_max(g, cur, with_cross):
                if with_cross:
                    until(dve, a_xexp, nth(cur - 1, 4, g + 1))
                group_max(SELF_BANK[g], g, p_s, nth(cur, 4, g + 1), d_max)

            def route(step, m):
                s = d_r1
                ex, left, m01 = (router[:, k, :] for k in (0, 1, 2))
                if step == 1:
                    until(dve, p_log, m)
                    dve.tensor_reduce(l_max, bank[:, 0, 0:E], AX_X, ALU.max, negate=True).then_inc(s, 1)
                if step == 2:
                    until(dve, a_rexp, m)
                    apart(dve)
                    dve.max(top8, ex).then_inc(s, 1)
                    dve.reciprocal(e_rs, e_sum).then_inc(s, 1)
                if step == 3:
                    until(dve, s, nth(m, 11, 3))
                    apart(dve)
                    dve.match_replace(left, top8, ex, -1.0).then_inc(s, 1)
                    dve.reduce_sum(t_sum, top8, AX_X).then_inc(s, 1)
                if step == 4:
                    until(dve, s, nth(m, 11, 5))
                    dve.tensor_scalar(t_den, t_sum, e_rs, 1e-20, ALU.mult, ALU.add).then_inc(s, 1)
                    dve.tensor_scalar(m01, left, 0.0, None, ALU.is_lt).then_inc(s, 1)
                if step == 5:
                    until(dve, s, nth(m, 11, 7))
                    until(dve, p_pos, m - 1)
                    dve.reciprocal(t_rd, t_den).then_inc(s, 1)
                    dve.tensor_copy(chosen[:, :], m01).then_inc(s, 1)
                if step == 6:
                    until(dve, s, nth(m, 11, 9))
                    dve.tensor_tensor(t_f, e_rs, t_rd, ALU.mult).then_inc(s, 1)
                if step == 7:
                    until(dve, s, nth(m, 11, 10))
                    dve.scalar_tensor_tensor(out=row[:, D + 1:ROW], in0=ex, scalar=t_f, in1=m01, op0=ALU.mult,
                                             op1=ALU.mult).then_inc(s, 1)

            dve.wait_ge(s_x_in, 16)
            norm_start("self", x_in[:, :], 1)
            norm_end("self", x_in[:, :], xn[:, :], 1)
            chain = [0]

            def chained(instruction):
                chain[0] += 1
                instruction.then_inc(d_wchain, 1)
                dve.wait_ge(d_wchain, chain[0])

            for n, (name, _) in enumerate(weights_in[:BY_DVE]):
                hi, lo = W[name]
                dve.wait_ge(s_hi, n + 1)
                dve.tensor_tensor(lo[:, :, :], STAGE[n][:, :, :], hi[:, :, :].bitcast(F32),
                                  ALU.subtract).then_inc(s_lo_dve, 1)
            dve.wait_ge(s_const, 16 * N_CONST)
            both, hi_b, lo_b = (t[0:2 * NB, :] for t in (xn2, x1, x2))
            chained(dve.tensor_copy(hi_b.bitcast(F32R), both))
            chained(dve.tensor_tensor(lo_b, both, hi_b, ALU.subtract))
            chained(dve.tensor_scalar(lo_b, lo_b, pick[:, 1:2], None, ALU.mult))
            dve.scalar_tensor_tensor(out=bias_rows[:, :], in0=hi_b, scalar=pick[:, 0:1], in1=lo_b,
                                     op0=ALU.mult, op1=ALU.add).then_inc(s_wprep, 1)
            next_xT(1)
            dve.wait_ge(s_init, N_INIT)
            for n, (src, dst, ws) in enumerate(((STAGE[2], roped[:, :], xq_ws), (STAGE[3], rot, xp_ws))):
                whole = dst[:, :].bitcast(BF16).rearrange("p (g n) -> p g n", g=KT)
                am = rstep[:, 0:KT]
                rs = rstep[:, KT:2 * KT]
                dve.wait_ge(s_wload[2 + n], 32)
                chained(dve.tensor_reduce(am, src[:, :, :], AX_X, ALU.max, apply_absolute_value=True))
                chained(dve.tensor_scalar(ws[:, :], am, 1.0 / QMAX, 1e-8, ALU.mult, ALU.max))
                chained(dve.reciprocal(rs, ws[:, :]))
                for g in range(KT):
                    last = dve.tensor_scalar(src[:, g, :], src[:, g, :], rs[:, g:g + 1], ROUND, ALU.mult, ALU.add)
                chained(last)
                chained(dve.tensor_scalar(src[:, :, :], src[:, :, :], ROUND + QMAX, ROUND - QMAX, ALU.min, ALU.max))
                if n == 1:
                    dve.wait_ge(s_lo_pool, len(weights_in) - BY_DVE)
                dve.tensor_scalar(whole, src[:, :, :], ROUND, None, ALU.subtract).then_inc(s_wprep, 1)
            for g in range(KT):
                last = dve.tensor_scalar(xn2[:, g * P:(g + 1) * P], idf[:, :], xp_ws[:, g:g + 1], None, ALU.mult)
            last.then_inc(s_wprep, 1)
            dve.tensor_scalar(xq_ws[:, :], xq_ws[:, :], SCALE, None, ALU.mult)
            dve.tensor_scalar(xq_bs[:, :], xq_bs[:, :], SCALE, None, ALU.mult).then_inc(s_wprep, 1)
            dve.wait_ge(s_wprep, 5)
            dve.wait_ge(s_wT, 3)
            dve.wait_ge(s_zeroed, 2)
            body(1, True, False, False, False)
            body(2, True, True, False, False)
            with dve.Fori(3, B) as cur:
                body(cur, True, True, True, False)
            body(B, True, True, True, True)
            body(B + 1, False, True, True, True)
            for routing in range(1, 8):
                route(routing, B)
            slot_candidates(B)
            route_slots(B)

            def multiply(n, k):
                until(dve, m_silu, n)
                until(dve, m_hT, n - 2)
                dve.tensor_tensor(hidden[k % 2], bank[:, 2 + k % 2, F:2 * F], gated[k % 2],
                                  ALU.mult).then_inc(m_h, 1)

            def scale_output(n, k, use):
                until(dve, s_added, (n - 2) * 16)
                until(dve, s_rows[k], use * 32)
                dve.tensor_copy(token_of[k % 2], rows[k][:, D:D + 1]).then_inc(m_y, 1)
                until(dve, m_down, n)
                dve.tensor_scalar(scaled_y[k % 2][:, :], bank[:, 6 + k % 2, :], share[k], None,
                                  ALU.mult).then_inc(m_y, 1)

            def lo_parts(n, k):
                until(dve, m_dhi, n)
                until(dve, m_down, n - 2)
                for u in range(2):
                    last = dve.tensor_tensor(dn_lo[k % 2][u], w_dn[k][:, u, :], dn_hi[k % 2][u].bitcast(F32),
                                             ALU.subtract)
                last.then_inc(m_dlo, 1)
                until(dve, m_hThi, n)
                dve.tensor_tensor(hiddenT_lo[k % 2][:, :], bank[0:FP, 4 + k % 2, 0:2 * P],
                                  hiddenT_hi[k % 2][:, :].bitcast(F32), ALU.subtract).then_inc(m_hTc, 1)

            def step(n, k, j):
                if not isinstance(n, int) or n >= 2:
                    multiply(n - 1, (k - 1) % RING)
                    lo_parts(n - 1, (k - 1) % RING)
                if not isinstance(n, int) or n >= 3:
                    scale_output(n - 2, (k - 2) % RING, j + 1 if k >= 2 else j)

            for k in range(RING):
                step(k + 1, k, 0)
            with dve.Fori(1, E // RING) as j:
                for k in range(RING):
                    step(j * RING + (k + 1), k, j)
            multiply(E, RING - 1)
            lo_parts(E, RING - 1)
            scale_output(E - 1, RING - 2, E // RING)
            scale_output(E, RING - 1, E // RING)

        @block.gpsimd
        def _(pool):
            def rsqrt(kind, m):
                c = ln[kind]
                until(pool, d_ln[kind], nth(m, 7, 3))
                pool.tensor_tensor(c["r0"], c["v"], half[:, :], ALU.pow).then_inc(g_pow[kind], 1)

            def scatter(m):
                until(pool, d_r2, nth(m, 6, 5))
                until(pool, g_tok, m)
                apart(pool)
                for k in range(TOPK):
                    pool.indirect_dma_start(routed, bass.IndirectOffsetOnAxis(ap=slots[:, k:k + 1], axis=0),
                                            row[:, :], None, bounds_check=SLOTS - 1,
                                            oob_is_err=False).then_inc(s_scatter, 16)

            def number_tokens(m):
                until(pool, s_scatter, nth(m - 1, 16 * TOPK, 16 * TOPK))
                apart(pool)
                pool.tensor_scalar(row[:, D:D + 1], row[:, D:D + 1], float(P), None, ALU.add).then_inc(g_tok, 1)

            def body(cur, with_self, with_cross, with_before, last_x):
                prev = cur - 1
                if with_self:
                    until(pool, s_ctx, cur * 16)
                    until(pool, p_xv, prev)
                    apart(pool)
                    pool.tensor_copy(cT_hi[:, :, :].rearrange("p t n -> p (t n)"), ctx_sb[:, :]).then_inc(g_cT, 1)
                if with_cross:
                    rsqrt("cross", prev)
                if with_self:
                    until(pool, g_cT, nth(cur, 2, 1))
                    pool.tensor_tensor(cT_lo[:, :, :].rearrange("p t n -> p (t n)"), ctx_sb[:, :],
                                       cT_hi[:, :, :].rearrange("p t n -> p (t n)").bitcast(F32),
                                       ALU.subtract).then_inc(g_cT, 1)
                if with_cross:
                    until(pool, d_ln["cross"], nth(prev, 7, 7))
                    pool.tensor_tensor(x1[:, :], x1[:, :], xp_bias[:, :], ALU.add).then_inc(g_x1b, 1)
                if with_self and not last_x:
                    rsqrt("self", cur + 1)
                if with_before:
                    scatter(prev - 1)
                if with_cross:
                    rsqrt("ffn", prev)
                    number_tokens(prev)

            pool.memset(half[:, :], -0.5).then_inc(s_init, 1)
            pool.memset(empty_row[:, :], 0.0).then_inc(s_init2, 1)
            pool.wait_ge(s_init2, 1)
            pool.iota(empty_row[:, D:D + 1], pattern=[[0, 1]], base=TOKENS, channel_multiplier=1,
                      allow_small_or_imprecise_dtypes=True).then_inc(s_init2, 1)
            pool.memset(ones_b[:, :], 1.0).then_inc(s_init, 1)
            pool.memset(ones_f[:, :], 1.0).then_inc(s_init, 1)
            pool.memset(xv1[:, :, DH:VW], 1.0).then_inc(s_init, 1)
            pool.memset(chosen_before[:, :], 0.0).then_inc(s_init, 1)
            rsqrt("self", 1)
            pool.wait_ge(s_const, 16 * N_CONST)
            for dst, src in ((idb[:, :], idf[:, :]), (mask_add[:, :], x3T[:, 0:P]), (before[:, :], x3T[:, P:2 * P]),
                             (bias_of[:, :, :].rearrange("r i n -> r (i n)"), roped[0:2 * NB, 0:NB * P])):
                pool.tensor_copy(dst, src).then_inc(s_init, 1)
            for n in range(BY_DVE, len(weights_in)):
                hi, lo = W[weights_in[n][0]]
                pool.wait_ge(s_hi, n + 1)
                pool.tensor_tensor(lo[:, :, :], STAGE[n % 4][:, :, :], hi[:, :, :].bitcast(F32),
                                   ALU.subtract).then_inc(s_lo_pool, 1)
            for n, kb in enumerate((kbd, xkbd)):
                pool.wait_ge(s_wprep, n + 2)
                pool.memset(kb[:, :, :, :], 0.0).then_inc(s_zeroed, 1)
            pool.iota(row[:, D:D + 1], pattern=[[0, 1]], base=-P, channel_multiplier=1,
                      allow_small_or_imprecise_dtypes=True).then_inc(s_init2, 1)
            pool.wait_ge(s_init2, 3)
            body(1, True, False, False, False)
            body(2, True, True, False, False)
            pool.wait_ge(s_filled, 16 * 5)
            with pool.Fori(3, B) as cur:
                body(cur, True, True, True, False)
            body(B, True, True, True, True)
            body(B + 1, False, True, True, True)
            scatter(B)
            pool.wait_ge(s_scatter, 16 * TOPK * B)

            def add_output(n, k):
                until(pool, m_y, nth(n, 2, 2))
                until(pool, s_added, (n - 1) * 16)
                apart(pool)
                pool.indirect_dma_start(out.rearrange("b p d -> (b p) d"),
                                        bass.IndirectOffsetOnAxis(ap=token_of[k % 2], axis=0),
                                        scaled_y[k % 2][:, :], None, bounds_check=TOKENS + P - 1,
                                        oob_is_err=True, compute_op=ALU.add).then_inc(s_added, 16)

            for k in range(RING):
                add_output(k + 1, k)
            with pool.Fori(1, E // RING) as j:
                for k in range(RING):
                    add_output(j * RING + (k + 1), k)
            pool.wait_ge(s_added, 16 * E)


def tables():
    theta = np.float32(10000.0) ** (np.float32(-2.0) * np.arange(DH // 2, dtype=np.float32) / np.float32(DH))
    ang = np.arange(1, P + 1, dtype=np.float32)[:, None] * theta[None, :].astype(np.float32)
    cos, sin = np.cos(ang), np.sin(ang)
    p = np.arange(P)
    of_bias = np.arange(2 * NB)[:, None] // 2 == np.arange(NB)[None, :]
    return {
        "cos_t": np.concatenate([cos, cos], 1).astype(np.float32),
        "sin_t": np.concatenate([-sin, sin], 1).astype(np.float32),
        "pick_t": (np.arange(2 * NB)[:, None] % 2 == np.arange(2)[None, :]).astype(np.float32),
        "bias_sel": np.repeat(of_bias.astype(np.float32), P, axis=1),
        "ident_f": np.eye(P, dtype=np.float32),
        "causal": np.where(p[None, :] > p[:, None], MASKED, 0.0).astype(np.float32),
        "prior": (p[:, None] < p[None, :]).astype(np.float32),
        "slot0": np.tile(np.float32(NOWHERE) - CAP * np.arange(E, dtype=np.float32), (P, 1)).astype(np.float32),
    }


def kernel(**inputs):
    from concourse import bacc
    from concourse.bass_utils import run_bass_kernel_spmd

    a = {k: np.asarray(v) for k, v in inputs.items()}
    wkv, bkv = a["L0_xattn_wkv"], a["L0_xattn_bkv"]
    arrays = {
        "x": a["x"], "ctxT_in": a["ctx_2048"].transpose(0, 2, 1),
        "qT_w": a["L0_attn_Wq"].T, "kT_w": a["L0_attn_Wk"].T, "vT_w": a["L0_attn_Wv"].T, "oT_w": a["L0_attn_Wo"].T,
        "xkT_w": wkv[:D].T, "xvT_w": wkv[D:].T, "xq_w": a["L0_xattn_wq"], "xp_w": a["L0_xattn_wp"],
        "biases": np.repeat(np.stack([a["L0_attn_bq"], a["L0_attn_bk"], a["L0_attn_bv"], bkv[:D], bkv[D:],
                                      a["L0_attn_bo"]]), 2, axis=0),
        "xbq": a["L0_xattn_bq"], "xbp": a["L0_xattn_bp"],
        "routerT": a["L0_ffn_router_w"].T, "w_gate": a["L0_ffn_w_gate"], "w_up": a["L0_ffn_w_up"],
        "w_down": a["L0_ffn_w_down"], **tables(),
    }
    arrays = {k: np.ascontiguousarray(v) for k, v in arrays.items()}
    nc = bacc.Bacc("TRN2", target_bir_lowering=False, num_devices=1)
    args = {k: nc.dram_tensor(f"in_{k}", v.shape, mybir.dt.from_np(v.dtype), kind="ExternalInput").ap()
            for k, v in arrays.items()}
    out = nc.dram_tensor("out", (B + 1, P, D), F32, kind="ExternalOutput").ap()
    layer(nc, out=out, **args)
    result = run_bass_kernel_spmd(nc, [{f"in_{k}": v for k, v in arrays.items()}], core_ids=[0])
    return result.results[0]["out"][:B]
```
